# Optimizing a Trainium2 kernel written in Bass

```python
import numpy as np
import jax
import jax.numpy as jnp

def _softmax(x, axis=-1):
    return jax.nn.softmax(x, axis=axis)

def _gelu(x):
    return jax.nn.gelu(x, approximate=True)

def _silu(x):
    return jax.nn.silu(x)

def _sigmoid(x):
    return jax.nn.sigmoid(x)

def _layernorm(x, axis=-1, eps=1e-05):
    m = jnp.mean(x, axis=axis, keepdims=True)
    v = jnp.var(x, axis=axis, keepdims=True)
    return (x - m) / jnp.sqrt(v + eps)

def _scatter_add(tgt, idx, src, axis=0):
    return tgt.at[idx].add(src)

def _segment_sum(src, seg, n):
    return jax.ops.segment_sum(src, seg, n)
kernel_name = 'mk_recurrent_d1_jaxref_r8_b968c3'

def setup_inputs(seed: int=0):
    np.random.seed(seed)
    _w = jnp.asarray

    def _L0_attn_setup():
        import jax, jax.numpy as jnp
        import numpy as np
        H, P, N, DM = (32, 64, 64, 128)
        DI = H * P
        TH = H * (N // 2)
        DPROJ = 2 * DI + 2 * N + H + TH + H

        def _rms(x, w, eps=1e-05):
            return x * jax.lax.rsqrt(jnp.mean(x * x, -1, keepdims=True) + eps) * w
        key = jax.random.key(seed)
        ks = jax.random.split(key, 5)
        return {'u': jax.random.normal(ks[0], (2, 256, DM), jnp.float32), 'in_proj_w': jax.random.normal(ks[1], (DPROJ, DM), jnp.float32) * (1.0 / np.sqrt(DM)), 'dt_bias': jax.random.normal(ks[2], (H,), jnp.float32), 'A_log': jnp.log(jax.random.uniform(ks[3], (H,), jnp.float32, 1.0, 16.0)), 'D': jnp.ones((H,), jnp.float32), 'B_norm_w': jnp.ones((N,), jnp.float32), 'C_norm_w': jnp.ones((N,), jnp.float32), 'B_bias': jnp.ones((H, N), jnp.float32), 'C_bias': jnp.ones((H, N), jnp.float32), 'norm_w': jnp.ones((DI,), jnp.float32), 'out_proj_w': jax.random.normal(ks[4], (DM, DI), jnp.float32) * (1.0 / np.sqrt(DI))}
    _L0_attn_in = _L0_attn_setup()

    def _L0_ffn_setup():
        import jax, jax.numpy as jnp
        import numpy as np
        FP8_E4M3_MAX = 448.0

        def fake_quant_fp8(t):
            amax = jnp.max(jnp.abs(t))
            scale = FP8_E4M3_MAX / jnp.maximum(amax, 1e-12)
            q = (t * scale).astype(jnp.float8_e4m3fn).astype(jnp.float32)
            return q / scale
        key = jax.random.key(seed)
        k1, k2, k3 = jax.random.split(key, 3)
        d_in, d_out = (128, 128)
        x = jax.random.normal(k1, (4, 1024, d_in), dtype=jnp.float32)
        weight = jax.random.normal(k2, (d_out, d_in), dtype=jnp.float32) * (1.0 / np.sqrt(d_in))
        bias = jax.random.normal(k3, (d_out,), dtype=jnp.float32) * 0.01
        return {'x': x, 'weight': weight, 'bias': bias}
    _L0_ffn_in = _L0_ffn_setup()
    _d = {'L0_attn_u': _L0_attn_in['u'], 'L0_attn_in_proj_w': _L0_attn_in['in_proj_w'], 'L0_attn_dt_bias': _L0_attn_in['dt_bias'], 'L0_attn_A_log': _L0_attn_in['A_log'], 'L0_attn_D': _L0_attn_in['D'], 'L0_attn_B_norm_w': _L0_attn_in['B_norm_w'], 'L0_attn_C_norm_w': _L0_attn_in['C_norm_w'], 'L0_attn_B_bias': _L0_attn_in['B_bias'], 'L0_attn_C_bias': _L0_attn_in['C_bias'], 'L0_attn_norm_w': _L0_attn_in['norm_w'], 'L0_attn_out_proj_w': _L0_attn_in['out_proj_w'], 'L0_ffn_weight': _L0_ffn_in['weight'], 'L0_ffn_bias': _L0_ffn_in['bias']}
    _x0 = _d['L0_attn_u']
    _d['L0_attn_u'] = jax.random.normal(jax.random.fold_in(jax.random.key(seed), 1), (4, 1024, 128), dtype=_x0.dtype)
    del _x0
    return _d

def reference(L0_attn_u, L0_attn_in_proj_w, L0_attn_dt_bias, L0_attn_A_log, L0_attn_D, L0_attn_B_norm_w, L0_attn_C_norm_w, L0_attn_B_bias, L0_attn_C_bias, L0_attn_norm_w, L0_attn_out_proj_w, L0_ffn_weight, L0_ffn_bias):

    def _L0_attn_ref(u, in_proj_w, dt_bias, A_log, D, B_norm_w, C_norm_w, B_bias, C_bias, norm_w, out_proj_w):
        import jax, jax.numpy as jnp
        import numpy as np
        H, P, N, DM = (32, 64, 64, 128)
        DI = H * P
        TH = H * (N // 2)
        DPROJ = 2 * DI + 2 * N + H + TH + H

        def _rms(x, w, eps=1e-05):
            return x * jax.lax.rsqrt(jnp.mean(x * x, -1, keepdims=True) + eps) * w
        Bsz, L, _ = u.shape
        proj = u @ in_proj_w.T
        z = proj[..., :DI]
        xin = proj[..., DI:2 * DI]
        Braw = proj[..., 2 * DI:2 * DI + N]
        Craw = proj[..., 2 * DI + N:2 * DI + 2 * N]
        off = 2 * DI + 2 * N
        dt_raw = proj[..., off:off + H]
        theta = proj[..., off + H:off + H + TH].reshape(Bsz, L, H, N // 2)
        lam = jax.nn.sigmoid(proj[..., off + H + TH:])
        dt = jax.nn.softplus(dt_raw + dt_bias)
        A = -jnp.exp(A_log)
        Bm = _rms(Braw, B_norm_w)[:, :, None, :] + B_bias
        Cm = _rms(Craw, C_norm_w)[:, :, None, :] + C_bias
        tc = jnp.cumsum(theta, axis=1)
        cos_t, sin_t = (jnp.cos(tc), jnp.sin(tc))

        def rope(v):
            v1, v2 = (v[..., :N // 2], v[..., N // 2:])
            return jnp.concatenate([v1 * cos_t - v2 * sin_t, v1 * sin_t + v2 * cos_t], -1)
        Bm, Cm = (rope(Bm), rope(Cm))
        xh = xin.reshape(Bsz, L, H, P)
        alpha = jnp.exp(dt * A)
        gamma = lam * dt
        beta = (1.0 - lam) * dt * alpha
        tofirst = lambda a: jnp.moveaxis(a, 1, 0)
        xs = (tofirst(xh), tofirst(Bm), tofirst(Cm), tofirst(alpha), tofirst(gamma), tofirst(beta))
        h0 = jnp.zeros((Bsz, H, P, N), jnp.float32)

        def step(carry, inp):
            h, prevBx = carry
            x_t, B_t, C_t, a_t, g_t, b_t = inp
            Bx = jnp.einsum('bhp,bhn->bhpn', x_t, B_t)
            h = a_t[..., None, None] * h + g_t[..., None, None] * Bx + b_t[..., None, None] * prevBx
            y = jnp.einsum('bhpn,bhn->bhp', h, C_t)
            return ((h, Bx), y)
        _, ys = jax.lax.scan(step, (h0, h0), xs)
        y = jnp.moveaxis(ys, 0, 1)
        y = y + xh * D[None, None, :, None]
        y = y.reshape(Bsz, L, DI)
        y = y * jax.nn.silu(z)
        y = _rms(y, norm_w)
        return y @ out_proj_w.T

    def _L0_ffn_ref(x, weight, bias):
        import jax, jax.numpy as jnp
        import numpy as np
        FP8_E4M3_MAX = 448.0

        def fake_quant_fp8(t):
            amax = jnp.max(jnp.abs(t))
            scale = FP8_E4M3_MAX / jnp.maximum(amax, 1e-12)
            q = (t * scale).astype(jnp.float8_e4m3fn).astype(jnp.float32)
            return q / scale
        xq = fake_quant_fp8(x)
        wq = fake_quant_fp8(weight)
        return jnp.einsum('bsd,od->bso', xq, wq) + bias
    x = L0_attn_u
    xn = _layernorm(x, axis=-1)
    s = _L0_attn_ref(xn, L0_attn_in_proj_w, L0_attn_dt_bias, L0_attn_A_log, L0_attn_D, L0_attn_B_norm_w, L0_attn_C_norm_w, L0_attn_B_bias, L0_attn_C_bias, L0_attn_norm_w, L0_attn_out_proj_w)
    g = _silu(_L0_ffn_ref(xn, L0_ffn_weight, L0_ffn_bias))
    x = x + s * g
    return x

_drawn_inputs = setup_inputs


def setup_inputs(seed=0):
    import zlib

    import numpy as np

    out = dict(_drawn_inputs(seed))
    spreads = {'L0_attn_D': (1.0, 0.6),
     'L0_attn_B_norm_w': (1.0, 0.6),
     'L0_attn_C_norm_w': (1.0, 0.6),
     'L0_attn_B_bias': (1.0, 0.6),
     'L0_attn_C_bias': (1.0, 0.6),
     'L0_attn_norm_w': (1.0, 0.2)}
    factors = {'L0_ffn_bias': 8.0}
    for name, (base, spread) in spreads.items():
        noise = np.random.default_rng([zlib.crc32(name.encode()), seed]).standard_normal(out[name].shape)
        drawn = base * np.exp(spread * noise) if base else spread * noise
        out[name] = jnp.asarray(drawn.astype(out[name].dtype))
    for name, factor in factors.items():
        out[name] = (out[name] * factor).astype(out[name].dtype)
    return out
```

```python
from contextlib import ExitStack

import concourse.bass as bass
from concourse import mybir

F32 = mybir.dt.float32
BF16 = mybir.dt.bfloat16
FP8 = mybir.dt.float8e4
ALU = mybir.AluOpType
ACT = mybir.ActivationFunctionType
AX = mybir.AxisListType

P = 128
H, HD, N, DM = 32, 64, 64, 128
DI = H * HD
BATCH, L = 4, 1024
TOK = BATCH * L
NC = TOK // P
CS = 4
ST = CS * P
NS = TOK // ST
NQ = H // 4
NP = H // 2
SPB = L // ST
EPS = 1e-5
PI = 3.14159274
TWO_PI = 6.283185
MAGIC = 12582912.0
MASKED = -1.0e30
FP8_MAX = 448.0


def bcast(ap, shape):
    return ap.to_broadcast(shape)


def prepare(nc, keep, dram, scratch):
    u, w_in, dt_bias, a_log, d_skip, b_norm, c_norm, b_bias, c_bias, norm_w, w_out, ffn_w, ffn_b = dram
    xn_d, tc_d, bc_d = scratch
    K = keep
    with ExitStack() as ctx:
        def sb(name, shape, dt=F32):
            return ctx.enter_context(nc.sbuf_tensor(name, shape, dt))

        def sem(name):
            return ctx.enter_context(nc.semaphore(name))

        ps = [ctx.enter_context(nc.psum_tensor(f"a_ps{i}", [P, 512], F32)) for i in range(7)]
        ps_bf = ctx.enter_context(nc.psum_tensor("a_psbf", [P, 4, P], BF16))
        big = sb("a_big", [P, NC * P])
        tmp = sb("a_tmp", [P, NC * P])
        xnT = sb("a_xnT", [P, TOK])
        tcT = sb("a_tcT", [P, TOK])
        ones = K["ones"]
        one_row = sb("a_one_row", [P, 1024])
        stage2 = sb("a_stage2", [P, 11 * P])
        prm = sb("a_prm", [P, P])
        cbn = sb("a_cbn", [H, P])
        row = sb("a_row", [1, 3 * H + P + 2 * N])
        rowb = sb("a_rowb", [P, 3 * H + P + 2 * N])
        wdl = sb("a_wdl", [P, 2 * H])
        wbc = sb("a_wbc", [P, P])
        cbT = sb("a_cbT", [P, H])
        mats = sb("a_mats", [P, 3, P])
        st32 = sb("a_st32", [P, 8, 2 * NC])
        cb1 = sb("a_cb1", [H, N])
        cbs = sb("a_cbs", [H, 1])
        cbs2 = sb("a_cbs2", [H, P])
        cbb = sb("a_cbb", [P, H])
        am = sb("a_am", [P, 2])
        am2 = sb("a_am2", [2, 2])
        s = [sb(f"a_s{i}", [P, NC * H]) for i in range(4)]
        dl = sb("a_dl", [P, NC * 2 * H])
        cum3 = sb("a_cum3", [P, NC, 3 * H], BF16)

        loaded = [sem(f"a_loaded{i}") for i in range(5)]
        consts = sem("a_consts")
        xn_done = sem("a_xn_done")
        w_t = sem("a_w_t")
        w_v = sem("a_w_v")
        w_a = sem("a_w_a")
        stored = sem("a_stored")
        dch = sem("a_dch")
        ach = sem("a_ach")
        pch = sem("a_pch")
        pe_m = sem("a_pe_m")
        v_m = sem("a_v_m")
        for_act = sem("a_for_act")
        a_m = sem("a_a_m")
        block = ctx.enter_context(nc.Block())

        zx_nat = tmp[:].rearrange("p (a m) -> p a m", a=NC)
        wo_nat = tcT[:, 0:DI]
        ident = K["ident"]

        @block.sync
        def _(sp):
            sp.dma_start(big[:].rearrange("p (c m) -> p c m", c=NC),
                         u.rearrange("b (c p) m -> p (b c) m", p=P)).then_inc(loaded[0], 16)
            sp.dma_start(zx_nat, w_in[0:2 * DI].rearrange("(a p) m -> p a m", p=P)).then_inc(loaded[1], 16)
            o = 2 * DI
            sp.dma_start(stage2[:, 0:P], w_in[o:o + P]).then_inc(loaded[2], 16)
            o += P
            sp.dma_start(stage2[0:H, 9 * P:10 * P], w_in[o:o + H]).then_inc(loaded[2], 16)
            sp.dma_start(stage2[:, P:9 * P].rearrange("p (a m) -> p a m", a=8),
                         w_in[o + H:o + H + 1024].rearrange("(a p) m -> p a m", p=P)).then_inc(loaded[2], 16)
            sp.dma_start(stage2[H:2 * H, 9 * P:10 * P], w_in[o + H + 1024:o + 2 * H + 1024]).then_inc(loaded[2], 16)
            sp.dma_start(stage2[:, 10 * P:11 * P], ffn_w).then_inc(loaded[2], 16)
            sp.dma_start(wo_nat, w_out).then_inc(loaded[3], 16)
            sp.dma_start(prm[0:16, :], norm_w.rearrange("(a p) -> a p", p=P)).then_inc(loaded[4], 16)
            for i, bias in enumerate((b_bias, c_bias)):
                r = 16 + 32 * i
                sp.dma_start(prm[r:r + 16, :], bias.rearrange("(q a) n -> q (a n)", a=2)).then_inc(loaded[4], 16)
                src = bias.rearrange("(q a) (f j) -> q a f j", a=2, f=2)
                dst = prm[r + 16:r + 32, :].rearrange("q (a f j) -> q a f j", a=2, f=2)
                for f in range(2):
                    sp.dma_start(dst[:, :, f, :], src[:, :, 1 - f, :]).then_inc(loaded[4], 16)
            sp.dma_start(cbn[:, 0:N], c_bias).then_inc(loaded[4], 16)
            sp.dma_start(cbn[:, N:2 * N], b_bias).then_inc(loaded[4], 16)
            at = 0
            for v, n in ((dt_bias, H), (a_log, H), (d_skip, H), (ffn_b, P), (b_norm, N), (c_norm, N)):
                sp.dma_start(row[0:1, at:at + n], v.rearrange("(a n) -> a n", a=1)).then_inc(loaded[4], 16)
                at += n
            sp.wait_ge(v_m, 2)
            sp.dma_start(xn_d.rearrange("s p t -> p s t"), xnT[:].rearrange("p (s t) -> p s t", s=NS)).then_inc(stored, 16)
            sp.dma_start(tc_d.rearrange("s p t -> p s t"), tcT[:].rearrange("p (s t) -> p s t", s=NS)).then_inc(stored, 16)
            sp.wait_ge(v_m, 5)
            sp.dma_start(bc_d.rearrange("s p t -> p s t"), tmp[:].rearrange("p (s t) -> p s t", s=NS)).then_inc(stored, 16)
            sp.wait_ge(stored, 48)

        @block.gpsimd
        def _(pool):
            n = [0]

            def link(ins):
                n[0] += 1
                ins.then_inc(pch, 1)
                pool.wait_ge(pch, n[0])

            link(nc.gpsimd.memset(ones[:], 1.0))
            link(nc.gpsimd.memset(one_row[:], 1.0))
            link(nc.gpsimd.memset(ident[:], 0.0))
            link(nc.gpsimd.affine_select(out=ident[:], in_=ident[:], compare_op=ALU.not_equal, fill=1.0, base=0,
                                         pattern=[[-1, P]], channel_multiplier=1))
            link(nc.gpsimd.memset(K["ident_bf"][:], 0.0))
            link(nc.gpsimd.affine_select(out=K["ident_bf"][:], in_=K["ident_bf"][:], compare_op=ALU.not_equal, fill=1.0,
                                         base=0, pattern=[[-1, P]], channel_multiplier=1))
            link(nc.gpsimd.memset(K["zeros_bf"][:], 0.0))
            link(nc.gpsimd.memset(mats[:], 0.0))
            link(nc.gpsimd.affine_select(out=mats[:, 0, :], in_=one_row[:, 0:P], compare_op=ALU.is_ge, fill=0.0, base=0,
                                         pattern=[[1, P]], channel_multiplier=-1))
            link(nc.gpsimd.affine_select(out=mats[:, 1, :], in_=mats[:, 1, :], compare_op=ALU.not_equal, fill=1.0, base=-1,
                                         pattern=[[-1, P]], channel_multiplier=1))
            link(nc.gpsimd.affine_select(out=mats[:, 2, :], in_=mats[:, 2, :], compare_op=ALU.not_equal, fill=1.0, base=P - 1,
                                         pattern=[[-1, P]], channel_multiplier=1))
            link(nc.gpsimd.memset(K["mask"][:], 0.0))
            link(nc.gpsimd.affine_select(out=K["mask"][:].rearrange("p (c t) -> p c t", c=CS),
                                         in_=K["mask"][:].rearrange("p (c t) -> p c t", c=CS), compare_op=ALU.is_ge,
                                         fill=MASKED, base=0, pattern=[[0, CS], [1, P]], channel_multiplier=-1))
            for name, v in (("sel", 1.0), ("nsel", -1.0)):
                link(nc.gpsimd.memset(K[name][:], 0.0))
                for i in range(3):
                    link(nc.gpsimd.affine_select(out=K[name][:], in_=K[name][:], compare_op=ALU.not_equal, fill=v,
                                                 base=-32 * i, pattern=[[-1, H]], channel_multiplier=1))
            link(nc.gpsimd.memset(K["cols"][:], MAGIC))
            link(nc.gpsimd.memset(K["cols"][:, 1:2], PI / 2))
            link(nc.gpsimd.memset(K["cols"][:, 2:3], EPS))
            for i in range(4):
                link(nc.gpsimd.memset(K["cols"][32 * i:32 * i + 32, 0:1], TWO_PI if i % 2 == 0 else -TWO_PI))
            link(nc.gpsimd.memset(K["goes_on"][:], 1.0))
            for i in range(BATCH):
                link(nc.gpsimd.memset(K["goes_on"][:, SPB * i:SPB * i + 1], 0.0))
            link(nc.gpsimd.memset(K["carry"][:], 0.0))
            nc.gpsimd.memset(am2[:], 0.0).then_inc(consts, 1)

        groups = []
        for g in range(8):
            groups.append([zx_nat[:, 4 * g + i, :] for i in range(4)])
        groups.append([stage2[:, 0:P], stage2[0:2 * H, 9 * P:10 * P], stage2[:, 10 * P:11 * P], prm[0:80, :]])
        for g in range(2):
            groups.append([stage2[:, (1 + 4 * g + i) * P:(2 + 4 * g + i) * P] for i in range(4)])
        for g in range(4):
            groups.append([wo_nat[:, (4 * g + i) * P:(4 * g + i + 1) * P] for i in range(4)])
        groups.append([cbn[:, :]])
        NG = len(groups)

        @block.tensor
        def _(pe):
            pe.wait_ge(consts, 1)
            pe.wait_ge(loaded[1], 16)
            for g, srcs in enumerate(groups):
                if g == 8:
                    pe.wait_ge(loaded[2], 80)
                    pe.wait_ge(loaded[4], 16 * 15)
                if g == 11:
                    pe.wait_ge(loaded[3], 16)
                if g >= 4:
                    pe.wait_ge(w_v if g % 2 == 0 else w_a, (g - 4) // 2 + 1)
                for i, src in enumerate(srcs):
                    r = src.shape[0]
                    last = nc.tensor.transpose(ps[g % 4][:, i * P:i * P + r], src, ident[0:r, 0:r])
                last.then_inc(w_t, 1)
            nc.tensor.matmul(ps[4][:, 0:row.shape[1]], one_row[0:1, 0:P], row[0:1, :], start=True, stop=True).then_inc(pe_m, 1)
            pe.wait_ge(xn_done, 1)
            pe.wait_ge(w_v, NG // 2)
            pe.wait_ge(w_a, NG // 2)
            for g in range(8):
                if g >= 4:
                    pe.wait_ge(w_v if g % 2 == 0 else w_a, NG // 2 + (g - 4) // 2 + 1)
                for i in range(4):
                    c = 4 * g + i
                    last = nc.tensor.transpose(ps[g % 4][:, i * P:i * P + P], big[:, c * P:c * P + P], ident[:])
                last.then_inc(w_t, 1)
            pe.wait_ge(v_m, 1)
            nc.tensor.transpose(ps[5][0:2, 0:P], am[:, 0:2], ident[:]).then_inc(pe_m, 1)
            pe.wait_ge(w_v, NG // 2 + 4)
            pe.wait_ge(w_a, NG // 2 + 4)
            for g in range(12):
                if g >= 4:
                    pe.wait_ge(w_v if g % 2 == 0 else w_a, NG // 2 + 4 + (g - 4) // 2 + 1)
                for i in range(4 if g < 8 else 8):
                    if g < 8:
                        c = 4 * g + i
                        last = nc.tensor.matmul(ps[g % 4][:, i * P:i * P + P], xnT[:, c * P:c * P + P], wbc[:],
                                                start=True, stop=True)
                    else:
                        c = 8 * (g - 8) + i
                        last = nc.tensor.matmul(ps[g % 4][:, i * 64:i * 64 + 64], xnT[:, c * P:c * P + P], wdl[:],
                                                start=True, stop=True)
                last.then_inc(w_t, 1)
            pe.wait_ge(v_m, 3)
            nc.tensor.matmul(ps[6][:, 0:2], ones[0:2, 0:P], am2[0:2, 0:2], start=True, stop=True)
            nc.tensor.matmul(ps[6][:, 64:64 + H], cbs2[:, :], ident[0:H, 0:H], start=True, stop=True).then_inc(pe_m, 1)
            pe.wait_ge(v_m, 4)
            pe.wait_ge(w_v, NG // 2 + 10)
            pe.wait_ge(w_a, NG // 2 + 10)
            for g in range(8):
                if g >= 4:
                    pe.wait_ge(w_v if g % 2 == 0 else w_a, NG // 2 + 10 + (g - 4) // 2 + 1)
                for i in range(4):
                    c = 4 * g + i
                    last = nc.tensor.transpose(ps[g % 4][:, i * P:i * P + P], big[:, c * P:c * P + P], ident[:])
                last.then_inc(w_t, 1)
            pe.wait_ge(v_m, 5)
            for c in range(NC):
                last = nc.tensor.matmul(ps[c // 16][:, (c % 16) * H:(c % 16 + 1) * H], tmp[:, c * P:c * P + P], cbT[:],
                                        start=True, stop=True)
            last.then_inc(pe_m, 1)
            pe.wait_ge(v_m, 6)
            for i in range(2):
                nc.tensor.matmul(ps[2 + i][:], mats[:, 0, :], s[2][:, 512 * i:512 * i + 512], start=True, stop=True)
                last = nc.tensor.matmul(ps[4 + i][:], ones[:, 0:P], s[2][:, 512 * i:512 * i + 512], start=True, stop=True)
            last.then_inc(pe_m, 1)
            pe.wait_ge(v_m, 7)
            for i in range(2):
                n = 512 - H * i
                nc.tensor.matmul(ps[i][:], mats[:, 1, :], s[1][:, 512 * i:512 * i + 512], start=True, stop=False)
                last = nc.tensor.matmul(ps[i][:, 0:n], mats[:, 2, :], s[1][:, 512 * i + H:512 * i + H + n], start=False, stop=True)
            last.then_inc(pe_m, 1)
            pe.wait_ge(v_m, 8)
            for g in range(8):
                if g >= 1:
                    pe.wait_ge(v_m, 8 + g)
                for i in range(4):
                    last = nc.tensor.transpose(ps_bf[0:3 * H, i, :], cum3[:, 4 * g + i, :], K["ident_bf"][:])
                last.then_inc(pe_m, 1)

        def weight_out(g, copy):
            b = ps[g % 4]
            if g < 8:
                return [copy(K["w_zx"][:, 512 * g:512 * g + 512], b[:])]
            if g == 8:
                return [copy(wbc[:], b[:, 0:P]), copy(wdl[:], b[:, P:P + 64]), copy(K["w_ffn"][:], b[:, 2 * P:3 * P]),
                        copy(K["prmT"][:, 0:80], b[:, 3 * P:3 * P + 80])]
            if g == 15:
                return [copy(cbT[:], b[:, 0:H])]
            raise AssertionError

        @block.vector
        def _(dve):
            n = [0]

            def link(ins):
                n[0] += 1
                ins.then_inc(dch, 1)
                dve.wait_ge(dch, n[0])

            def rsqrt_refined(r, v, t):
                link(nc.vector.tensor_tensor(t, r, r, ALU.mult))
                link(nc.vector.tensor_tensor(t, t, v, ALU.mult))
                link(nc.vector.tensor_scalar(t, t, -0.5, 1.5, ALU.mult, ALU.add))
                link(nc.vector.tensor_tensor(r, r, t, ALU.mult))

            big3 = big[:].rearrange("p (c m) -> p c m", c=NC)
            tmp3 = tmp[:].rearrange("p (c m) -> p c m", c=NC)
            st = [st32[:, i, 0:NC] for i in range(8)]
            dve.wait_ge(consts, 1)
            for g in range(0, NG, 2):
                dve.wait_ge(w_t, g + 1)
                b = ps[g % 4]
                if g in (10,):
                    dst = K["w_th"][:, 1024:2048].rearrange("p (h d j) -> p h d j", h=16, d=2)
                    src = b[:].rearrange("p (h j) -> p h j", h=16).unsqueeze(2)
                    link(nc.vector.tensor_scalar(dst, bcast(src, [P, 16, 2, 32]), 0.15915494309189535, None, ALU.mult))
                    dve.sem_inc(w_v, 1)
                elif g in (12, 14):
                    a0 = 4 * (g - 11)
                    for i in range(4):
                        link(nc.vector.tensor_scalar(K["w_o"][:, (a0 + i) * P:(a0 + i + 1) * P], b[:, i * P:i * P + P],
                                                     K["prmT"][:, a0 + i:a0 + i + 1], None, ALU.mult))
                    dve.sem_inc(w_v, 1)
                else:
                    outs = weight_out(g, nc.vector.tensor_copy)
                    for o in outs[:-1]:
                        link(o)
                    outs[-1].then_inc(w_v, 1)
            dve.wait_ge(w_v, NG // 2)
            dve.wait_ge(loaded[0], 16)
            link(nc.vector.tensor_reduce(st[0], big3, AX.X, ALU.add))
            link(nc.vector.tensor_scalar(st[0], st[0], 1.0 / DM, None, ALU.mult))
            dve.wait_ge(w_a, NG // 2)
            link(nc.vector.tensor_tensor(big3, big3, bcast(st[0].unsqueeze(2), [P, NC, DM]), ALU.subtract))
            link(nc.vector.tensor_tensor(tmp3, big3, big3, ALU.mult))
            link(nc.vector.tensor_reduce(st[1], tmp3, AX.X, ALU.add))
            link(nc.vector.tensor_scalar(st[1], st[1], 1.0 / DM, EPS, ALU.mult, ALU.add))
            dve.sem_inc(for_act, 1)
            dve.wait_ge(a_m, 1)
            link(nc.vector.reciprocal(st[3], st[2]))
            rsqrt_refined(st[3], st[1], st[5])
            link(nc.vector.tensor_tensor(big3, big3, bcast(st[3].unsqueeze(2), [P, NC, DM]), ALU.mult))
            dve.sem_inc(xn_done, 1)
            link(nc.vector.tensor_reduce(am[:, 0:1], big[:], AX.X, ALU.max))
            link(nc.vector.tensor_reduce(st[6][:, 0:1], big[:], AX.X, ALU.min))
            link(nc.vector.tensor_reduce(am[:, 1:2], stage2[:, 10 * P:11 * P], AX.X, ALU.max))
            link(nc.vector.tensor_reduce(st[6][:, 1:2], stage2[:, 10 * P:11 * P], AX.X, ALU.min))
            link(nc.vector.tensor_scalar(st[6][:, 0:2], st[6][:, 0:2], -1.0, None, ALU.mult))
            nc.vector.tensor_tensor(am[:, 0:2], am[:, 0:2], st[6][:, 0:2], ALU.max).then_inc(v_m, 1)
            for g in range(0, 8, 2):
                dve.wait_ge(w_t, NG + g + 1)
                nc.vector.tensor_copy(xnT[:, 512 * g:512 * g + 512], ps[g % 4][:]).then_inc(w_v, 1)
            dve.wait_ge(w_a, NG // 2 + 4)
            dve.wait_ge(w_v, NG // 2 + 4)
            for b in range(BATCH):
                link(nc.vector.tensor_tensor_scan(tcT[:, b * L:(b + 1) * L], one_row[:], xnT[:, b * L:(b + 1) * L],
                                                  0.0, ALU.mult, ALU.add))
            dve.sem_inc(v_m, 1)
            link(nc.vector.tensor_copy(K["sel_pair"][:].rearrange("k (h d) -> k h d", d=64),
                                       bcast(K["sel"][:].unsqueeze(2), [3 * H, H, 64])))
            dve.wait_ge(pe_m, 1)
            link(nc.vector.tensor_copy(rowb[:], ps[4][:, 0:row.shape[1]]))
            link(nc.vector.tensor_copy(K["d_ffnb"][:], rowb[:, 3 * H:3 * H + P]))
            dve.wait_ge(pe_m, 2)
            link(nc.vector.tensor_reduce(st[6][0:2, 2:3], ps[5][0:2, 0:P], AX.X, ALU.max))
            link(nc.vector.tensor_scalar(am2[0:2, 0:2], ident[0:2, 0:2], st[6][0:2, 2:3], None, ALU.mult))
            link(nc.vector.tensor_tensor(cb1[:], cbn[:, 0:N], cbn[:, N:2 * N], ALU.mult))
            link(nc.vector.tensor_reduce(cbs[:], cb1[:], AX.X, ALU.add))
            nc.vector.tensor_copy(cbs2[:], bcast(cbs[:], [H, P])).then_inc(v_m, 1)
            dlv = dl[:].rearrange("p (c k) -> p c k", k=64)
            for g in range(0, 12, 2):
                dve.wait_ge(w_t, NG + 8 + g + 1)
                if g < 8:
                    nc.vector.tensor_copy(big[:, 512 * g:512 * g + 512], ps[g % 4][:]).then_inc(w_v, 1)
                else:
                    nc.vector.tensor_copy(dl[:, 512 * (g - 8):512 * (g - 7)], ps[g % 4][:]).then_inc(w_v, 1)
            dve.wait_ge(pe_m, 3)
            link(nc.vector.tensor_copy(K["amax"][:], ps[6][:, 0:2]))
            link(nc.vector.tensor_copy(cbb[:], ps[6][:, 64:64 + H]))
            dve.wait_ge(w_a, NG // 2 + 10)
            dve.wait_ge(w_v, NG // 2 + 10)
            big64 = big[:].rearrange("p (g n) -> p g n", n=N)
            tmp64 = tmp[:].rearrange("p (g n) -> p g n", n=N)
            v64, r64, t64 = st32[:, 1, :], st32[:, 3, :], st32[:, 5, :]
            link(nc.vector.tensor_tensor(tmp[:], big[:], big[:], ALU.mult))
            link(nc.vector.tensor_reduce(v64, tmp64, AX.X, ALU.add))
            link(nc.vector.tensor_scalar(v64, v64, 1.0 / N, EPS, ALU.mult, ALU.add))
            dve.sem_inc(for_act, 1)
            dve.wait_ge(a_m, 2)
            link(nc.vector.reciprocal(r64, st32[:, 2, :]))
            rsqrt_refined(r64, v64, t64)
            link(nc.vector.tensor_tensor(big64, big64, bcast(r64.unsqueeze(2), [P, 2 * NC, N]), ALU.mult))
            wn = rowb[:, 3 * H + P:3 * H + 2 * P].unsqueeze(1)
            link(nc.vector.tensor_tensor(big3, big3, bcast(wn, [P, NC, P]), ALU.mult))
            pr = tcT[:, 0:NC * N].rearrange("p (c n) -> p c n", n=N)
            dve.wait_ge(stored, 32)
            link(nc.vector.tensor_tensor(pr, big3[:, :, 0:N], big3[:, :, N:2 * N], ALU.mult))
            link(nc.vector.tensor_reduce(st[0], pr, AX.X, ALU.add))
            dve.sem_inc(v_m, 1)
            for g in range(0, 8, 2):
                dve.wait_ge(w_t, NG + 20 + g + 1)
                nc.vector.tensor_copy(tmp[:, 512 * g:512 * g + 512], ps[g % 4][:]).then_inc(w_v, 1)
            dve.wait_ge(w_a, NG // 2 + 14)
            dve.wait_ge(w_v, NG // 2 + 14)
            dve.sem_inc(v_m, 1)
            v3 = [x[:].rearrange("p (c h) -> p c h", h=H) for x in s]
            one_h = lambda a: bcast(rowb[:, a * H:(a + 1) * H].unsqueeze(1), [P, NC, H])
            link(nc.vector.tensor_tensor(v3[0], dlv[:, :, 0:H], one_h(0), ALU.add))
            link(nc.vector.tensor_scalar(s[1][:], s[0][:], -1.0, None, ALU.mult))
            link(nc.vector.tensor_tensor(s[1][:], s[1][:], s[0][:], ALU.min))
            nc.vector.tensor_copy(v3[3], dlv[:, :, H:2 * H]).then_inc(for_act, 1)
            dve.wait_ge(a_m, 3)
            link(nc.vector.tensor_scalar(s[2][:], s[1][:], 1.0, None, ALU.add))
            nc.vector.tensor_copy(K["kk"][:], s[2][:]).then_inc(for_act, 1)
            link(nc.vector.tensor_scalar(K["dec"][:], s[2][:], -1.0, None, ALU.add))
            link(nc.vector.tensor_tensor(s[1][:], s[1][:], K["dec"][:], ALU.subtract))
            link(nc.vector.reciprocal(K["dec"][:], s[2][:]))
            link(nc.vector.tensor_tensor(s[1][:], s[1][:], K["dec"][:], ALU.mult))
            link(nc.vector.tensor_scalar(s[0][:], s[0][:], 0.0, None, ALU.max))
            link(nc.vector.tensor_tensor(s[0][:], s[0][:], s[1][:], ALU.add))
            dve.wait_ge(a_m, 4)
            link(nc.vector.tensor_tensor(s[0][:], s[0][:], K["kk"][:], ALU.add))
            link(nc.vector.tensor_scalar(s[3][:], s[3][:], 1.0, None, ALU.add))
            link(nc.vector.reciprocal(s[3][:], s[3][:]))
            link(nc.vector.tensor_tensor(K["kk"][:], s[3][:], s[0][:], ALU.mult))
            link(nc.vector.tensor_scalar(s[1][:], s[3][:], -1.0, 1.0, ALU.mult, ALU.add))
            link(nc.vector.tensor_tensor(s[1][:], s[1][:], s[0][:], ALU.mult))
            link(nc.vector.tensor_scalar(s[0][:], s[0][:], -1.0, None, ALU.mult))
            link(nc.vector.tensor_tensor(v3[2], v3[0], one_h(1), ALU.mult))
            dve.sem_inc(v_m, 1)
            dve.wait_ge(pe_m, 4)
            for i in range(2):
                o = v3[3][:, 16 * i:16 * i + 16, :]
                link(nc.vector.tensor_tensor(o, ps[i][:].rearrange("p (c h) -> p c h", h=H),
                                             bcast(st[0][:, 16 * i:16 * i + 16].unsqueeze(2), [P, 16, H]), ALU.add))
            link(nc.vector.tensor_tensor(v3[3], v3[3], bcast(cbb[:].unsqueeze(1), [P, NC, H]), ALU.add))
            dve.sem_inc(v_m, 1)
            dve.wait_ge(pe_m, 5)
            for i in range(2):
                a, b = 512 * i, 512 * i + 512
                link(nc.vector.tensor_copy(s[0][:, a:b], ps[2 + i][:]))
                link(nc.vector.tensor_tensor(K["dec"][:, a:b], ps[4 + i][:], s[0][:, a:b], ALU.subtract))
            dt3 = K["dtot"][:].rearrange("p (c r) -> p c r", r=NP)
            for i in range(2):
                for j in range(2):
                    q = slice(64 * j, 64 * j + 64)
                    link(nc.vector.tensor_copy(dt3[q, 16 * i:16 * i + 16, :],
                                               ps[4 + i][q, :].rearrange("p (c r j) -> p c r j", r=NP, j=2)[:, :, :, j]))
            c0 = s[0][:].rearrange("p (c h) -> p c h", h=H)
            for i in range(3):
                part = cum3[:, :, H * i:H * i + H]
                link(nc.vector.tensor_copy(part, c0))
                if i < 2:
                    link(nc.vector.tensor_tensor(c0, c0, part, ALU.subtract))
            dve.sem_inc(v_m, 1)
            dve.wait_ge(pe_m, 6)
            for i in range(2):
                a, b = 512 * i, 512 * i + 512
                link(nc.vector.tensor_tensor(K["kk"][:, a:b], K["kk"][:, a:b], ps[i][:], ALU.add))
                link(nc.vector.tensor_tensor(s[3][:, a:b], s[3][:, a:b], ps[i][:], ALU.mult))
            cc3 = K["cc"][:].rearrange("p (c h) -> p c h", h=H)
            link(nc.vector.tensor_scalar(s[3][:], s[3][:], -1.0, None, ALU.mult))
            link(nc.vector.tensor_tensor(cc3, v3[3], one_h(2), ALU.add))
            for g in range(8):
                dve.wait_ge(pe_m, 7 + g)
                nc.vector.tensor_copy(K["cumT"][:, 512 * g:512 * g + 512],
                                      ps_bf[0:3 * H].rearrange("p c t -> p (c t)")).then_inc(v_m, 1)


        @block.scalar
        def _(act):
            n = [0]

            def link(ins):
                n[0] += 1
                ins.then_inc(ach, 1)
                act.wait_ge(ach, n[0])

            act.wait_ge(consts, 1)
            for g in range(1, NG, 2):
                act.wait_ge(w_t, g + 1)
                b = ps[g % 4]
                if g == 9:
                    dst = K["w_th"][:, 0:1024].rearrange("p (h d j) -> p h d j", h=16, d=2)
                    for d in range(2):
                        link(nc.scalar.mul(dst[:, :, d, :], b[:].rearrange("p (h j) -> p h j", h=16), 0.15915494309189535))
                    act.sem_inc(w_a, 1)
                elif g in (11, 13):
                    act.wait_ge(w_v, 5)
                    a0 = 4 * (g - 11)
                    for i in range(4):
                        link(nc.scalar.activation(K["w_o"][:, (a0 + i) * P:(a0 + i + 1) * P], b[:, i * P:i * P + P],
                                                  ACT.Copy, scale=K["prmT"][:, a0 + i:a0 + i + 1]))
                    act.sem_inc(w_a, 1)
                else:
                    weight_out(g, nc.scalar.copy)[0].then_inc(w_a, 1)
            act.wait_ge(for_act, 1)
            nc.scalar.activation(st32[:, 2, 0:NC], st32[:, 1, 0:NC], ACT.Sqrt).then_inc(a_m, 1)
            for g in range(1, 8, 2):
                act.wait_ge(w_t, NG + g + 1)
                nc.scalar.copy(xnT[:, 512 * g:512 * g + 512], ps[g % 4][:]).then_inc(w_a, 1)
            for g in range(1, 12, 2):
                act.wait_ge(w_t, NG + 8 + g + 1)
                dst = big[:, 512 * g:512 * g + 512] if g < 8 else dl[:, 512 * (g - 8):512 * (g - 7)]
                nc.scalar.copy(dst, ps[g % 4][:]).then_inc(w_a, 1)
            act.wait_ge(for_act, 2)
            nc.scalar.activation(st32[:, 2, :], st32[:, 1, :], ACT.Sqrt).then_inc(a_m, 1)
            for g in range(1, 8, 2):
                act.wait_ge(w_t, NG + 20 + g + 1)
                nc.scalar.copy(tmp[:, 512 * g:512 * g + 512], ps[g % 4][:]).then_inc(w_a, 1)
            act.wait_ge(for_act, 3)
            link(nc.scalar.activation(rowb[:, H:2 * H], rowb[:, H:2 * H], ACT.Exp))
            link(nc.scalar.activation(s[3][:], s[3][:], ACT.Exp, scale=-1.0))
            nc.scalar.activation(s[1][:], s[1][:], ACT.Exp).then_inc(a_m, 1)
            act.wait_ge(for_act, 4)
            nc.scalar.activation(K["kk"][:], K["kk"][:], ACT.Ln).then_inc(a_m, 1)
            act.wait_ge(v_m, 8)
            link(nc.scalar.activation(K["dec"][:], K["dec"][:], ACT.Exp))
            link(nc.scalar.activation(K["dtot"][:], K["dtot"][:], ACT.Exp))


def units(nc, K, scratch):
    xn_d, tc_d, bc_d = scratch
    with ExitStack() as ctx:
        def sb(name, shape, dt=F32):
            return ctx.enter_context(nc.sbuf_tensor(name, shape, dt))

        def sem(name):
            return ctx.enter_context(nc.semaphore(name))

        def bank(name):
            return ctx.enter_context(nc.psum_tensor(name, [P, 512], F32))

        R = [bank("r0"), bank("r1")]
        Dp = bank("d")
        Op = bank("o")
        Sp = [bank("s0"), bank("s1")]
        Yp = [bank("y0"), bank("y1")]

        LOADS = 16 * 14
        xnz = sb("xnz", [P, ST])
        xns = sb("xns", [P, ST])
        tcs = sb("tcs", [P, ST])
        bcs = sb("bcs", [P, 4, ST])
        rnd = sb("rnd", [P, 2, ST])
        ang = sb("ang", [P, 2, ST])
        sn = sb("sn", [P, 2, ST])
        cs = sb("cs", [P, 2, ST])
        part = sb("part", [P, 4, ST])
        rot = sb("rot", [P, 2, 2, 2, ST])
        eb = sb("eb", [P, 2, ST])
        ce = sb("ce", [P, 2, ST])
        xk = sb("xk", [P, 2, CS, 4 * HD])
        xc = sb("xc", [P, 2, CS, 4 * HD])
        E = sb("E", [P, 2, ST])
        M = sb("M", [P, 4, ST])
        bw = sb("bw", [P, 2, CS, P])
        hs = sb("hs", [P, CS, 2, HD])
        th = sb("th", [P, 2, ST])
        yT = sb("yT", [P, 2, ST])
        sq = sb("sq", [P, 2, ST])
        sqa = sb("sqa", [P, ST])

        sb_loaded = sem("sb_loaded")
        u_ready, bt_ready, x_ready, eb_ready = sem("u_ready"), sem("bt_ready"), sem("x_ready"), sem("eb_ready")
        st_ready, z_ready, out_ready, ssq_ready = sem("st_ready"), sem("z_ready"), sem("out_ready"), sem("ssq_ready")
        d_ready, s_ready, y_ready = sem("d_ready"), sem("s_ready"), sem("y_ready")
        e_ready, m_ready = sem("e_ready"), sem("m_ready")
        rounded, turned, absd = sem("rounded"), sem("turned"), sem("absd")
        sin_ready = sem("sin_ready")
        part_ready, rot_ready = sem("part_ready"), sem("rot_ready")
        ebs_ready, ce_ready = sem("ebs_ready"), sem("ce_ready")
        xk_ready, bw_ready, h_ready = sem("xk_ready"), sem("bw_ready"), sem("h_ready")
        th_ready, sz_ready, yt_ready, sq_ready = sem("th_ready"), sem("sz_ready"), sem("yt_ready"), sem("sq_ready")
        sqa_ready = sem("sqa_ready")
        hch = sem("hch")
        acc_done, ssq_taken, z_loaded = sem("acc_done"), sem("ssq_taken"), sem("z_loaded")
        block = ctx.enter_context(nc.Block())

        def at(per, t, k):
            return t * per + max(k, 0) + 1

        T1, T2, T4, T8 = NQ, 2 * NQ, 4 * NQ, 8 * NQ

        def follow(t, q):
            return t + 1 if q == NQ - 1 else t

        @block.sync
        def _(sp):
            def load(t):
                sp.dma_start(xns[:], xn_d[t]).then_inc(sb_loaded, 16)
                sp.dma_start(tcs[:], tc_d[t]).then_inc(sb_loaded, 16)
                for i in range(2):
                    for j in range(2):
                        sp.dma_start(bcs[64 * j:64 * j + 64, 2 * i, :], bc_d[t, 64 * i:64 * i + 64, :]).then_inc(sb_loaded, 16)
                        for f in range(2):
                            r = 64 * j + 32 * f
                            sp.dma_start(bcs[r:r + 32, 2 * i + 1, :],
                                         bc_d[t, 64 * i + 32 * (1 - f):64 * i + 32 * (2 - f), :]).then_inc(sb_loaded, 16)

            load(0)
            sp.dma_start(xnz[:], xn_d[0]).then_inc(z_loaded, 16)
            with sp.Fori(0, NS) as t:
                sp.wait_ge(u_ready, at(T2, t, T2))
                sp.wait_ge(x_ready, at(T2, t, T2))
                sp.wait_ge(part_ready, at(T8, t, T8))
                load((t + 1) % NS)
                sp.wait_ge(z_ready, at(T2, t, T2))
                sp.dma_start(xnz[:], xn_d[(t + 1) % NS]).then_inc(z_loaded, 16)
            sp.wait_ge(sb_loaded, LOADS * (NS + 1))
            sp.wait_ge(z_loaded, 16 * (NS + 1))


        @block.tensor
        def _(pe):
            for s in (u_ready, bt_ready, x_ready, eb_ready, st_ready, z_ready, out_ready, ssq_ready, d_ready, s_ready, y_ready):
                pe.sem_inc(s, 1)

            def angles(t, q, p):
                w = K["w_th"][:, (q * 2 + p) * P:(q * 2 + p + 1) * P]
                nc.tensor.matmul(R[p][:], w, tcs[:], start=True, stop=True).then_inc(u_ready, 1)

            def x_by_token(q, i):
                for c in range(2):
                    last = nc.tensor.matmul(R[1 - i][:, 256 * c:256 * c + 256], xns[:, (2 * i + c) * P:(2 * i + c + 1) * P],
                                            K["w_zx"][:, DI + q * 256:DI + q * 256 + 256], start=True, stop=True)
                last.then_inc(x_ready, 1)

            def b_by_token(q, p):
                for c in range(CS):
                    last = nc.tensor.transpose(R[1 - p][:, c * P:c * P + P], rot[:, q % 2, p, 0, c * P:c * P + P], K["ident"][:])
                last.then_inc(bt_ready, 1)

            def exponents(t, q, tt, h):
                pe.wait_ge(e_ready, at(T4, t, 4 * q + h))
                head = 4 * (q % NQ) + h
                nc.tensor.matmul(Dp[:], K["ident_bf"][:], K["mask"][:], start=True, stop=False, skip_group_check=True)
                nc.tensor.matmul(Dp[:], bcast(K["sel"][:, head:head + 1], [3 * H, P]), K["cumT"][:, bass.ds(tt * ST, ST)],
                                 start=False, stop=False, skip_group_check=True)
                for c in range(CS):
                    last = nc.tensor.matmul(Dp[:, c * P:c * P + P], K["cumT"][:, bass.ds(tt * ST + c * P, P)],
                                            bcast(K["nsel"][:, head:head + 1], [3 * H, P]), start=False,
                                            stop=c == CS - 1, skip_group_check=True)
                last.then_inc(d_ready, 1)

            def scores(t, q, h):
                p, rows = h // 2, slice(64 * (h % 2), 64 * (h % 2) + 64)
                pe.wait_ge(m_ready, at(T4, t, 4 * q + h - 1))
                for c in range(CS):
                    k = slice(c * P, c * P + P)
                    last = nc.tensor.matmul(Sp[h % 2][:, k], rot[rows, q % 2, p, 0, k], rot[rows, q % 2, p, 1, k],
                                            start=True, stop=True)
                last.then_inc(s_ready, 1)

            pe.wait_ge(sb_loaded, LOADS)
            angles(0, 0, 0)
            angles(0, 0, 1)
            for i in range(2):
                pe.wait_ge(turned, at(T2, 0, 2))
                x_by_token(0, i)
            for p in range(2):
                pe.wait_ge(rot_ready, at(T4, 0, 4))
                pe.wait_ge(xk_ready, at(T2, 0, p + 1))
                b_by_token(0, p)
            for h in range(2):
                exponents(0, 0, 0, h)
                scores(0, 0, h)
            with pe.Fori(0, NS) as t:
                for q in range(NQ):
                    par = q % 2
                    tn = t if q < NQ - 1 else (t + 1) % NS
                    if q == NQ - 1:
                        pe.wait_ge(sb_loaded, (t + 2) * LOADS)
                    for p in range(2):
                        pe.wait_ge(bw_ready, at(T2, t, 2 * q + 2 - p))
                        angles(t, (q + 1) % NQ, p)
                    exponents(t, q, t, 2)
                    scores(t, q, 2)
                    pe.wait_ge(turned, at(T2, t, 2 * q + 3))
                    for c in range(CS):
                        for p in range(2):
                            for j in range(2):
                                last = nc.tensor.matmul(R[0][64 * j:64 * j + 64, (2 * c + p) * 64:(2 * c + p) * 64 + 64],
                                                        bw[:, p, c, 64 * j:64 * j + 64],
                                                        xk[:, par, c, (2 * p + j) * 64:(2 * p + j) * 64 + 64],
                                                        start=True, stop=True)
                    last.then_inc(st_ready, 1)
                    exponents(t, q, t, 3)
                    scores(t, q, 3)
                    for p in range(2):
                        if p == 0:
                            pe.wait_ge(turned, at(T2, t, 2 * q + 4))
                        else:
                            pe.wait_ge(h_ready, at(T1, t, q + 1))
                        nc.tensor.matmul(R[1 - p][:], K["sel_pair"][:, (2 * q + p) * P:(2 * q + p + 1) * P],
                                         K["cumT"][:, bass.ds(t * ST, ST)], start=True, stop=True).then_inc(eb_ready, 1)
                    for i in range(2):
                        pe.wait_ge(ebs_ready, at(T2, t, 2 * q + i + 1))
                        x_by_token((q + 1) % NQ, i)
                    if q == 0:
                        pe.wait_ge(z_loaded, (t + 1) * 16)
                    for p in range(2):
                        pe.wait_ge(xk_ready, at(T2, t, 2 * q + 2 + p + 1))
                        w = K["w_zx"][:, (2 * q + p) * P:(2 * q + p + 1) * P]
                        nc.tensor.matmul(R[1 - p][:], w, xnz[:], start=True, stop=True).then_inc(z_ready, 1)
                    for p in range(2):
                        pe.wait_ge(m_ready, at(T4, t, 4 * q + 2 * p + 2))
                        pe.wait_ge(ce_ready, at(T2, t, 2 * q + p + 1))
                        pe.wait_ge(yt_ready, at(T2, t, 2 * q - 1 + p))
                        for c in range(CS):
                            k = slice(c * P, c * P + P)
                            nc.tensor.matmul(Yp[p][:, k], xc[:, par, c, 128 * p:128 * p + 128], K["ident"][:],
                                             start=True, stop=False, is_transpose=True, skip_group_check=True)
                            for j in range(2):
                                nc.tensor.matmul(Yp[p][64 * j:64 * j + 64, k],
                                                 xk[:, par, c, (2 * p + j) * 64:(2 * p + j) * 64 + 64], M[:, 2 * p + j, k],
                                                 start=False, stop=False, skip_group_check=True)
                            for j in range(2):
                                rows = slice(64 * j, 64 * j + 64)
                                last = nc.tensor.matmul(Yp[p][rows, k], hs[rows, c, p, :], ce[rows, p, k],
                                                        start=False, stop=True, skip_group_check=True)
                        last.then_inc(y_ready, 1)
                    pe.wait_ge(rot_ready, at(T4, t, 4 * q + 8))
                    for p in range(2):
                        pe.wait_ge(sz_ready, at(T2, t, 2 * q + p + 1))
                        b_by_token(q + 1, p)
                    for h in range(2):
                        if h == 0 and q == NQ - 1:
                            pe.wait_ge(sqa_ready, at(T2, t, T2))
                            for c in range(CS):
                                last = nc.tensor.matmul(Dp[:, c:c + 1], sqa[:, c * P:c * P + P], K["ones"][:, 0:1],
                                                        start=True, stop=True)
                            last.then_inc(ssq_ready, 1)
                            pe.wait_ge(ssq_taken, at(1, t, 1))
                        exponents(t, q + 1, tn, h)
                        scores(t, q + 1, h)
                    if q == 0:
                        pe.wait_ge(acc_done, at(1, t, 0))
                        nc.tensor.matmul(Op[:], K["zeros_bf"][:], K["mask"][:], start=True, stop=False, skip_group_check=True)
                    pe.wait_ge(yt_ready, at(T2, t, 2 * q + 2))
                    for c in range(CS):
                        k = slice(c * P, c * P + P)
                        for p in range(2):
                            last = nc.tensor.matmul(Op[:, k], yT[:, p, k], K["w_o"][:, (2 * q + p) * P:(2 * q + p + 1) * P],
                                                    start=False, stop=q == NQ - 1 and c == CS - 1 and p == 1,
                                                    skip_group_check=True)
                    last.then_inc(out_ready, 1)

        @block.vector
        def _(dve):
            for s in (turned, bw_ready, m_ready, xk_ready, hch, h_ready, part_ready, sz_ready, yt_ready, acc_done, ssq_taken):
                dve.sem_inc(s, 1)

            def angles(t, q):
                for p in range(2):
                    dve.wait_ge(rounded, at(T2, t, 2 * q + p + 1))
                    dve.wait_ge(sin_ready, at(T4, t, 4 * q - 4 + 2 * p + 2))
                    nc.vector.scalar_tensor_tensor(out=ang[:, p, :], in0=rnd[:, p, :], scalar=MAGIC, in1=R[p][:],
                                                   op0=ALU.subtract, op1=ALU.subtract).then_inc(turned, 1)

            def x_scaled(t, q, tt):
                for p in range(2):
                    dve.wait_ge(x_ready, at(T2, t, 2 * q + p + 1))
                    dve.wait_ge(y_ready, at(T2, t, 2 * q - 2))
                    for dst, f in ((xk, "kk"), (xc, "cc")):
                        v = K[f][:, bass.ds(tt * (CS * H) + 2 * p * H, 2 * H)].rearrange("p (c h) -> p c h", h=H)
                        v = v[:, :, 4 * (q % NQ):4 * (q % NQ) + 4].unsqueeze(3)
                        last = nc.vector.tensor_tensor(dst[:, q % 2, 2 * p:2 * p + 2, :].rearrange("p c (h d) -> p c h d", h=4),
                                                       R[1 - p][:].rearrange("p (c h d) -> p c h d", c=2, h=4),
                                                       bcast(v, [P, 2, 4, HD]), ALU.mult)
                    last.then_inc(xk_ready, 1)

            def rotation(t, q):
                if q % NQ == 0:
                    dve.wait_ge(sb_loaded, (t + (q // NQ + 1)) * LOADS)
                for p in range(2):
                    pair = (q % NQ) * 2 + p
                    dve.wait_ge(sin_ready, at(T4, t, 4 * q + 2 * p + 2))
                    for w in range(2):
                        dve.wait_ge(rot_ready, at(T4, t, 4 * q + 2 * p + w - 1))
                        for f, trig in ((0, cs), (1, sn)):
                            col = K["prmT"][:, 16 * (1 + 2 * w + f) + pair:16 * (1 + 2 * w + f) + pair + 1]
                            nc.vector.scalar_tensor_tensor(out=part[:, 2 * w + f, :], in0=bcs[:, 2 * w + f, :], scalar=col,
                                                           in1=trig[:, p, :], op0=ALU.add, op1=ALU.mult).then_inc(part_ready, 1)

            def b_decayed(t, q, tt):
                dve.wait_ge(st_ready, at(T1, t, q))
                for p in range(2):
                    dve.wait_ge(bt_ready, at(T2, t, 2 * q + p + 1))
                    v = K["dec"][:, bass.ds(tt * (CS * H), CS * H)].rearrange("p (c h) -> p c h", h=H)
                    v = v[:, :, 4 * (q % NQ) + 2 * p:4 * (q % NQ) + 2 * p + 2].unsqueeze(3)
                    nc.vector.tensor_tensor(bw[:, p, :, :].rearrange("p c (j n) -> p c j n", j=2),
                                            R[1 - p][:].rearrange("p (c j n) -> p c j n", c=CS, j=2),
                                            bcast(v, [P, CS, 2, N]), ALU.mult).then_inc(bw_ready, 1)

            def scores(t, q, h):
                dve.wait_ge(e_ready, at(T4, t, 4 * q + h + 1))
                dve.wait_ge(s_ready, at(T4, t, 4 * q + h + 1))
                dve.wait_ge(y_ready, at(T2, t, 2 * q - 1 + h // 2))
                nc.vector.tensor_tensor(M[:, h, :], Sp[h % 2][:], E[:, h % 2, :], ALU.mult).then_inc(m_ready, 1)

            angles(0, 0)
            x_scaled(0, 0, 0)
            rotation(0, 0)
            b_decayed(0, 0, 0)
            scores(0, 0, 0)
            scores(0, 0, 1)
            with dve.Fori(0, NS) as t:
                def state(q, c):
                    dve.wait_ge(hch, at(9 * NQ, t, 9 * q + 1 + 2 * c))
                    for p in range(2):
                        dst = hs[:, c + 1, p, :] if c < CS - 1 else K["carry"][:, 2 * q + p, :]
                        nc.vector.scalar_tensor_tensor(
                            out=dst, in0=hs[:, c, p, :], scalar=K["dtot"][:, bass.ds(t * (CS * NP) + c * NP + 2 * q + p, 1)],
                            in1=R[0][:, (2 * c + p) * 64:(2 * c + p) * 64 + 64], op0=ALU.mult, op1=ALU.add).then_inc(hch, 1)

                for q in range(NQ):
                    tn = t if q < NQ - 1 else (t + 1) % NS
                    dve.wait_ge(y_ready, at(T2, t, 2 * q))
                    dve.wait_ge(hch, at(9 * NQ, t, 9 * q))
                    nc.vector.tensor_scalar(hs[:, 0, :, :], K["carry"][:, 2 * q:2 * q + 2, :], K["goes_on"][:, bass.ds(t, 1)],
                                            None, ALU.mult).then_inc(hch, 1)
                    angles(t, q + 1)
                    dve.wait_ge(st_ready, at(T1, t, q + 1))
                    state(q, 0)
                    scores(t, q, 2)
                    state(q, 1)
                    state(q, 2)
                    state(q, 3)
                    dve.wait_ge(hch, at(9 * NQ, t, 9 * q + 9))
                    dve.sem_inc(h_ready, 1)
                    scores(t, q, 3)
                    x_scaled(t, q + 1, tn)
                    rotation(t, q + 1)
                    for p in range(2):
                        dve.wait_ge(th_ready, at(T2, t, 2 * q + p + 1))
                        nc.vector.scalar_tensor_tensor(out=th[:, p, :], in0=th[:, p, :], scalar=1.0, in1=R[1 - p][:],
                                                       op0=ALU.add, op1=ALU.mult).then_inc(sz_ready, 1)
                    for p in range(2):
                        dve.wait_ge(sz_ready, at(T2, t, 2 * q + p + 1))
                        dve.wait_ge(y_ready, at(T2, t, 2 * q + p + 1))
                        dve.wait_ge(out_ready, at(T1, t, q))
                        dve.wait_ge(sq_ready, at(T2, t, 2 * q))
                        nc.vector.tensor_tensor(yT[:, p, :], Yp[p][:], th[:, p, :], ALU.mult).then_inc(yt_ready, 1)
                    b_decayed(t, q + 1, tn)
                    if q == NQ - 1:
                        dve.wait_ge(ssq_ready, at(1, t, 1))
                        nc.vector.tensor_copy(K["ssq"][:, bass.ds(t * CS, CS)], Dp[:, 0:CS]).then_inc(ssq_taken, 1)
                    scores(t, q + 1, 0)
                    scores(t, q + 1, 1)
                dve.wait_ge(out_ready, at(T1, t, T1))
                nc.vector.tensor_copy(K["s_acc"][:, bass.ds(t * ST, ST)], Op[:]).then_inc(acc_done, 1)

        @block.scalar
        def _(act):
            for s in (rounded, sin_ready, absd, e_ready, ebs_ready, th_ready, sq_ready):
                act.sem_inc(s, 1)

            def rounding(t, q):
                for p in range(2):
                    act.wait_ge(u_ready, at(T2, t, 2 * q + p + 1))
                    act.wait_ge(sin_ready, at(T4, t, 4 * q - 4 + 2 * p + 2))
                    nc.scalar.activation(rnd[:, p, :], R[p][:], ACT.Identity, bias=K["cols"][:, 3:4]).then_inc(rounded, 1)

            def sines(t, q):
                for p in range(2):
                    act.wait_ge(turned, at(T2, t, 2 * q + p + 1))
                    nc.scalar.activation(rnd[:, p, :], ang[:, p, :], ACT.Abs).then_inc(absd, 1)
                    act.wait_ge(part_ready, at(T8, t, 8 * q - 8 + 4 * p + 4))
                    nc.scalar.activation(sn[:, p, :], ang[:, p, :], ACT.Sin, scale=K["cols"][:, 0:1]).then_inc(sin_ready, 1)
                    act.wait_ge(absd, at(T2, t, 2 * q + p + 1))
                    nc.scalar.activation(cs[:, p, :], rnd[:, p, :], ACT.Sin, scale=-TWO_PI, bias=K["cols"][:, 1:2]).then_inc(sin_ready, 1)

            def decays(t, q, h):
                act.wait_ge(d_ready, at(T4, t, 4 * q + h + 1))
                act.wait_ge(m_ready, at(T4, t, 4 * q + h - 1))
                nc.scalar.activation(E[:, h % 2, :], Dp[:], ACT.Exp).then_inc(e_ready, 1)

            rounding(0, 0)
            sines(0, 0)
            decays(0, 0, 0)
            decays(0, 0, 1)
            with act.Fori(0, NS) as t:
                for q in range(NQ):
                    rounding(t, q + 1)
                    decays(t, q, 2)
                    decays(t, q, 3)
                    for p in range(2):
                        act.wait_ge(eb_ready, at(T2, t, 2 * q + p + 1))
                        act.wait_ge(ce_ready, at(T2, t, 2 * q - 1 + p))
                        nc.scalar.activation(eb[:, p, :], R[1 - p][:], ACT.Exp).then_inc(ebs_ready, 1)
                    sines(t, q + 1)
                    for p in range(2):
                        act.wait_ge(z_ready, at(T2, t, 2 * q + p + 1))
                        act.wait_ge(yt_ready, at(T2, t, 2 * q - 1 + p))
                        nc.scalar.activation(th[:, p, :], R[1 - p][:], ACT.Tanh, scale=0.5).then_inc(th_ready, 1)
                    for p in range(2):
                        act.wait_ge(yt_ready, at(T2, t, 2 * q + p + 1))
                        act.wait_ge(sqa_ready, at(T2, t, 2 * q - 1 + p))
                        nc.scalar.activation(sq[:, p, :], yT[:, p, :], ACT.Square).then_inc(sq_ready, 1)
                    decays(t, q + 1, 0)
                    decays(t, q + 1, 1)

        @block.gpsimd
        def _(pool):
            for s in (rot_ready, ce_ready, sqa_ready):
                pool.sem_inc(s, 1)

            def sums(t, q):
                for p in range(2):
                    for w in range(2):
                        pool.wait_ge(part_ready, at(T8, t, 8 * q + 4 * p + 2 * w + 2))
                        pool.wait_ge(y_ready, at(T2, t, 2 * q - 2))
                        nc.gpsimd.tensor_tensor(rot[:, q % 2, p, w, :], part[:, 2 * w, :], part[:, 2 * w + 1, :],
                                                ALU.add).then_inc(rot_ready, 1)

            sums(0, 0)
            with pool.Fori(0, NS) as t:
                pool.wait_ge(ssq_ready, at(1, t, 0))
                for q in range(NQ):
                    for p in range(2):
                        pool.wait_ge(ebs_ready, at(T2, t, 2 * q + p + 1))
                        pool.wait_ge(rot_ready, at(T4, t, 4 * q + 4))
                        pool.wait_ge(y_ready, at(T2, t, 2 * q - 1 + p))
                        nc.gpsimd.tensor_tensor(ce[:, p, :], rot[:, q % 2, p, 1, :], eb[:, p, :], ALU.mult).then_inc(ce_ready, 1)
                    sums(t, q + 1)
                    if q == 0:
                        pool.wait_ge(sq_ready, at(T2, t, 2))
                        nc.gpsimd.tensor_tensor(sqa[:], sq[:, 0, :], sq[:, 1, :], ALU.add).then_inc(sqa_ready, 1)
                        pool.wait_ge(sqa_ready, at(T2, t, 1))
                        pool.sem_inc(sqa_ready, 1)
                        continue
                    for p in range(2):
                        pool.wait_ge(sq_ready, at(T2, t, 2 * q + p + 1))
                        pool.wait_ge(sqa_ready, at(T2, t, 2 * q + p))
                        nc.gpsimd.tensor_tensor(sqa[:], sqa[:], sq[:, p, :], ALU.add).then_inc(sqa_ready, 1)


def finish(nc, K, u, xn_d, out):
    with ExitStack() as ctx:
        def sb(name, shape, dt=F32):
            return ctx.enter_context(nc.sbuf_tensor(name, shape, dt))

        def sem(name):
            return ctx.enter_context(nc.semaphore(name))

        ps = [ctx.enter_context(nc.psum_tensor(f"f_ps{i}", [P, 512], F32)) for i in range(2)]
        xn = sb("f_xn", [P, 2, ST])
        xin = sb("f_xin", [P, 2, ST])
        v = sb("f_v", [P, ST])
        half = sb("f_half", [P, ST], FP8)
        small = sb("f_small", [P, ST])
        tiny = sb("f_tiny", [P, ST])
        xq = sb("f_xq", [P, 2, ST], BF16)
        wq = sb("f_wq", [P, P], BF16)
        gate = sb("f_gate", [P, ST])
        th = sb("f_th", [P, ST])
        o = sb("f_o", [P, 2, ST])
        sc = sb("f_sc", [P, 6])
        r = sb("f_r", [P, 4, NC])
        loaded = [sem("f_loaded0"), sem("f_loaded1")]
        chain, for_act, act_done = sem("f_chain"), sem("f_for_act"), sem("f_act_done")
        xq_ready, g_ready, o_ready, g_taken, stored = sem("f_xq"), sem("f_g"), sem("f_o_ready"), sem("f_g_taken"), [sem("f_st0"), sem("f_st1")]
        block = ctx.enter_context(nc.Block())
        u_v = u.rearrange("b (s c p) m -> (b s) p c m", c=CS, p=P)
        o_v = out.rearrange("b (s c p) m -> (b s) p c m", c=CS, p=P)

        @block.sync
        def _(sp):
            for t in range(NS):
                if t >= 2:
                    sp.wait_ge(o_ready, t - 1)
                sp.dma_start(xn[:, t % 2, :], xn_d[t]).then_inc(loaded[t % 2], 16)
                sp.dma_start(xin[:, t % 2, :].rearrange("p (c m) -> p c m", c=CS), u_v[t]).then_inc(loaded[t % 2], 16)
                if t >= 1:
                    sp.wait_ge(o_ready, t)
                    sp.dma_start(o_v[t - 1], o[:, (t - 1) % 2, :].rearrange("p (c m) -> p c m", c=CS)).then_inc(stored[(t - 1) % 2], 16)
            sp.wait_ge(o_ready, NS)
            sp.dma_start(o_v[NS - 1], o[:, (NS - 1) % 2, :].rearrange("p (c m) -> p c m", c=CS)).then_inc(stored[(NS - 1) % 2], 16)
            for i in range(2):
                sp.wait_ge(stored[i], 16 * (NS // 2))

        @block.tensor
        def _(pe):
            for t in range(NS):
                pe.wait_ge(xq_ready, t + 2)
                if t >= 2:
                    pe.wait_ge(g_taken, t - 1)
                for c in range(CS):
                    last = nc.tensor.matmul(ps[t % 2][:, c * P:c * P + P], xq[:, t % 2, c * P:c * P + P], wq[:], start=True, stop=True)
                last.then_inc(g_ready, 1)

        @block.scalar
        def _(act):
            act.wait_ge(for_act, 1)
            nc.scalar.activation(r[:, 1, :], r[:, 0, :], ACT.Sqrt).then_inc(act_done, 1)
            for t in range(NS):
                act.wait_ge(for_act, t + 2)
                nc.scalar.activation(th[:], gate[:], ACT.Tanh, scale=0.5).then_inc(act_done, 1)

        @block.vector
        def _(dve):
            n = [0]

            def link(ins):
                n[0] += 1
                ins.then_inc(chain, 1)
                dve.wait_ge(chain, n[0])

            link(nc.vector.tensor_scalar(r[:, 0, :], K["ssq"][:], 0.25 / DI, EPS, ALU.mult, ALU.add))
            dve.sem_inc(for_act, 1)
            dve.wait_ge(act_done, 1)
            link(nc.vector.reciprocal(r[:, 2, :], r[:, 1, :]))
            link(nc.vector.tensor_tensor(r[:, 3, :], r[:, 2, :], r[:, 2, :], ALU.mult))
            link(nc.vector.tensor_tensor(r[:, 3, :], r[:, 3, :], r[:, 0, :], ALU.mult))
            link(nc.vector.tensor_scalar(r[:, 3, :], r[:, 3, :], -0.5, 1.5, ALU.mult, ALU.add))
            link(nc.vector.tensor_tensor(r[:, 2, :], r[:, 2, :], r[:, 3, :], ALU.mult))
            link(nc.vector.tensor_scalar(r[:, 2, :], r[:, 2, :], 0.25, None, ALU.mult))
            link(nc.vector.tensor_scalar(sc[:, 0:2], K["amax"][:], 1e-12, None, ALU.max))
            link(nc.vector.reciprocal(sc[:, 0:2], sc[:, 0:2]))
            link(nc.vector.tensor_scalar(sc[:, 0:2], sc[:, 0:2], FP8_MAX, None, ALU.mult))
            link(nc.vector.reciprocal(sc[:, 2:4], sc[:, 0:2]))
            link(nc.vector.tensor_tensor(sc[:, 4:5], sc[:, 2:3], sc[:, 3:4], ALU.mult))

            def quantise(dst, src, scale, m):
                link(nc.vector.tensor_scalar(v[:, 0:m], src, scale, None, ALU.mult))
                link(nc.vector.tensor_scalar(half[:, 0:m], v[:, 0:m], 0.5, None, ALU.mult, saturate=False))
                link(nc.vector.tensor_scalar(small[:, 0:m], v[:, 0:m], 24576.0, -24576.0, ALU.add, ALU.add))
                link(nc.vector.tensor_tensor(tiny[:, 0:m], v[:, 0:m], v[:, 0:m], ALU.mult))
                link(nc.vector.tensor_scalar(tiny[:, 0:m], tiny[:, 0:m], 2.0 ** -10, None, ALU.is_lt))
                link(nc.vector.scalar_tensor_tensor(out=small[:, 0:m], in0=half[:, 0:m], scalar=-2.0, in1=small[:, 0:m],
                                                    op0=ALU.mult, op1=ALU.add))
                link(nc.vector.tensor_tensor(small[:, 0:m], small[:, 0:m], tiny[:, 0:m], ALU.mult))
                nc.vector.scalar_tensor_tensor(out=dst, in0=half[:, 0:m], scalar=2.0, in1=small[:, 0:m],
                                               op0=ALU.mult, op1=ALU.add).then_inc(xq_ready, 1)

            quantise(wq[:], K["w_ffn"][:], sc[:, 1:2], P)
            dve.wait_ge(xq_ready, 1)
            for t in range(NS):
                dve.wait_ge(loaded[t % 2], 32 * (t // 2 + 1))
                if t >= 2:
                    dve.wait_ge(g_ready, t - 1)
                quantise(xq[:, t % 2, :], xn[:, t % 2, :], sc[:, 0:1], ST)
                dve.wait_ge(xq_ready, t + 2)
                dve.wait_ge(g_ready, t + 1)
                b4 = lambda a: bcast(a.unsqueeze(1), [P, CS, P])
                dve.wait_ge(act_done, t + 1)
                v4 = lambda a: a.rearrange("p (c m) -> p c m", c=CS)
                link(nc.vector.scalar_tensor_tensor(out=v4(gate[:]), in0=v4(ps[t % 2][:]), scalar=sc[:, 4:5],
                                                    in1=b4(K["d_ffnb"][:]), op0=ALU.mult, op1=ALU.add))
                dve.sem_inc(g_taken, 1)
                dve.sem_inc(for_act, 1)
                if t >= 2:
                    dve.wait_ge(stored[t % 2], 16 * (t // 2))
                link(nc.vector.tensor_tensor(v4(o[:, t % 2, :]), v4(K["s_acc"][:, t * ST:(t + 1) * ST]),
                                             bcast(r[:, 2, t * CS:(t + 1) * CS].unsqueeze(2), [P, CS, P]), ALU.mult))
                dve.wait_ge(act_done, t + 2)
                link(nc.vector.scalar_tensor_tensor(out=small[:], in0=th[:], scalar=1.0, in1=gate[:], op0=ALU.add, op1=ALU.mult))
                link(nc.vector.tensor_tensor(small[:], small[:], o[:, t % 2, :], ALU.mult))
                link(nc.vector.tensor_tensor(o[:, t % 2, :], small[:], xin[:, t % 2, :], ALU.add))
                dve.sem_inc(o_ready, 1)


def program(nc, dram, out):
    scratch = [nc.dram_tensor(n, [NS, P, ST], F32, kind="Internal").ap() for n in ("xn_t", "tc_t", "bc_t")]
    with ExitStack() as ctx:
        shapes = dict(ident=[P, P], ones=[P, P], w_zx=[P, 2 * DI], w_th=[P, 2 * H * 32], w_o=[P, DI], w_ffn=[P, P], prmT=[P, 80],
                      cols=[P, 4], goes_on=[P, NS], carry=[P, NP, HD], s_acc=[P, TOK], kk=[P, NC * H], cc=[P, NC * H],
                      dec=[P, NC * H], dtot=[P, NC * NP], ssq=[P, NC], amax=[P, 2], d_ffnb=[P, P])
        K = {n: ctx.enter_context(nc.sbuf_tensor("k_" + n, s, F32)) for n, s in shapes.items()}
        for n, s in dict(ident_bf=[P, P], zeros_bf=[P, P], mask=[P, ST], sel=[3 * H, H], sel_pair=[3 * H, NP * P], nsel=[3 * H, H], cumT=[3 * H, TOK]).items():
            K[n] = ctx.enter_context(nc.sbuf_tensor("k_" + n, s, BF16))
        prepare(nc, K, dram, scratch)
        units(nc, K, scratch)
        finish(nc, K, dram[0], scratch[0], out)


NAMES = ["u", "in_proj_w", "dt_bias", "A_log", "D", "B_norm_w", "C_norm_w", "B_bias", "C_bias", "norm_w", "out_proj_w"]


def kernel(**inputs):
    import numpy as np
    import concourse.bacc as bacc
    from concourse.bass_utils import run_bass_kernel_spmd as run

    nc = bacc.Bacc("TRN2", target_bir_lowering=False, num_devices=1)
    arrays, dram = {}, []
    for name in ["L0_attn_" + n for n in NAMES] + ["L0_ffn_weight", "L0_ffn_bias"]:
        a = np.ascontiguousarray(inputs[name])
        arrays["in_" + name] = a
        dram.append(nc.dram_tensor("in_" + name, a.shape, mybir.dt.from_np(a.dtype), kind="ExternalInput").ap())
    out = nc.dram_tensor("out", (BATCH, L, DM), F32, kind="ExternalOutput").ap()
    program(nc, dram, out)
    return run(nc, [arrays], core_ids=[0]).results[0]["out"]
```

```python
from contextlib import ExitStack

import concourse.bass as bass
from concourse import mybir

F32 = mybir.dt.float32
BF16 = mybir.dt.bfloat16
FP8 = mybir.dt.float8e4
ALU = mybir.AluOpType
ACT = mybir.ActivationFunctionType
AX = mybir.AxisListType

P = 128
H, HD, N, DM = 32, 64, 64, 128
DI = H * HD
BATCH, L = 4, 1024
TOK = BATCH * L
NC = TOK // P
CS = 4
ST = CS * P
NS = TOK // ST
NQ = H // 4
NP = H // 2
SPB = L // ST
EPS = 1e-5
PI = 3.14159274
TWO_PI = 6.283185
MAGIC = 12582912.0
MASKED = -1.0e30
FP8_MAX = 448.0


def bcast(ap, shape):
    return ap.to_broadcast(shape)


def prepare(nc, keep, dram, scratch):
    u, w_in, dt_bias, a_log, d_skip, b_norm, c_norm, b_bias, c_bias, norm_w, w_out, ffn_w, ffn_b = dram
    xn_d, tc_d, bc_d = scratch
    K = keep
    with ExitStack() as ctx:
        def sb(name, shape, dt=F32):
            return ctx.enter_context(nc.sbuf_tensor(name, shape, dt))

        def sem(name):
            return ctx.enter_context(nc.semaphore(name))

        ps = [ctx.enter_context(nc.psum_tensor(f"a_ps{i}", [P, 512], F32)) for i in range(7)]
        ps_bf = ctx.enter_context(nc.psum_tensor("a_psbf", [P, 4, P], BF16))
        big = sb("a_big", [P, NC * P])
        tmp = sb("a_tmp", [P, NC * P])
        xnT = sb("a_xnT", [P, TOK])
        tcT = sb("a_tcT", [P, TOK])
        ones = K["ones"]
        one_row = sb("a_one_row", [P, 1024])
        stage2 = sb("a_stage2", [P, 11 * P])
        prm = sb("a_prm", [P, P])
        cbn = sb("a_cbn", [H, P])
        row = sb("a_row", [1, 3 * H + P + 2 * N])
        rowb = sb("a_rowb", [P, 3 * H + P + 2 * N])
        wdl = sb("a_wdl", [P, 2 * H])
        wbc = sb("a_wbc", [P, P])
        cbT = sb("a_cbT", [P, H])
        mats = sb("a_mats", [P, 3, P])
        st32 = sb("a_st32", [P, 8, 2 * NC])
        cb1 = sb("a_cb1", [H, N])
        cbs = sb("a_cbs", [H, 1])
        cbs2 = sb("a_cbs2", [H, P])
        cbb = sb("a_cbb", [P, H])
        am = sb("a_am", [P, 2])
        am2 = sb("a_am2", [2, 2])
        s = [sb(f"a_s{i}", [P, NC * H]) for i in range(4)]
        dl = sb("a_dl", [P, NC * 2 * H])
        cum3 = sb("a_cum3", [P, NC, 3 * H], BF16)

        loaded = [sem(f"a_loaded{i}") for i in range(5)]
        consts = sem("a_consts")
        xn_done = sem("a_xn_done")
        w_t = sem("a_w_t")
        w_v = sem("a_w_v")
        w_a = sem("a_w_a")
        stored = sem("a_stored")
        dch = sem("a_dch")
        ach = sem("a_ach")
        pch = sem("a_pch")
        pe_m = sem("a_pe_m")
        v_m = sem("a_v_m")
        for_act = sem("a_for_act")
        a_m = sem("a_a_m")
        block = ctx.enter_context(nc.Block())

        zx_nat = tmp[:].rearrange("p (a m) -> p a m", a=NC)
        wo_nat = tcT[:, 0:DI]
        ident = K["ident"]

        @block.sync
        def _(sp):
            sp.dma_start(big[:].rearrange("p (c m) -> p c m", c=NC),
                         u.rearrange("b (c p) m -> p (b c) m", p=P)).then_inc(loaded[0], 16)
            sp.dma_start(zx_nat, w_in[0:2 * DI].rearrange("(a p) m -> p a m", p=P)).then_inc(loaded[1], 16)
            o = 2 * DI
            sp.dma_start(stage2[:, 0:P], w_in[o:o + P]).then_inc(loaded[2], 16)
            o += P
            sp.dma_start(stage2[0:H, 9 * P:10 * P], w_in[o:o + H]).then_inc(loaded[2], 16)
            sp.dma_start(stage2[:, P:9 * P].rearrange("p (a m) -> p a m", a=8),
                         w_in[o + H:o + H + 1024].rearrange("(a p) m -> p a m", p=P)).then_inc(loaded[2], 16)
            sp.dma_start(stage2[H:2 * H, 9 * P:10 * P], w_in[o + H + 1024:o + 2 * H + 1024]).then_inc(loaded[2], 16)
            sp.dma_start(stage2[:, 10 * P:11 * P], ffn_w).then_inc(loaded[2], 16)
            sp.dma_start(wo_nat, w_out).then_inc(loaded[3], 16)
            sp.dma_start(prm[0:16, :], norm_w.rearrange("(a p) -> a p", p=P)).then_inc(loaded[4], 16)
            for i, bias in enumerate((b_bias, c_bias)):
                r = 16 + 32 * i
                sp.dma_start(prm[r:r + 16, :], bias.rearrange("(q a) n -> q (a n)", a=2)).then_inc(loaded[4], 16)
                src = bias.rearrange("(q a) (f j) -> q a f j", a=2, f=2)
                dst = prm[r + 16:r + 32, :].rearrange("q (a f j) -> q a f j", a=2, f=2)
                for f in range(2):
                    sp.dma_start(dst[:, :, f, :], src[:, :, 1 - f, :]).then_inc(loaded[4], 16)
            sp.dma_start(cbn[:, 0:N], c_bias).then_inc(loaded[4], 16)
            sp.dma_start(cbn[:, N:2 * N], b_bias).then_inc(loaded[4], 16)
            at = 0
            for v, n in ((dt_bias, H), (a_log, H), (d_skip, H), (ffn_b, P), (b_norm, N), (c_norm, N)):
                sp.dma_start(row[0:1, at:at + n], v.rearrange("(a n) -> a n", a=1)).then_inc(loaded[4], 16)
                at += n
            sp.wait_ge(v_m, 2)
            sp.dma_start(xn_d.rearrange("s p t -> p s t"), xnT[:].rearrange("p (s t) -> p s t", s=NS)).then_inc(stored, 16)
            sp.dma_start(tc_d.rearrange("s p t -> p s t"), tcT[:].rearrange("p (s t) -> p s t", s=NS)).then_inc(stored, 16)
            sp.wait_ge(v_m, 5)
            sp.dma_start(bc_d.rearrange("s p t -> p s t"), tmp[:].rearrange("p (s t) -> p s t", s=NS)).then_inc(stored, 16)
            sp.wait_ge(stored, 48)

        @block.gpsimd
        def _(pool):
            n = [0]

            def link(ins):
                n[0] += 1
                ins.then_inc(pch, 1)
                pool.wait_ge(pch, n[0])

            link(nc.gpsimd.memset(ones[:], 1.0))
            link(nc.gpsimd.memset(one_row[:], 1.0))
            link(nc.gpsimd.memset(ident[:], 0.0))
            link(nc.gpsimd.affine_select(out=ident[:], in_=ident[:], compare_op=ALU.not_equal, fill=1.0, base=0,
                                         pattern=[[-1, P]], channel_multiplier=1))
            link(nc.gpsimd.memset(K["ident_bf"][:], 0.0))
            link(nc.gpsimd.affine_select(out=K["ident_bf"][:], in_=K["ident_bf"][:], compare_op=ALU.not_equal, fill=1.0,
                                         base=0, pattern=[[-1, P]], channel_multiplier=1))
            link(nc.gpsimd.memset(K["zeros_bf"][:], 0.0))
            link(nc.gpsimd.memset(mats[:], 0.0))
            link(nc.gpsimd.affine_select(out=mats[:, 0, :], in_=one_row[:, 0:P], compare_op=ALU.is_ge, fill=0.0, base=0,
                                         pattern=[[1, P]], channel_multiplier=-1))
            link(nc.gpsimd.affine_select(out=mats[:, 1, :], in_=mats[:, 1, :], compare_op=ALU.not_equal, fill=1.0, base=-1,
                                         pattern=[[-1, P]], channel_multiplier=1))
            link(nc.gpsimd.affine_select(out=mats[:, 2, :], in_=mats[:, 2, :], compare_op=ALU.not_equal, fill=1.0, base=P - 1,
                                         pattern=[[-1, P]], channel_multiplier=1))
            link(nc.gpsimd.memset(K["mask"][:], 0.0))
            link(nc.gpsimd.affine_select(out=K["mask"][:].rearrange("p (c t) -> p c t", c=CS),
                                         in_=K["mask"][:].rearrange("p (c t) -> p c t", c=CS), compare_op=ALU.is_ge,
                                         fill=MASKED, base=0, pattern=[[0, CS], [1, P]], channel_multiplier=-1))
            for name, v in (("sel", 1.0), ("nsel", -1.0)):
                link(nc.gpsimd.memset(K[name][:], 0.0))
                for i in range(3):
                    link(nc.gpsimd.affine_select(out=K[name][:], in_=K[name][:], compare_op=ALU.not_equal, fill=v,
                                                 base=-32 * i, pattern=[[-1, H]], channel_multiplier=1))
            link(nc.gpsimd.memset(K["cols"][:, 0:1], PI / 2))
            link(nc.gpsimd.memset(K["cols"][:, 1:2], MAGIC))
            link(nc.gpsimd.memset(K["goes_on"][:], 1.0))
            for i in range(BATCH):
                link(nc.gpsimd.memset(K["goes_on"][:, SPB * i:SPB * i + 1], 0.0))
            link(nc.gpsimd.memset(K["carry"][:], 0.0))
            nc.gpsimd.memset(am2[:], 0.0).then_inc(consts, 1)

        groups = []
        for g in range(8):
            groups.append([zx_nat[:, 4 * g + i, :] for i in range(4)])
        groups.append([stage2[:, 0:P], stage2[0:2 * H, 9 * P:10 * P], stage2[:, 10 * P:11 * P], prm[0:80, :]])
        for g in range(2):
            groups.append([stage2[:, (1 + 4 * g + i) * P:(2 + 4 * g + i) * P] for i in range(4)])
        for g in range(4):
            groups.append([wo_nat[:, (4 * g + i) * P:(4 * g + i + 1) * P] for i in range(4)])
        groups.append([cbn[:, :]])
        NG = len(groups)

        @block.tensor
        def _(pe):
            pe.wait_ge(consts, 1)
            pe.wait_ge(loaded[1], 16)
            for g, srcs in enumerate(groups):
                if g == 8:
                    pe.wait_ge(loaded[2], 80)
                    pe.wait_ge(loaded[4], 16 * 15)
                if g == 11:
                    pe.wait_ge(loaded[3], 16)
                if g >= 4:
                    pe.wait_ge(w_v if g % 2 == 0 else w_a, (g - 4) // 2 + 1)
                for i, src in enumerate(srcs):
                    r = src.shape[0]
                    last = nc.tensor.transpose(ps[g % 4][:, i * P:i * P + r], src, ident[0:r, 0:r])
                last.then_inc(w_t, 1)
            nc.tensor.matmul(ps[4][:, 0:row.shape[1]], one_row[0:1, 0:P], row[0:1, :], start=True, stop=True).then_inc(pe_m, 1)
            pe.wait_ge(xn_done, 1)
            pe.wait_ge(w_v, NG // 2)
            pe.wait_ge(w_a, NG // 2)
            for g in range(8):
                if g >= 4:
                    pe.wait_ge(w_v if g % 2 == 0 else w_a, NG // 2 + (g - 4) // 2 + 1)
                for i in range(4):
                    c = 4 * g + i
                    last = nc.tensor.transpose(ps[g % 4][:, i * P:i * P + P], big[:, c * P:c * P + P], ident[:])
                last.then_inc(w_t, 1)
            pe.wait_ge(v_m, 1)
            nc.tensor.transpose(ps[5][0:2, 0:P], am[:, 0:2], ident[:]).then_inc(pe_m, 1)
            pe.wait_ge(w_v, NG // 2 + 4)
            pe.wait_ge(w_a, NG // 2 + 4)
            for g in range(12):
                if g >= 4:
                    pe.wait_ge(w_v if g % 2 == 0 else w_a, NG // 2 + 4 + (g - 4) // 2 + 1)
                for i in range(4 if g < 8 else 8):
                    if g < 8:
                        c = 4 * g + i
                        last = nc.tensor.matmul(ps[g % 4][:, i * P:i * P + P], xnT[:, c * P:c * P + P], wbc[:],
                                                start=True, stop=True)
                    else:
                        c = 8 * (g - 8) + i
                        last = nc.tensor.matmul(ps[g % 4][:, i * 64:i * 64 + 64], xnT[:, c * P:c * P + P], wdl[:],
                                                start=True, stop=True)
                last.then_inc(w_t, 1)
            pe.wait_ge(v_m, 3)
            nc.tensor.matmul(ps[6][:, 0:2], ones[0:2, 0:P], am2[0:2, 0:2], start=True, stop=True)
            nc.tensor.matmul(ps[6][:, 64:64 + H], cbs2[:, :], ident[0:H, 0:H], start=True, stop=True).then_inc(pe_m, 1)
            pe.wait_ge(v_m, 4)
            pe.wait_ge(w_v, NG // 2 + 10)
            pe.wait_ge(w_a, NG // 2 + 10)
            for g in range(8):
                if g >= 4:
                    pe.wait_ge(w_v if g % 2 == 0 else w_a, NG // 2 + 10 + (g - 4) // 2 + 1)
                for i in range(4):
                    c = 4 * g + i
                    last = nc.tensor.transpose(ps[g % 4][:, i * P:i * P + P], big[:, c * P:c * P + P], ident[:])
                last.then_inc(w_t, 1)
            pe.wait_ge(v_m, 5)
            for c in range(NC):
                last = nc.tensor.matmul(ps[c // 16][:, (c % 16) * H:(c % 16 + 1) * H], tmp[:, c * P:c * P + P], cbT[:],
                                        start=True, stop=True)
            last.then_inc(pe_m, 1)
            pe.wait_ge(v_m, 6)
            for i in range(2):
                nc.tensor.matmul(ps[2 + i][:], mats[:, 0, :], s[2][:, 512 * i:512 * i + 512], start=True, stop=True)
                last = nc.tensor.matmul(ps[4 + i][:], ones[:, 0:P], s[2][:, 512 * i:512 * i + 512], start=True, stop=True)
            last.then_inc(pe_m, 1)
            pe.wait_ge(v_m, 7)
            for i in range(2):
                n = 512 - H * i
                nc.tensor.matmul(ps[i][:], mats[:, 1, :], s[1][:, 512 * i:512 * i + 512], start=True, stop=False)
                last = nc.tensor.matmul(ps[i][:, 0:n], mats[:, 2, :], s[1][:, 512 * i + H:512 * i + H + n], start=False, stop=True)
            last.then_inc(pe_m, 1)
            pe.wait_ge(v_m, 8)
            for g in range(8):
                if g >= 1:
                    pe.wait_ge(v_m, 8 + g)
                for i in range(4):
                    last = nc.tensor.transpose(ps_bf[0:3 * H, i, :], cum3[:, 4 * g + i, :], K["ident_bf"][:])
                last.then_inc(pe_m, 1)

        def weight_out(g, copy):
            b = ps[g % 4]
            if g < 8:
                return [copy(K["w_zx"][:, 512 * g:512 * g + 512], b[:])]
            if g == 8:
                return [copy(wbc[:], b[:, 0:P]), copy(wdl[:], b[:, P:P + 64]), copy(K["w_ffn"][:], b[:, 2 * P:3 * P]),
                        copy(K["prmT"][:, 0:80], b[:, 3 * P:3 * P + 80])]
            if g == 15:
                return [copy(cbT[:], b[:, 0:H])]
            raise AssertionError

        @block.vector
        def _(dve):
            n = [0]

            def link(ins):
                n[0] += 1
                ins.then_inc(dch, 1)
                dve.wait_ge(dch, n[0])

            def rsqrt_refined(r, v, t):
                link(nc.vector.tensor_tensor(t, r, r, ALU.mult))
                link(nc.vector.tensor_tensor(t, t, v, ALU.mult))
                link(nc.vector.tensor_scalar(t, t, -0.5, 1.5, ALU.mult, ALU.add))
                link(nc.vector.tensor_tensor(r, r, t, ALU.mult))

            big3 = big[:].rearrange("p (c m) -> p c m", c=NC)
            tmp3 = tmp[:].rearrange("p (c m) -> p c m", c=NC)
            st = [st32[:, i, 0:NC] for i in range(8)]
            dve.wait_ge(consts, 1)
            for g in range(0, NG, 2):
                dve.wait_ge(w_t, g + 1)
                b = ps[g % 4]
                if g == 10:
                    nc.vector.tensor_scalar(K["w_th"][:, 512:1024], b[:], 0.15915494309189535, None, ALU.mult).then_inc(w_v, 1)
                elif g in (12, 14):
                    a0 = 4 * (g - 11)
                    for i in range(4):
                        link(nc.vector.tensor_scalar(K["w_o"][:, (a0 + i) * P:(a0 + i + 1) * P], b[:, i * P:i * P + P],
                                                     K["prmT"][:, a0 + i:a0 + i + 1], None, ALU.mult))
                    dve.sem_inc(w_v, 1)
                else:
                    outs = weight_out(g, nc.vector.tensor_copy)
                    for o in outs[:-1]:
                        link(o)
                    outs[-1].then_inc(w_v, 1)
            dve.wait_ge(w_v, NG // 2)
            dve.wait_ge(loaded[0], 16)
            link(nc.vector.tensor_reduce(st[0], big3, AX.X, ALU.add))
            link(nc.vector.tensor_scalar(st[0], st[0], 1.0 / DM, None, ALU.mult))
            dve.wait_ge(w_a, NG // 2)
            link(nc.vector.tensor_tensor(big3, big3, bcast(st[0].unsqueeze(2), [P, NC, DM]), ALU.subtract))
            link(nc.vector.tensor_tensor(tmp3, big3, big3, ALU.mult))
            link(nc.vector.tensor_reduce(st[1], tmp3, AX.X, ALU.add))
            link(nc.vector.tensor_scalar(st[1], st[1], 1.0 / DM, EPS, ALU.mult, ALU.add))
            dve.sem_inc(for_act, 1)
            dve.wait_ge(a_m, 1)
            link(nc.vector.reciprocal(st[3], st[2]))
            rsqrt_refined(st[3], st[1], st[5])
            link(nc.vector.tensor_tensor(big3, big3, bcast(st[3].unsqueeze(2), [P, NC, DM]), ALU.mult))
            dve.sem_inc(xn_done, 1)
            link(nc.vector.tensor_reduce(am[:, 0:1], big[:], AX.X, ALU.max))
            link(nc.vector.tensor_reduce(st[6][:, 0:1], big[:], AX.X, ALU.min))
            link(nc.vector.tensor_reduce(am[:, 1:2], stage2[:, 10 * P:11 * P], AX.X, ALU.max))
            link(nc.vector.tensor_reduce(st[6][:, 1:2], stage2[:, 10 * P:11 * P], AX.X, ALU.min))
            link(nc.vector.tensor_scalar(st[6][:, 0:2], st[6][:, 0:2], -1.0, None, ALU.mult))
            nc.vector.tensor_tensor(am[:, 0:2], am[:, 0:2], st[6][:, 0:2], ALU.max).then_inc(v_m, 1)
            for g in range(0, 8, 2):
                dve.wait_ge(w_t, NG + g + 1)
                nc.vector.tensor_copy(xnT[:, 512 * g:512 * g + 512], ps[g % 4][:]).then_inc(w_v, 1)
            dve.wait_ge(w_a, NG // 2 + 4)
            dve.wait_ge(w_v, NG // 2 + 4)
            for b in range(BATCH):
                link(nc.vector.tensor_tensor_scan(tcT[:, b * L:(b + 1) * L], one_row[:], xnT[:, b * L:(b + 1) * L],
                                                  0.0, ALU.mult, ALU.add))
            dve.sem_inc(v_m, 1)
            link(nc.vector.tensor_copy(K["sel_pair"][:].rearrange("k (h d) -> k h d", d=64),
                                       bcast(K["sel"][:].unsqueeze(2), [3 * H, H, 64])))
            dve.wait_ge(pe_m, 1)
            link(nc.vector.tensor_copy(rowb[:], ps[4][:, 0:row.shape[1]]))
            link(nc.vector.tensor_copy(K["d_ffnb"][:], rowb[:, 3 * H:3 * H + P]))
            dve.wait_ge(pe_m, 2)
            link(nc.vector.tensor_reduce(st[6][0:2, 2:3], ps[5][0:2, 0:P], AX.X, ALU.max))
            link(nc.vector.tensor_scalar(am2[0:2, 0:2], ident[0:2, 0:2], st[6][0:2, 2:3], None, ALU.mult))
            link(nc.vector.tensor_tensor(cb1[:], cbn[:, 0:N], cbn[:, N:2 * N], ALU.mult))
            link(nc.vector.tensor_reduce(cbs[:], cb1[:], AX.X, ALU.add))
            nc.vector.tensor_copy(cbs2[:], bcast(cbs[:], [H, P])).then_inc(v_m, 1)
            dlv = dl[:].rearrange("p (c k) -> p c k", k=64)
            for g in range(0, 12, 2):
                dve.wait_ge(w_t, NG + 8 + g + 1)
                if g < 8:
                    nc.vector.tensor_copy(big[:, 512 * g:512 * g + 512], ps[g % 4][:]).then_inc(w_v, 1)
                else:
                    nc.vector.tensor_copy(dl[:, 512 * (g - 8):512 * (g - 7)], ps[g % 4][:]).then_inc(w_v, 1)
            dve.wait_ge(pe_m, 3)
            link(nc.vector.tensor_copy(K["amax"][:], ps[6][:, 0:2]))
            link(nc.vector.tensor_copy(cbb[:], ps[6][:, 64:64 + H]))
            dve.wait_ge(w_a, NG // 2 + 10)
            dve.wait_ge(w_v, NG // 2 + 10)
            big64 = big[:].rearrange("p (g n) -> p g n", n=N)
            tmp64 = tmp[:].rearrange("p (g n) -> p g n", n=N)
            v64, r64, t64 = st32[:, 1, :], st32[:, 3, :], st32[:, 5, :]
            link(nc.vector.tensor_tensor(tmp[:], big[:], big[:], ALU.mult))
            link(nc.vector.tensor_reduce(v64, tmp64, AX.X, ALU.add))
            link(nc.vector.tensor_scalar(v64, v64, 1.0 / N, EPS, ALU.mult, ALU.add))
            dve.sem_inc(for_act, 1)
            dve.wait_ge(a_m, 2)
            link(nc.vector.reciprocal(r64, st32[:, 2, :]))
            rsqrt_refined(r64, v64, t64)
            link(nc.vector.tensor_tensor(big64, big64, bcast(r64.unsqueeze(2), [P, 2 * NC, N]), ALU.mult))
            wn = rowb[:, 3 * H + P:3 * H + 2 * P].unsqueeze(1)
            link(nc.vector.tensor_tensor(big3, big3, bcast(wn, [P, NC, P]), ALU.mult))
            pr = tcT[:, 0:NC * N].rearrange("p (c n) -> p c n", n=N)
            dve.wait_ge(stored, 32)
            link(nc.vector.tensor_tensor(pr, big3[:, :, 0:N], big3[:, :, N:2 * N], ALU.mult))
            link(nc.vector.tensor_reduce(st[0], pr, AX.X, ALU.add))
            dve.sem_inc(v_m, 1)
            for g in range(0, 8, 2):
                dve.wait_ge(w_t, NG + 20 + g + 1)
                nc.vector.tensor_copy(tmp[:, 512 * g:512 * g + 512], ps[g % 4][:]).then_inc(w_v, 1)
            dve.wait_ge(w_a, NG // 2 + 14)
            dve.wait_ge(w_v, NG // 2 + 14)
            dve.sem_inc(v_m, 1)
            v3 = [x[:].rearrange("p (c h) -> p c h", h=H) for x in s]
            one_h = lambda a: bcast(rowb[:, a * H:(a + 1) * H].unsqueeze(1), [P, NC, H])
            link(nc.vector.tensor_tensor(v3[0], dlv[:, :, 0:H], one_h(0), ALU.add))
            link(nc.vector.tensor_scalar(s[1][:], s[0][:], -1.0, None, ALU.mult))
            link(nc.vector.tensor_tensor(s[1][:], s[1][:], s[0][:], ALU.min))
            nc.vector.tensor_copy(v3[3], dlv[:, :, H:2 * H]).then_inc(for_act, 1)
            dve.wait_ge(a_m, 3)
            link(nc.vector.tensor_scalar(s[2][:], s[1][:], 1.0, None, ALU.add))
            nc.vector.tensor_copy(K["kk"][:], s[2][:]).then_inc(for_act, 1)
            link(nc.vector.tensor_scalar(K["dec"][:], s[2][:], -1.0, None, ALU.add))
            link(nc.vector.tensor_tensor(s[1][:], s[1][:], K["dec"][:], ALU.subtract))
            link(nc.vector.reciprocal(K["dec"][:], s[2][:]))
            link(nc.vector.tensor_tensor(s[1][:], s[1][:], K["dec"][:], ALU.mult))
            link(nc.vector.tensor_scalar(s[0][:], s[0][:], 0.0, None, ALU.max))
            link(nc.vector.tensor_tensor(s[0][:], s[0][:], s[1][:], ALU.add))
            dve.wait_ge(a_m, 4)
            link(nc.vector.tensor_tensor(s[0][:], s[0][:], K["kk"][:], ALU.add))
            link(nc.vector.tensor_scalar(s[3][:], s[3][:], 1.0, None, ALU.add))
            link(nc.vector.reciprocal(s[3][:], s[3][:]))
            link(nc.vector.tensor_tensor(K["kk"][:], s[3][:], s[0][:], ALU.mult))
            link(nc.vector.tensor_scalar(s[1][:], s[3][:], -1.0, 1.0, ALU.mult, ALU.add))
            link(nc.vector.tensor_tensor(s[1][:], s[1][:], s[0][:], ALU.mult))
            link(nc.vector.tensor_scalar(s[0][:], s[0][:], -1.0, None, ALU.mult))
            link(nc.vector.tensor_tensor(v3[2], v3[0], one_h(1), ALU.mult))
            dve.sem_inc(v_m, 1)
            dve.wait_ge(pe_m, 4)
            for i in range(2):
                o = v3[3][:, 16 * i:16 * i + 16, :]
                link(nc.vector.tensor_tensor(o, ps[i][:].rearrange("p (c h) -> p c h", h=H),
                                             bcast(st[0][:, 16 * i:16 * i + 16].unsqueeze(2), [P, 16, H]), ALU.add))
            link(nc.vector.tensor_tensor(v3[3], v3[3], bcast(cbb[:].unsqueeze(1), [P, NC, H]), ALU.add))
            dve.sem_inc(v_m, 1)
            dve.wait_ge(pe_m, 5)
            for i in range(2):
                a, b = 512 * i, 512 * i + 512
                link(nc.vector.tensor_copy(s[0][:, a:b], ps[2 + i][:]))
                link(nc.vector.tensor_tensor(K["dec"][:, a:b], ps[4 + i][:], s[0][:, a:b], ALU.subtract))
            dt3 = K["dtot"][:].rearrange("p (c r) -> p c r", r=NP)
            for i in range(2):
                for j in range(2):
                    q = slice(64 * j, 64 * j + 64)
                    link(nc.vector.tensor_copy(dt3[q, 16 * i:16 * i + 16, :],
                                               ps[4 + i][q, :].rearrange("p (c r j) -> p c r j", r=NP, j=2)[:, :, :, j]))
            c0 = s[0][:].rearrange("p (c h) -> p c h", h=H)
            for i in range(3):
                part = cum3[:, :, H * i:H * i + H]
                link(nc.vector.tensor_copy(part, c0))
                if i < 2:
                    link(nc.vector.tensor_tensor(c0, c0, part, ALU.subtract))
            dve.sem_inc(v_m, 1)
            dve.wait_ge(pe_m, 6)
            for i in range(2):
                a, b = 512 * i, 512 * i + 512
                link(nc.vector.tensor_tensor(K["kk"][:, a:b], K["kk"][:, a:b], ps[i][:], ALU.add))
                link(nc.vector.tensor_tensor(s[3][:, a:b], s[3][:, a:b], ps[i][:], ALU.mult))
            cc3 = K["cc"][:].rearrange("p (c h) -> p c h", h=H)
            link(nc.vector.tensor_scalar(s[3][:], s[3][:], -1.0, None, ALU.mult))
            link(nc.vector.tensor_tensor(cc3, v3[3], one_h(2), ALU.add))
            for g in range(8):
                dve.wait_ge(pe_m, 7 + g)
                nc.vector.tensor_copy(K["cumT"][:, 512 * g:512 * g + 512],
                                      ps_bf[0:3 * H].rearrange("p c t -> p (c t)")).then_inc(v_m, 1)


        @block.scalar
        def _(act):
            n = [0]

            def link(ins):
                n[0] += 1
                ins.then_inc(ach, 1)
                act.wait_ge(ach, n[0])

            act.wait_ge(consts, 1)
            for g in range(1, NG, 2):
                act.wait_ge(w_t, g + 1)
                b = ps[g % 4]
                if g == 9:
                    nc.scalar.mul(K["w_th"][:, 0:512], b[:], 0.15915494309189535).then_inc(w_a, 1)
                elif g in (11, 13):
                    act.wait_ge(w_v, 5)
                    a0 = 4 * (g - 11)
                    for i in range(4):
                        link(nc.scalar.activation(K["w_o"][:, (a0 + i) * P:(a0 + i + 1) * P], b[:, i * P:i * P + P],
                                                  ACT.Copy, scale=K["prmT"][:, a0 + i:a0 + i + 1]))
                    act.sem_inc(w_a, 1)
                else:
                    weight_out(g, nc.scalar.copy)[0].then_inc(w_a, 1)
            act.wait_ge(for_act, 1)
            nc.scalar.activation(st32[:, 2, 0:NC], st32[:, 1, 0:NC], ACT.Sqrt).then_inc(a_m, 1)
            for g in range(1, 8, 2):
                act.wait_ge(w_t, NG + g + 1)
                nc.scalar.copy(xnT[:, 512 * g:512 * g + 512], ps[g % 4][:]).then_inc(w_a, 1)
            for g in range(1, 12, 2):
                act.wait_ge(w_t, NG + 8 + g + 1)
                dst = big[:, 512 * g:512 * g + 512] if g < 8 else dl[:, 512 * (g - 8):512 * (g - 7)]
                nc.scalar.copy(dst, ps[g % 4][:]).then_inc(w_a, 1)
            act.wait_ge(for_act, 2)
            nc.scalar.activation(st32[:, 2, :], st32[:, 1, :], ACT.Sqrt).then_inc(a_m, 1)
            for g in range(1, 8, 2):
                act.wait_ge(w_t, NG + 20 + g + 1)
                nc.scalar.copy(tmp[:, 512 * g:512 * g + 512], ps[g % 4][:]).then_inc(w_a, 1)
            act.wait_ge(for_act, 3)
            link(nc.scalar.activation(rowb[:, H:2 * H], rowb[:, H:2 * H], ACT.Exp))
            link(nc.scalar.activation(s[3][:], s[3][:], ACT.Exp, scale=-1.0))
            nc.scalar.activation(s[1][:], s[1][:], ACT.Exp).then_inc(a_m, 1)
            act.wait_ge(for_act, 4)
            nc.scalar.activation(K["kk"][:], K["kk"][:], ACT.Ln).then_inc(a_m, 1)
            act.wait_ge(v_m, 8)
            link(nc.scalar.activation(K["dec"][:], K["dec"][:], ACT.Exp))
            link(nc.scalar.activation(K["dtot"][:], K["dtot"][:], ACT.Exp))


def units(nc, K, scratch):
    xn_d, tc_d, bc_d = scratch
    with ExitStack() as ctx:
        def sb(name, shape, dt=F32):
            return ctx.enter_context(nc.sbuf_tensor(name, shape, dt))

        def sem(name):
            return ctx.enter_context(nc.semaphore(name))

        def bank(name):
            return ctx.enter_context(nc.psum_tensor(name, [P, 512], F32))

        R = [bank("r0"), bank("r1")]
        Dp = bank("d")
        Op = bank("o")
        Sp = [bank("s0"), bank("s1")]
        Yp = [bank("y0"), bank("y1")]

        BC_LOADS = 16 * 6
        DUP = 16 * 4
        xnz = sb("xnz", [P, ST])
        xns = sb("xns", [P, ST])
        tcs = sb("tcs", [P, ST])
        bcs = sb("bcs", [P, 4, ST])
        rnd = sb("rnd", [P, ST])
        ang = sb("ang", [P, ST])
        tri = sb("tri", [P, 3, ST])
        trig = sb("trig", [P, 2, 2, ST])
        part = sb("part", [P, 4, ST])
        rot = sb("rot", [P, 2, 2, 2, ST])
        eb = sb("eb", [P, 2, ST])
        ce = sb("ce", [P, 2, ST])
        xk = sb("xk", [P, 2, CS, 4 * HD])
        xc = sb("xc", [P, 2, CS, 4 * HD])
        E = sb("E", [P, 2, ST])
        M = sb("M", [P, 4, ST])
        bw = sb("bw", [P, 2, CS, P])
        hs = sb("hs", [P, CS, 2, HD])
        th = sb("th", [P, 2, ST])
        yT = sb("yT", [P, 2, ST])
        sq = sb("sq", [P, 2, ST])
        sqa = sb("sqa", [P, ST])

        tc_loaded, xn_loaded, bc_loaded, z_loaded = sem("tc_loaded"), sem("xn_loaded"), sem("bc_loaded"), sem("z_loaded")
        dup = [sem("dup0"), sem("dup1")]
        u_ready, bt_ready, x_ready, eb_ready = sem("u_ready"), sem("bt_ready"), sem("x_ready"), sem("eb_ready")
        st_ready, z_ready, out_ready, ssq_ready = sem("st_ready"), sem("z_ready"), sem("out_ready"), sem("ssq_ready")
        d_ready, s_ready, y_ready = sem("d_ready"), sem("s_ready"), sem("y_ready")
        e_ready, m_ready = sem("e_ready"), sem("m_ready")
        rounded, turned, absd = sem("rounded"), sem("turned"), sem("absd")
        sin_ready = sem("sin_ready")
        part_ready, rot_ready = sem("part_ready"), sem("rot_ready")
        ebs_ready, ce_ready = sem("ebs_ready"), sem("ce_ready")
        xk_ready, bw_ready = sem("xk_ready"), sem("bw_ready")
        th_ready, sz_ready, yt_ready, sq_ready = sem("th_ready"), sem("sz_ready"), sem("yt_ready"), sem("sq_ready")
        sqa_ready = sem("sqa_ready")
        hch = sem("hch")
        acc_done, ssq_taken = sem("acc_done"), sem("ssq_taken")
        block = ctx.enter_context(nc.Block())

        def at(per, t, k):
            return t * per + max(k, 0) + 1

        T1, T2, T3, T4, T8 = NQ, 2 * NQ, 3 * NQ, 4 * NQ, 8 * NQ

        @block.sync
        def _(sp):
            def load_bc(t):
                src = bc_d[t].rearrange("(i n) t -> n i t", i=2)
                for j in range(2):
                    sp.dma_start(bcs[64 * j:64 * j + 64, 0:4:2, :], src).then_inc(bc_loaded, 16)
                    for f in range(2):
                        r = 64 * j + 32 * f
                        sp.dma_start(bcs[r:r + 32, 1:4:2, :], src[32 * (1 - f):32 * (2 - f)]).then_inc(bc_loaded, 16)

            def spread(t, q):
                sp.wait_ge(sin_ready, at(T3, t, 3 * q + 3))
                for p in range(2):
                    for j in range(2):
                        h = 2 * p + j
                        for d in range(2):
                            r = 64 * j + 32 * d
                            sp.dma_start(trig[r:r + 32, p, :, :],
                                         tri[32 * h:32 * h + 32, d:3:2 - d, :]).then_inc(dup[p], 16)

            sp.dma_start(tcs[:], tc_d[0]).then_inc(tc_loaded, 16)
            sp.dma_start(xns[:], xn_d[0]).then_inc(xn_loaded, 16)
            load_bc(0)
            sp.dma_start(xnz[:], xn_d[0]).then_inc(z_loaded, 16)
            spread(0, 0)
            spread(0, 1)
            with sp.Fori(0, NS) as t:
                tn = (t + 1) % NS
                for q in range(NQ):
                    if q == NQ - 3:
                        sp.wait_ge(u_ready, at(T1, t, T1))
                        sp.dma_start(tcs[:], tc_d[tn]).then_inc(tc_loaded, 16)
                    if q == NQ - 2:
                        sp.wait_ge(x_ready, at(T2, t, T2))
                        sp.dma_start(xns[:], xn_d[tn]).then_inc(xn_loaded, 16)
                        sp.wait_ge(part_ready, at(T8, t, T8))
                        load_bc(tn)
                    spread(t, q + 2)
                sp.wait_ge(z_ready, at(T2, t, T2))
                sp.dma_start(xnz[:], xn_d[tn]).then_inc(z_loaded, 16)
            sp.wait_ge(tc_loaded, 16 * (NS + 1))
            sp.wait_ge(xn_loaded, 16 * (NS + 1))
            sp.wait_ge(bc_loaded, BC_LOADS * (NS + 1))
            sp.wait_ge(z_loaded, 16 * (NS + 1))
            for p in range(2):
                sp.wait_ge(dup[p], DUP * (NS * NQ + 2))


        @block.tensor
        def _(pe):
            for s in (u_ready, bt_ready, x_ready, eb_ready, st_ready, z_ready, out_ready, ssq_ready, d_ready, s_ready, y_ready):
                pe.sem_inc(s, 1)

            def angles(q):
                w = K["w_th"][:, (q % NQ) * P:(q % NQ + 1) * P]
                nc.tensor.matmul(R[0][:], w, tcs[:], start=True, stop=True).then_inc(u_ready, 1)

            def x_by_token(q, i):
                for c in range(2):
                    last = nc.tensor.matmul(R[i][:, 256 * c:256 * c + 256], xns[:, (2 * i + c) * P:(2 * i + c + 1) * P],
                                            K["w_zx"][:, DI + q * 256:DI + q * 256 + 256], start=True, stop=True)
                last.then_inc(x_ready, 1)

            def b_by_token(q, p):
                for c in range(CS):
                    last = nc.tensor.transpose(R[p][:, c * P:c * P + P], rot[:, q % 2, p, 0, c * P:c * P + P], K["ident"][:])
                last.then_inc(bt_ready, 1)

            def exponents(t, q, tt, h):
                pe.wait_ge(ebs_ready, at(T2, t, 2 * q))
                pe.wait_ge(e_ready, at(T4, t, 4 * q + h))
                head = 4 * (q % NQ) + h
                nc.tensor.matmul(Dp[:], K["ident_bf"][:], K["mask"][:], start=True, stop=False, skip_group_check=True)
                nc.tensor.matmul(Dp[:], bcast(K["sel"][:, head:head + 1], [3 * H, P]), K["cumT"][:, bass.ds(tt * ST, ST)],
                                 start=False, stop=False, skip_group_check=True)
                for c in range(CS):
                    last = nc.tensor.matmul(Dp[:, c * P:c * P + P], K["cumT"][:, bass.ds(tt * ST + c * P, P)],
                                            bcast(K["nsel"][:, head:head + 1], [3 * H, P]), start=False,
                                            stop=c == CS - 1, skip_group_check=True)
                last.then_inc(d_ready, 1)

            def row_exponents(t, q, p):
                pe.wait_ge(e_ready, at(T4, t, 4 * q + 4))
                pe.wait_ge(ebs_ready, at(T2, t, 2 * q + p))
                nc.tensor.matmul(Dp[:], K["sel_pair"][:, (2 * q + p) * P:(2 * q + p + 1) * P],
                                 K["cumT"][:, bass.ds(t * ST, ST)], start=True, stop=True).then_inc(eb_ready, 1)

            def scores(t, q, h):
                p, rows = h // 2, slice(64 * (h % 2), 64 * (h % 2) + 64)
                pe.wait_ge(m_ready, at(T4, t, 4 * q + h - 1))
                for c in range(CS):
                    k = slice(c * P, c * P + P)
                    last = nc.tensor.matmul(Sp[h % 2][:, k], rot[rows, q % 2, p, 0, k], rot[rows, q % 2, p, 1, k],
                                            start=True, stop=True)
                last.then_inc(s_ready, 1)

            def project(t, q, chunks):
                if q == 0 and chunks[0] == 0:
                    pe.wait_ge(acc_done, at(1, t, 0))
                    nc.tensor.matmul(Op[:], K["zeros_bf"][:], K["mask"][:], start=True, stop=False, skip_group_check=True)
                pe.wait_ge(yt_ready, at(T2, t, 2 * q + 2))
                for c in chunks:
                    k = slice(c * P, c * P + P)
                    for p in range(2):
                        last = nc.tensor.matmul(Op[:, k], yT[:, p, k], K["w_o"][:, (2 * q + p) * P:(2 * q + p + 1) * P],
                                                start=False, stop=q == NQ - 1 and c == CS - 1 and p == 1,
                                                skip_group_check=True)
                if chunks[-1] == CS - 1:
                    last.then_inc(out_ready, 1)

            pe.wait_ge(tc_loaded, 16)
            angles(0)
            pe.wait_ge(turned, at(T1, 0, 1))
            angles(1)
            pe.wait_ge(xn_loaded, 16)
            pe.wait_ge(turned, at(T1, 0, 2))
            for i in range(2):
                x_by_token(0, i)
            pe.wait_ge(rot_ready, at(T4, 0, 4))
            for p in range(2):
                pe.wait_ge(xk_ready, at(T2, 0, p + 1))
                b_by_token(0, p)
            for h in range(2):
                exponents(0, 0, 0, h)
                scores(0, 0, h)
            with pe.Fori(0, NS) as t:
                for q in range(NQ):
                    par = q % 2
                    tn = t if q < NQ - 1 else (t + 1) % NS
                    if q == NQ - 2:
                        pe.wait_ge(tc_loaded, (t + 2) * 16)
                    pe.wait_ge(bw_ready, at(T2, t, 2 * q + 1))
                    angles(q + 2)
                    if q == 0:
                        pe.wait_ge(ssq_taken, at(1, t, 0))
                    exponents(t, q, t, 2)
                    scores(t, q, 2)
                    pe.wait_ge(bw_ready, at(T2, t, 2 * q + 2))
                    for c in range(CS):
                        for p in range(2):
                            for j in range(2):
                                last = nc.tensor.matmul(R[1][64 * j:64 * j + 64, (2 * c + p) * 64:(2 * c + p) * 64 + 64],
                                                        bw[:, p, c, 64 * j:64 * j + 64],
                                                        xk[:, par, c, (2 * p + j) * 64:(2 * p + j) * 64 + 64],
                                                        start=True, stop=True)
                    last.then_inc(st_ready, 1)
                    exponents(t, q, t, 3)
                    scores(t, q, 3)
                    row_exponents(t, q, 0)
                    if q == NQ - 1:
                        pe.wait_ge(xn_loaded, (t + 2) * 16)
                    pe.wait_ge(turned, at(T1, t, q + 3))
                    x_by_token((q + 1) % NQ, 0)
                    row_exponents(t, q, 1)
                    if q > 0:
                        project(t, q - 1, (0, 1))
                    pe.wait_ge(hch, at(9 * NQ, t, 9 * q + 9))
                    x_by_token((q + 1) % NQ, 1)
                    if q > 0:
                        project(t, q - 1, (2, 3))
                    if q == 0:
                        pe.wait_ge(z_loaded, (t + 1) * 16)
                    for p in range(2):
                        pe.wait_ge(xk_ready, at(T2, t, 2 * q + 2 + p + 1))
                        w = K["w_zx"][:, (2 * q + p) * P:(2 * q + p + 1) * P]
                        nc.tensor.matmul(R[p][:], w, xnz[:], start=True, stop=True).then_inc(z_ready, 1)
                    for p in range(2):
                        pe.wait_ge(m_ready, at(T4, t, 4 * q + 2 * p + 2))
                        pe.wait_ge(ce_ready, at(T2, t, 2 * q + p + 1))
                        pe.wait_ge(yt_ready, at(T2, t, 2 * q - 1 + p))
                        for c in range(CS):
                            k = slice(c * P, c * P + P)
                            nc.tensor.matmul(Yp[p][:, k], xc[:, par, c, 128 * p:128 * p + 128], K["ident"][:],
                                             start=True, stop=False, is_transpose=True, skip_group_check=True)
                            for j in range(2):
                                nc.tensor.matmul(Yp[p][64 * j:64 * j + 64, k],
                                                 xk[:, par, c, (2 * p + j) * 64:(2 * p + j) * 64 + 64], M[:, 2 * p + j, k],
                                                 start=False, stop=False, skip_group_check=True)
                            for j in range(2):
                                rows = slice(64 * j, 64 * j + 64)
                                last = nc.tensor.matmul(Yp[p][rows, k], hs[rows, c, p, :], ce[rows, p, k],
                                                        start=False, stop=True, skip_group_check=True)
                        last.then_inc(y_ready, 1)
                    pe.wait_ge(rot_ready, at(T4, t, 4 * q + 8))
                    for p in range(2):
                        pe.wait_ge(sz_ready, at(T2, t, 2 * q + p + 1))
                        b_by_token(q + 1, p)
                    for h in range(2):
                        exponents(t, q + 1, tn, h)
                        scores(t, q + 1, h)
                project(t, NQ - 1, range(CS))
                pe.wait_ge(sqa_ready, at(T2, t, T2))
                pe.wait_ge(e_ready, at(T4, t, T4 + 2))
                for c in range(CS):
                    last = nc.tensor.matmul(Dp[:, c:c + 1], sqa[:, c * P:c * P + P], K["ones"][:, 0:1],
                                            start=True, stop=True)
                last.then_inc(ssq_ready, 1)

        @block.vector
        def _(dve):
            for s in (turned, bw_ready, m_ready, xk_ready, hch, part_ready, sz_ready, yt_ready, acc_done, ssq_taken):
                dve.sem_inc(s, 1)

            def angles(t, q):
                dve.wait_ge(rounded, at(T1, t, q + 1))
                dve.wait_ge(sin_ready, at(T3, t, 3 * q))
                nc.vector.scalar_tensor_tensor(out=ang[:], in0=rnd[:], scalar=MAGIC, in1=R[0][:],
                                               op0=ALU.subtract, op1=ALU.subtract).then_inc(turned, 1)

            def x_scaled(t, q, tt, i):
                dve.wait_ge(x_ready, at(T2, t, 2 * q + i + 1))
                dve.wait_ge(y_ready, at(T2, t, 2 * q - 2))
                for dst, f in ((xk, "kk"), (xc, "cc")):
                    v = K[f][:, bass.ds(tt * (CS * H) + 2 * i * H, 2 * H)].rearrange("p (c h) -> p c h", h=H)
                    v = v[:, :, 4 * (q % NQ):4 * (q % NQ) + 4].unsqueeze(3)
                    last = nc.vector.tensor_tensor(dst[:, q % 2, 2 * i:2 * i + 2, :].rearrange("p c (h d) -> p c h d", h=4),
                                                   R[i][:].rearrange("p (c h d) -> p c h d", c=2, h=4),
                                                   bcast(v, [P, 2, 4, HD]), ALU.mult)
                last.then_inc(xk_ready, 1)

            def rotation(t, q, p, w, f):
                pair = (q % NQ) * 2 + p
                col = K["prmT"][:, 16 * (1 + 2 * w + f) + pair:16 * (1 + 2 * w + f) + pair + 1]
                if w == 0 and f == 0:
                    dve.wait_ge(dup[p], t * (DUP * NQ) + DUP * (q + 1))
                    if q % NQ == 0 and p == 0:
                        dve.wait_ge(bc_loaded, (t + (q // NQ + 1)) * BC_LOADS)
                if f == 0:
                    dve.wait_ge(rot_ready, at(T4, t, 4 * q + 2 * p + w - 1))
                nc.vector.scalar_tensor_tensor(out=part[:, 2 * w + f, :], in0=bcs[:, 2 * w + f, :], scalar=col,
                                               in1=trig[:, p, 1 - f, :], op0=ALU.add, op1=ALU.mult).then_inc(part_ready, 1)

            def b_decayed(t, q, tt):
                dve.wait_ge(st_ready, at(T1, t, q))
                for p in range(2):
                    dve.wait_ge(bt_ready, at(T2, t, 2 * q + p + 1))
                    v = K["dec"][:, bass.ds(tt * (CS * H), CS * H)].rearrange("p (c h) -> p c h", h=H)
                    v = v[:, :, 4 * (q % NQ) + 2 * p:4 * (q % NQ) + 2 * p + 2].unsqueeze(3)
                    nc.vector.tensor_tensor(bw[:, p, :, :].rearrange("p c (j n) -> p c j n", j=2),
                                            R[p][:].rearrange("p (c j n) -> p c j n", c=CS, j=2),
                                            bcast(v, [P, CS, 2, N]), ALU.mult).then_inc(bw_ready, 1)

            def scores(t, q, h):
                dve.wait_ge(e_ready, at(T4, t, 4 * q + h + 1))
                dve.wait_ge(s_ready, at(T4, t, 4 * q + h + 1))
                dve.wait_ge(y_ready, at(T2, t, 2 * q - 1 + h // 2))
                nc.vector.tensor_tensor(M[:, h, :], Sp[h % 2][:], E[:, h % 2, :], ALU.mult).then_inc(m_ready, 1)

            angles(0, 0)
            angles(0, 1)
            x_scaled(0, 0, 0, 0)
            x_scaled(0, 0, 0, 1)
            for p in range(2):
                for w in range(2):
                    for f in range(2):
                        rotation(0, 0, p, w, f)
            b_decayed(0, 0, 0)
            scores(0, 0, 0)
            scores(0, 0, 1)
            with dve.Fori(0, NS) as t:
                def state(q, c):
                    dve.wait_ge(hch, at(9 * NQ, t, 9 * q + 1 + 2 * c))
                    for p in range(2):
                        dst = hs[:, c + 1, p, :] if c < CS - 1 else K["carry"][:, 2 * q + p, :]
                        nc.vector.scalar_tensor_tensor(
                            out=dst, in0=hs[:, c, p, :], scalar=K["dtot"][:, bass.ds(t * (CS * NP) + c * NP + 2 * q + p, 1)],
                            in1=R[1][:, (2 * c + p) * 64:(2 * c + p) * 64 + 64], op0=ALU.mult, op1=ALU.add).then_inc(hch, 1)

                for q in range(NQ):
                    tn = t if q < NQ - 1 else (t + 1) % NS
                    dve.wait_ge(y_ready, at(T2, t, 2 * q))
                    dve.wait_ge(hch, at(9 * NQ, t, 9 * q))
                    nc.vector.tensor_scalar(hs[:, 0, :, :], K["carry"][:, 2 * q:2 * q + 2, :], K["goes_on"][:, bass.ds(t, 1)],
                                            None, ALU.mult).then_inc(hch, 1)
                    rotation(t, q + 1, 0, 0, 0)
                    rotation(t, q + 1, 0, 0, 1)
                    angles(t, q + 2)
                    scores(t, q, 2)
                    rotation(t, q + 1, 0, 1, 0)
                    dve.wait_ge(st_ready, at(T1, t, q + 1))
                    state(q, 0)
                    rotation(t, q + 1, 0, 1, 1)
                    state(q, 1)
                    rotation(t, q + 1, 1, 0, 0)
                    state(q, 2)
                    state(q, 3)
                    x_scaled(t, q + 1, tn, 0)
                    x_scaled(t, q + 1, tn, 1)
                    scores(t, q, 3)
                    rotation(t, q + 1, 1, 0, 1)
                    rotation(t, q + 1, 1, 1, 0)
                    rotation(t, q + 1, 1, 1, 1)
                    for p in range(2):
                        dve.wait_ge(th_ready, at(T2, t, 2 * q + p + 1))
                        nc.vector.scalar_tensor_tensor(out=th[:, p, :], in0=th[:, p, :], scalar=1.0, in1=R[p][:],
                                                       op0=ALU.add, op1=ALU.mult).then_inc(sz_ready, 1)
                    for p in range(2):
                        dve.wait_ge(sz_ready, at(T2, t, 2 * q + p + 1))
                        dve.wait_ge(y_ready, at(T2, t, 2 * q + p + 1))
                        dve.wait_ge(out_ready, at(T1, t, q))
                        dve.wait_ge(sq_ready, at(T2, t, 2 * q))
                        nc.vector.tensor_tensor(yT[:, p, :], Yp[p][:], th[:, p, :], ALU.mult).then_inc(yt_ready, 1)
                    b_decayed(t, q + 1, tn)
                    scores(t, q + 1, 0)
                    scores(t, q + 1, 1)
                dve.wait_ge(ssq_ready, at(1, t, 1))
                nc.vector.tensor_copy(K["ssq"][:, bass.ds(t * CS, CS)], Dp[:, 0:CS]).then_inc(ssq_taken, 1)
                dve.wait_ge(out_ready, at(T1, t, T1))
                nc.vector.tensor_copy(K["s_acc"][:, bass.ds(t * ST, ST)], Op[:]).then_inc(acc_done, 1)

        @block.scalar
        def _(act):
            for s in (rounded, sin_ready, absd, e_ready, ebs_ready, th_ready, sq_ready):
                act.sem_inc(s, 1)

            def rounding(t, q):
                act.wait_ge(u_ready, at(T1, t, q + 1))
                act.wait_ge(sin_ready, at(T3, t, 3 * q))
                nc.scalar.activation(rnd[:], R[0][:], ACT.Identity, bias=K["cols"][:, 1:2]).then_inc(rounded, 1)

            def sines(t, q, first=False):
                act.wait_ge(turned, at(T1, t, q + 1))
                nc.scalar.activation(rnd[:], ang[:], ACT.Abs).then_inc(absd, 1)
                if not first:
                    for p in range(2):
                        act.wait_ge(dup[p], t * (DUP * NQ) + DUP * q)
                nc.scalar.activation(tri[:, 0, :], ang[:], ACT.Sin, scale=TWO_PI).then_inc(sin_ready, 1)
                nc.scalar.activation(tri[:, 1, :], ang[:], ACT.Sin, scale=-TWO_PI).then_inc(sin_ready, 1)
                act.wait_ge(absd, at(T1, t, q + 1))
                act.wait_ge(part_ready, at(T8, t, 8 * q))
                nc.scalar.activation(tri[:, 2, :], rnd[:], ACT.Sin, scale=-TWO_PI, bias=K["cols"][:, 0:1]).then_inc(sin_ready, 1)

            def decays(t, q, h):
                act.wait_ge(d_ready, at(T4, t, 4 * q + h + 1))
                act.wait_ge(m_ready, at(T4, t, 4 * q + h - 1))
                nc.scalar.activation(E[:, h % 2, :], Dp[:], ACT.Exp).then_inc(e_ready, 1)

            def squares(t, q, p):
                act.wait_ge(yt_ready, at(T2, t, 2 * q + p + 1))
                act.wait_ge(sqa_ready, at(T2, t, 2 * q - 1 + p))
                nc.scalar.activation(sq[:, p, :], yT[:, p, :], ACT.Square).then_inc(sq_ready, 1)

            rounding(0, 0)
            sines(0, 0, first=True)
            rounding(0, 1)
            sines(0, 1)
            decays(0, 0, 0)
            decays(0, 0, 1)
            with act.Fori(0, NS) as t:
                for q in range(NQ):
                    rounding(t, q + 2)
                    decays(t, q, 2)
                    decays(t, q, 3)
                    for p in range(2):
                        act.wait_ge(eb_ready, at(T2, t, 2 * q + p + 1))
                        act.wait_ge(ce_ready, at(T2, t, 2 * q - 1 + p))
                        nc.scalar.activation(eb[:, p, :], Dp[:], ACT.Exp).then_inc(ebs_ready, 1)
                    for p in range(2):
                        act.wait_ge(z_ready, at(T2, t, 2 * q + p + 1))
                        act.wait_ge(yt_ready, at(T2, t, 2 * q - 1 + p))
                        nc.scalar.activation(th[:, p, :], R[p][:], ACT.Tanh, scale=0.5).then_inc(th_ready, 1)
                    sines(t, q + 2)
                    squares(t, q, 0)
                    decays(t, q + 1, 0)
                    squares(t, q, 1)
                    decays(t, q + 1, 1)

        @block.gpsimd
        def _(pool):
            for s in (rot_ready, ce_ready, sqa_ready):
                pool.sem_inc(s, 1)

            def sums(t, q, p):
                for w in range(2):
                    pool.wait_ge(part_ready, at(T8, t, 8 * q + 4 * p + 2 * w + 2))
                    pool.wait_ge(y_ready, at(T2, t, 2 * q - 2))
                    nc.gpsimd.tensor_tensor(rot[:, q % 2, p, w, :], part[:, 2 * w, :], part[:, 2 * w + 1, :],
                                            ALU.add).then_inc(rot_ready, 1)

            def c_decayed(t, q):
                for p in range(2):
                    pool.wait_ge(ebs_ready, at(T2, t, 2 * q + p + 1))
                    pool.wait_ge(rot_ready, at(T4, t, 4 * q + 4))
                    pool.wait_ge(y_ready, at(T2, t, 2 * q - 1 + p))
                    nc.gpsimd.tensor_tensor(ce[:, p, :], rot[:, q % 2, p, 1, :], eb[:, p, :], ALU.mult).then_inc(ce_ready, 1)

            sums(0, 0, 0)
            sums(0, 0, 1)
            with pool.Fori(0, NS) as t:
                pool.wait_ge(ssq_ready, at(1, t, 0))
                for q in range(NQ):
                    sums(t, q + 1, 0)
                    c_decayed(t, q)
                    sums(t, q + 1, 1)
                    if q == 0:
                        pool.wait_ge(sq_ready, at(T2, t, 2))
                        nc.gpsimd.tensor_tensor(sqa[:], sq[:, 0, :], sq[:, 1, :], ALU.add).then_inc(sqa_ready, 1)
                        pool.wait_ge(sqa_ready, at(T2, t, 1))
                        pool.sem_inc(sqa_ready, 1)
                        continue
                    for p in range(2):
                        pool.wait_ge(sq_ready, at(T2, t, 2 * q + p + 1))
                        pool.wait_ge(sqa_ready, at(T2, t, 2 * q + p))
                        nc.gpsimd.tensor_tensor(sqa[:], sqa[:], sq[:, p, :], ALU.add).then_inc(sqa_ready, 1)


def finish(nc, K, u, xn_d, out):
    with ExitStack() as ctx:
        def sb(name, shape, dt=F32):
            return ctx.enter_context(nc.sbuf_tensor(name, shape, dt))

        def sem(name):
            return ctx.enter_context(nc.semaphore(name))

        ps = [ctx.enter_context(nc.psum_tensor(f"f_ps{i}", [P, 512], F32)) for i in range(2)]
        AHEAD = 4
        xn = sb("f_xn", [P, AHEAD, ST])
        xin = sb("f_xin", [P, AHEAD, ST])
        v = sb("f_v", [P, 2, ST])
        mag = sb("f_mag", [P, 2, ST])
        half = sb("f_half", [P, ST], FP8)
        small = sb("f_small", [P, ST])
        wv = sb("f_wv", [P, 2, P])
        xq = sb("f_xq", [P, 2, ST], BF16)
        wq = sb("f_wq", [P, P], BF16)
        gate = sb("f_gate", [P, 2, ST])
        th = sb("f_th", [P, 2, ST])
        sr = sb("f_sr", [P, 2, ST])
        o = sb("f_o", [P, 2, ST])
        sc = sb("f_sc", [P, 6])
        r = sb("f_r", [P, 4, NC])
        loaded = [sem(f"f_loaded{i}") for i in range(AHEAD)]
        stored = [sem("f_st0"), sem("f_st1")]
        chain, for_act, root_done = sem("f_chain"), sem("f_for_act"), sem("f_root_done")
        scales_done = sem("f_scales")
        scaled = sem("f_scaled")
        xq_ready, g_ready, gate_done, th_done = sem("f_xq"), sem("f_g"), sem("f_gate_done"), sem("f_th_done")
        sr_done, prod_done, o_ready = sem("f_sr_done"), sem("f_prod_done"), sem("f_o_ready")
        block = ctx.enter_context(nc.Block())
        u_v = u.rearrange("b (s c p) m -> (b s) p c m", c=CS, p=P)
        o_v = out.rearrange("b (s c p) m -> (b s) p c m", c=CS, p=P)
        v4 = lambda a: a.rearrange("p (c m) -> p c m", c=CS)

        @block.sync
        def _(sp):
            def store(t):
                sp.wait_ge(o_ready, t + 1)
                sp.dma_start(o_v[t], v4(o[:, t % 2, :])).then_inc(stored[t % 2], 16)

            for t in range(NS):
                if t >= AHEAD:
                    sp.wait_ge(o_ready, t - AHEAD + 1)
                sp.dma_start(xn[:, t % AHEAD, :], xn_d[t]).then_inc(loaded[t % AHEAD], 16)
                sp.dma_start(v4(xin[:, t % AHEAD, :]), u_v[t]).then_inc(loaded[t % AHEAD], 16)
                if t >= AHEAD - 1:
                    store(t - AHEAD + 1)
            for t in range(NS - AHEAD + 1, NS):
                store(t)
            for i in range(2):
                sp.wait_ge(stored[i], 16 * (NS // 2))

        @block.tensor
        def _(pe):
            for t in range(NS):
                pe.wait_ge(xq_ready, t + 2)
                if t >= 2:
                    pe.wait_ge(gate_done, t - 1)
                for c in range(CS):
                    last = nc.tensor.matmul(ps[t % 2][:, c * P:c * P + P], xq[:, t % 2, c * P:c * P + P], wq[:], start=True, stop=True)
                last.then_inc(g_ready, 1)

        @block.scalar
        def _(act):
            act.wait_ge(for_act, 1)
            nc.scalar.activation(r[:, 1, :], r[:, 0, :], ACT.Sqrt).then_inc(root_done, 1)
            act.wait_ge(scales_done, 1)
            nc.scalar.activation(wv[:, 0, :], K["w_ffn"][:], ACT.Copy, scale=sc[:, 1:2]).then_inc(scaled, 1)
            nc.scalar.activation(wv[:, 1, :], K["w_ffn"][:], ACT.Abs, scale=sc[:, 1:2]).then_inc(scaled, 1)
            for t in range(NS + 1):
                if t < NS:
                    act.wait_ge(loaded[t % AHEAD], 32 * (t // AHEAD + 1))
                    if t >= 2:
                        act.wait_ge(xq_ready, t)
                    nc.scalar.activation(v[:, t % 2, :], xn[:, t % AHEAD, :], ACT.Copy, scale=sc[:, 0:1]).then_inc(scaled, 1)
                    nc.scalar.activation(mag[:, t % 2, :], xn[:, t % AHEAD, :], ACT.Abs, scale=sc[:, 0:1]).then_inc(scaled, 1)
                if t >= 1:
                    act.wait_ge(gate_done, t)
                    if t >= 3:
                        act.wait_ge(prod_done, t - 2)
                    nc.scalar.activation(th[:, (t - 1) % 2, :], gate[:, (t - 1) % 2, :], ACT.Tanh, scale=0.5).then_inc(th_done, 1)

        @block.vector
        def _(dve):
            n = [0]

            def link(ins):
                n[0] += 1
                ins.then_inc(chain, 1)
                dve.wait_ge(chain, n[0])

            link(nc.vector.tensor_scalar(r[:, 0, :], K["ssq"][:], 0.25 / DI, EPS, ALU.mult, ALU.add))
            dve.sem_inc(for_act, 1)
            link(nc.vector.tensor_scalar(sc[:, 0:2], K["amax"][:], 1e-12, None, ALU.max))
            link(nc.vector.reciprocal(sc[:, 0:2], sc[:, 0:2]))
            link(nc.vector.tensor_scalar(sc[:, 0:2], sc[:, 0:2], FP8_MAX, None, ALU.mult))
            dve.sem_inc(scales_done, 1)
            link(nc.vector.reciprocal(sc[:, 2:4], sc[:, 0:2]))
            link(nc.vector.tensor_tensor(sc[:, 4:5], sc[:, 2:3], sc[:, 3:4], ALU.mult))
            dve.wait_ge(root_done, 1)
            link(nc.vector.reciprocal(r[:, 2, :], r[:, 1, :]))
            link(nc.vector.tensor_tensor(r[:, 3, :], r[:, 2, :], r[:, 2, :], ALU.mult))
            link(nc.vector.tensor_tensor(r[:, 3, :], r[:, 3, :], r[:, 0, :], ALU.mult))
            link(nc.vector.tensor_scalar(r[:, 3, :], r[:, 3, :], -0.5, 1.5, ALU.mult, ALU.add))
            link(nc.vector.tensor_tensor(r[:, 2, :], r[:, 2, :], r[:, 3, :], ALU.mult))
            link(nc.vector.tensor_scalar(r[:, 2, :], r[:, 2, :], 0.25, None, ALU.mult))
            dve.sem_inc(scales_done, 1)

            def quantise(dst, x, mg, m):
                link(nc.vector.tensor_scalar(half[:, 0:m], x, 0.5, None, ALU.mult, saturate=False))
                link(nc.vector.tensor_scalar(small[:, 0:m], x, 24576.0, -24576.0, ALU.add, ALU.add))
                link(nc.vector.scalar_tensor_tensor(out=small[:, 0:m], in0=half[:, 0:m], scalar=-2.0, in1=small[:, 0:m],
                                                    op0=ALU.mult, op1=ALU.add))
                link(nc.vector.scalar_tensor_tensor(out=small[:, 0:m], in0=mg, scalar=2.0 ** -5, in1=small[:, 0:m],
                                                    op0=ALU.is_lt, op1=ALU.mult))
                nc.vector.scalar_tensor_tensor(out=dst, in0=half[:, 0:m], scalar=2.0, in1=small[:, 0:m],
                                               op0=ALU.mult, op1=ALU.add).then_inc(xq_ready, 1)

            dve.wait_ge(scaled, 2)
            quantise(wq[:], wv[:, 0, :], wv[:, 1, :], P)
            dve.wait_ge(xq_ready, 1)
            b4 = lambda a: bcast(a.unsqueeze(1), [P, CS, P])
            for t in range(NS + 2):
                if t < NS:
                    dve.wait_ge(scaled, 2 * t + 4)
                    if t >= 2:
                        dve.wait_ge(g_ready, t - 1)
                    quantise(xq[:, t % 2, :], v[:, t % 2, :], mag[:, t % 2, :], ST)
                    dve.wait_ge(xq_ready, t + 2)
                if 1 <= t <= NS:
                    i = (t - 1) % 2
                    dve.wait_ge(g_ready, t)
                    if t >= 3:
                        dve.wait_ge(prod_done, t - 2)
                        dve.wait_ge(th_done, t - 2)
                    nc.vector.scalar_tensor_tensor(out=v4(gate[:, i, :]), in0=v4(ps[i][:]), scalar=sc[:, 4:5],
                                                   in1=b4(K["d_ffnb"][:]), op0=ALU.mult, op1=ALU.add).then_inc(gate_done, 1)
                if t >= 2:
                    i = t % 2
                    dve.wait_ge(th_done, t - 1)
                    dve.wait_ge(gate_done, t - 1)
                    link(nc.vector.scalar_tensor_tensor(out=gate[:, i, :], in0=th[:, i, :], scalar=1.0, in1=gate[:, i, :],
                                                        op0=ALU.add, op1=ALU.mult))
                    dve.wait_ge(sr_done, t - 1)
                    nc.vector.tensor_tensor(sr[:, i, :], gate[:, i, :], sr[:, i, :], ALU.mult).then_inc(prod_done, 1)

        @block.gpsimd
        def _(pool):
            pool.wait_ge(scales_done, 2)
            for t in range(NS + 1):
                if t < NS:
                    if t >= 2:
                        pool.wait_ge(o_ready, t - 1)
                    nc.gpsimd.tensor_tensor(v4(sr[:, t % 2, :]), v4(K["s_acc"][:, t * ST:(t + 1) * ST]),
                                            bcast(r[:, 2, t * CS:(t + 1) * CS].unsqueeze(2), [P, CS, P]), ALU.mult).then_inc(sr_done, 1)
                if t >= 1:
                    i = (t - 1) % 2
                    pool.wait_ge(prod_done, t)
                    pool.wait_ge(loaded[(t - 1) % AHEAD], 32 * ((t - 1) // AHEAD + 1))
                    if t >= 3:
                        pool.wait_ge(stored[i], 16 * ((t - 1) // 2))
                    nc.gpsimd.tensor_tensor(o[:, i, :], sr[:, i, :], xin[:, (t - 1) % AHEAD, :], ALU.add).then_inc(o_ready, 1)


def program(nc, dram, out):
    scratch = [nc.dram_tensor(n, [NS, P, ST], F32, kind="Internal").ap() for n in ("xn_t", "tc_t", "bc_t")]
    with ExitStack() as ctx:
        shapes = dict(ident=[P, P], ones=[P, P], w_zx=[P, 2 * DI], w_th=[P, H * 32], w_o=[P, DI], w_ffn=[P, P], prmT=[P, 80],
                      cols=[P, 2], goes_on=[P, NS], carry=[P, NP, HD], s_acc=[P, TOK], kk=[P, NC * H], cc=[P, NC * H],
                      dec=[P, NC * H], dtot=[P, NC * NP], ssq=[P, NC], amax=[P, 2], d_ffnb=[P, P])
        K = {n: ctx.enter_context(nc.sbuf_tensor("k_" + n, s, F32)) for n, s in shapes.items()}
        for n, s in dict(ident_bf=[P, P], zeros_bf=[P, P], mask=[P, ST], sel=[3 * H, H], sel_pair=[3 * H, NP * P], nsel=[3 * H, H], cumT=[3 * H, TOK]).items():
            K[n] = ctx.enter_context(nc.sbuf_tensor("k_" + n, s, BF16))
        prepare(nc, K, dram, scratch)
        units(nc, K, scratch)
        finish(nc, K, dram[0], scratch[0], out)


NAMES = ["u", "in_proj_w", "dt_bias", "A_log", "D", "B_norm_w", "C_norm_w", "B_bias", "C_bias", "norm_w", "out_proj_w"]


def kernel(**inputs):
    import numpy as np
    import concourse.bacc as bacc
    from concourse.bass_utils import run_bass_kernel_spmd as run

    nc = bacc.Bacc("TRN2", target_bir_lowering=False, num_devices=1)
    arrays, dram = {}, []
    for name in ["L0_attn_" + n for n in NAMES] + ["L0_ffn_weight", "L0_ffn_bias"]:
        a = np.ascontiguousarray(inputs[name])
        arrays["in_" + name] = a
        dram.append(nc.dram_tensor("in_" + name, a.shape, mybir.dt.from_np(a.dtype), kind="ExternalInput").ap())
    out = nc.dram_tensor("out", (BATCH, L, DM), F32, kind="ExternalOutput").ap()
    program(nc, dram, out)
    return run(nc, [arrays], core_ids=[0]).results[0]["out"]
```

```python
from contextlib import ExitStack

import concourse.bass as bass
from concourse import mybir

F32 = mybir.dt.float32
BF16 = mybir.dt.bfloat16
FP8 = mybir.dt.float8e4
ALU = mybir.AluOpType
ACT = mybir.ActivationFunctionType
AX = mybir.AxisListType

P = 128
H, HD, N, DM = 32, 64, 64, 128
DI = H * HD
BATCH, L = 4, 1024
TOK = BATCH * L
NC = TOK // P
CS = 4
ST = CS * P
NS = TOK // ST
NQ = H // 4
NP = H // 2
SPB = L // ST
EPS = 1e-5
PI = 3.14159274
TWO_PI = 6.283185
TURN = 0.15915494309189535
MAGIC = 12582912.0
MASKED = -1.0e30
FP8_MAX = 448.0


def bcast(ap, shape):
    return ap.to_broadcast(shape)


def prepare(nc, K, dram, scratch, cum_stored):
    u, w_in, dt_bias, a_log, d_skip, b_norm, c_norm, b_bias, c_bias, norm_w, w_out, ffn_w, ffn_b = dram
    xn_d, tc_d, bc_d, cum_d = scratch
    with ExitStack() as ctx:
        def sb(name, shape, dt=F32):
            return ctx.enter_context(nc.sbuf_tensor(name, shape, dt))

        def sem(name):
            return ctx.enter_context(nc.semaphore(name))

        ps = [ctx.enter_context(nc.psum_tensor(f"a_ps{i}", [P, 512], F32)) for i in range(6)]
        ps_bf = [ctx.enter_context(nc.psum_tensor(f"a_psbf{i}", [P, 8, P], BF16)) for i in range(2)]
        big = sb("a_big", [P, NC * P])
        tmp = sb("a_tmp", [P, NC * P])
        xnT = sb("a_xnT", [P, TOK])
        tcT = sb("a_tcT", [P, TOK])
        ones = K["ones"]
        one_row = sb("a_one_row", [P, 1024])
        stage2 = sb("a_stage2", [P, 11 * P])
        prm = sb("a_prm", [P, P])
        cbn = sb("a_cbn", [H, P])
        row = sb("a_row", [1, 3 * H + P + 2 * N])
        rowb = sb("a_rowb", [P, 3 * H + P + 2 * N])
        wdl = sb("a_wdl", [P, 2 * H])
        wbc = sb("a_wbc", [P, P])
        cbT = sb("a_cbT", [P, H])
        mats = sb("a_mats", [P, 3, P])
        st32 = sb("a_st32", [P, 8, 2 * NC])
        cb1 = sb("a_cb1", [H, N])
        cbs = sb("a_cbs", [H, 1])
        cbs2 = sb("a_cbs2", [H, P])
        cbb = sb("a_cbb", [P, H])
        sel = sb("a_sel", [3 * H, H], BF16)
        wnc = sb("a_wnc", [P, 1])
        s = [sb(f"a_s{i}", [P, NC * H]) for i in range(4)]
        dl = sb("a_dl", [P, NC * 2 * H])
        cum3 = sb("a_cum3", [P, NC, 3 * H], BF16)

        u_loaded = [sem(f"a_u_loaded{i}") for i in range(BATCH)]
        zx_loaded, rest_loaded, wo_loaded, prm_loaded = sem("a_zx"), sem("a_rest"), sem("a_wo"), sem("a_prm")
        ident_ready = sem("a_ident_ready")
        consts = sem("a_consts")
        xn_done = sem("a_xn_done")
        bc_done = sem("a_bc_done")
        w_t = sem("a_w_t")
        w_v = sem("a_w_v")
        w_a = sem("a_w_a")
        stored = sem("a_stored")
        dch = sem("a_dch")
        ach = sem("a_ach")
        centred, squared = sem("a_centred"), sem("a_squared")
        pch = sem("a_pch")
        pe_m = sem("a_pe_m")
        v_m = sem("a_v_m")
        for_act = sem("a_for_act")
        a_m = sem("a_a_m")
        block = ctx.enter_context(nc.Block())

        zx_nat = tmp[:].rearrange("p (a m) -> p a m", a=NC)
        wo_nat = tcT[:, 0:DI]
        ident = K["ident"]

        @block.sync
        def _(sp):
            for i in range(BATCH):
                sp.dma_start(big[:, i * L:(i + 1) * L].rearrange("p (c m) -> p c m", m=DM),
                             u[i].rearrange("(c p) m -> p c m", p=P)).then_inc(u_loaded[i], 16)
            sp.dma_start(zx_nat, w_in[0:2 * DI].rearrange("(a p) m -> p a m", p=P)).then_inc(zx_loaded, 16)
            o = 2 * DI
            sp.dma_start(stage2[:, 0:P], w_in[o:o + P]).then_inc(rest_loaded, 16)
            o += P
            sp.dma_start(stage2[0:H, 9 * P:10 * P], w_in[o:o + H]).then_inc(rest_loaded, 16)
            sp.dma_start(stage2[:, P:9 * P].rearrange("p (a m) -> p a m", a=8),
                         w_in[o + H:o + H + 1024].rearrange("(a p) m -> p a m", p=P)).then_inc(rest_loaded, 16)
            sp.dma_start(stage2[H:2 * H, 9 * P:10 * P], w_in[o + H + 1024:o + 2 * H + 1024]).then_inc(rest_loaded, 16)
            sp.dma_start(stage2[:, 10 * P:11 * P], ffn_w).then_inc(rest_loaded, 16)
            sp.dma_start(wo_nat, w_out).then_inc(wo_loaded, 16)
            sp.dma_start(prm[0:16, :], norm_w.rearrange("(a p) -> a p", p=P)).then_inc(prm_loaded, 16)
            for i, bias in enumerate((b_bias, c_bias)):
                r = 16 + 32 * i
                sp.dma_start(prm[r:r + 16, :], bias.rearrange("(q a) n -> q (a n)", a=2)).then_inc(prm_loaded, 16)
                src = bias.rearrange("(q a) (f j) -> q a f j", a=2, f=2)
                dst = prm[r + 16:r + 32, :].rearrange("q (a f j) -> q a f j", a=2, f=2)
                for f in range(2):
                    sp.dma_start(dst[:, :, f, :], src[:, :, 1 - f, :]).then_inc(prm_loaded, 16)
            sp.dma_start(cbn[:, 0:N], c_bias).then_inc(prm_loaded, 16)
            sp.dma_start(cbn[:, N:2 * N], b_bias).then_inc(prm_loaded, 16)
            for i, v in enumerate((b_norm, c_norm)):
                sp.dma_start(wnc[N * i:N * i + N, :], v.rearrange("(n a) -> n a", a=1)).then_inc(prm_loaded, 16)
            at = 0
            for v, n in ((dt_bias, H), (a_log, H), (d_skip, H), (ffn_b, P), (b_norm, N), (c_norm, N)):
                sp.dma_start(row[0:1, at:at + n], v.rearrange("(a n) -> a n", a=1)).then_inc(prm_loaded, 16)
                at += n
            sp.wait_ge(v_m, 2)
            sp.dma_start(xn_d.rearrange("s p t -> p s t"), xnT[:].rearrange("p (s t) -> p s t", s=NS)).then_inc(stored, 16)
            sp.dma_start(tc_d.rearrange("s p t -> p s t"), tcT[:].rearrange("p (s t) -> p s t", s=NS)).then_inc(stored, 16)
            sp.wait_ge(v_m, 5)
            sp.dma_start(bc_d.rearrange("s p t -> p s t"), tmp[:].rearrange("p (s t) -> p s t", s=NS)).then_inc(stored, 16)
            sp.wait_ge(v_m, 12)
            for i in range(3):
                sp.dma_start(cum_d.rearrange("t c i h s -> i h (t c) s")[i],
                             K["cumT"][H * i:H * i + H, :].rearrange("h (x s) -> h x s", s=P)).then_inc(cum_stored, 16)
            sp.wait_ge(stored, 48)

        @block.gpsimd
        def _(pool):
            n = [0]

            def link(ins):
                n[0] += 1
                ins.then_inc(pch, 1)
                pool.wait_ge(pch, n[0])

            link(nc.gpsimd.memset(ident[:], 0.0))
            link(nc.gpsimd.affine_select(out=ident[:], in_=ident[:], compare_op=ALU.not_equal, fill=1.0, base=0,
                                         pattern=[[-1, P]], channel_multiplier=1))
            pool.sem_inc(ident_ready, 1)
            link(nc.gpsimd.memset(ones[:], 1.0))
            link(nc.gpsimd.memset(one_row[:], 1.0))
            link(nc.gpsimd.memset(K["ident_bf"][:], 0.0))
            link(nc.gpsimd.affine_select(out=K["ident_bf"][:], in_=K["ident_bf"][:], compare_op=ALU.not_equal, fill=1.0,
                                         base=0, pattern=[[-1, P]], channel_multiplier=1))
            link(nc.gpsimd.memset(K["zeros_bf"][:], 0.0))
            link(nc.gpsimd.memset(mats[:], 0.0))
            link(nc.gpsimd.affine_select(out=mats[:, 0, :], in_=one_row[:, 0:P], compare_op=ALU.is_ge, fill=0.0, base=0,
                                         pattern=[[1, P]], channel_multiplier=-1))
            link(nc.gpsimd.affine_select(out=mats[:, 1, :], in_=mats[:, 1, :], compare_op=ALU.not_equal, fill=1.0, base=-1,
                                         pattern=[[-1, P]], channel_multiplier=1))
            link(nc.gpsimd.affine_select(out=mats[:, 2, :], in_=mats[:, 2, :], compare_op=ALU.not_equal, fill=1.0, base=P - 1,
                                         pattern=[[-1, P]], channel_multiplier=1))
            link(nc.gpsimd.memset(K["mask"][:], 0.0))
            link(nc.gpsimd.affine_select(out=K["mask"][:].rearrange("p (c t) -> p c t", c=CS),
                                         in_=K["mask"][:].rearrange("p (c t) -> p c t", c=CS), compare_op=ALU.is_ge,
                                         fill=MASKED, base=0, pattern=[[0, CS], [1, P]], channel_multiplier=-1))
            link(nc.gpsimd.memset(sel[:], 0.0))
            for i in range(3):
                link(nc.gpsimd.affine_select(out=sel[:], in_=sel[:], compare_op=ALU.not_equal, fill=1.0,
                                             base=-32 * i, pattern=[[-1, H]], channel_multiplier=1))
            link(nc.gpsimd.tensor_copy(K["pick"][0:3 * H, :].rearrange("k (h d) -> k h d", d=P),
                                       bcast(sel[:].unsqueeze(2), [3 * H, H, P])))
            link(nc.gpsimd.memset(K["cols"][:, 0:1], PI / 2))
            link(nc.gpsimd.memset(K["cols"][:, 1:2], MAGIC))
            link(nc.gpsimd.memset(K["goes_on"][:], 1.0))
            for i in range(BATCH):
                link(nc.gpsimd.memset(K["goes_on"][:, SPB * i:SPB * i + 1], 0.0))
            link(nc.gpsimd.memset(K["carry"][:], 0.0))
            pool.sem_inc(consts, 1)
            own = K["cumT"][3 * H:3 * H + 3 * CS, :]
            own4 = own.rearrange("r (t c s) -> r t c s", t=NS, c=CS)
            link(nc.gpsimd.memset(own, -1.0))
            for base, mult in ((0, 1), (2, -1)):
                link(nc.gpsimd.affine_select(out=own4, in_=own4, compare_op=ALU.is_ge, fill=0.0, base=base,
                                             pattern=[[0, NS], [-3 * mult, CS], [0, P]], channel_multiplier=mult))

        groups = []
        for g in range(8):
            groups.append([zx_nat[:, 4 * g + i, :] for i in range(4)])
        groups.append([stage2[:, 0:P], stage2[0:2 * H, 9 * P:10 * P], stage2[:, 10 * P:11 * P], prm[0:80, :]])
        for g in range(2):
            groups.append([stage2[:, (1 + 4 * g + i) * P:(2 + 4 * g + i) * P] for i in range(4)])
        for g in range(4):
            groups.append([wo_nat[:, (4 * g + i) * P:(4 * g + i + 1) * P] for i in range(4)])
        groups.append([cbn[:, :]])
        NG = len(groups)

        @block.tensor
        def _(pe):
            pe.wait_ge(ident_ready, 1)
            pe.wait_ge(zx_loaded, 16)
            for g, srcs in enumerate(groups):
                if g == 8:
                    pe.wait_ge(rest_loaded, 80)
                    pe.wait_ge(prm_loaded, 16 * 17)
                if g == 11:
                    pe.wait_ge(wo_loaded, 16)
                if g >= 4:
                    pe.wait_ge(w_v if g % 2 == 0 else w_a, (g - 4) // 2 + 1)
                for i, src in enumerate(srcs):
                    r = src.shape[0]
                    last = nc.tensor.transpose(ps[g % 4][:, i * P:i * P + r], src, ident[0:r, 0:r])
                last.then_inc(w_t, 1)
            pe.wait_ge(consts, 1)
            nc.tensor.matmul(ps[4][:, 0:row.shape[1]], one_row[0:1, 0:P], row[0:1, :], start=True, stop=True).then_inc(pe_m, 1)
            pe.wait_ge(w_v, NG // 2)
            pe.wait_ge(w_a, NG // 2)
            for g in range(8):
                if g >= 4:
                    pe.wait_ge(w_v if g % 2 == 0 else w_a, NG // 2 + (g - 4) // 2 + 1)
                pe.wait_ge(xn_done, g // 2 + 1)
                for i in range(4):
                    c = 4 * g + i
                    last = nc.tensor.transpose(ps[g % 4][:, i * P:i * P + P], big[:, c * P:c * P + P], ident[:])
                last.then_inc(w_t, 1)
            pe.wait_ge(w_v, NG // 2 + 4)
            pe.wait_ge(w_a, NG // 2 + 4)
            for g in range(12):
                if g >= 4:
                    pe.wait_ge(w_v, NG // 2 + g + 1)
                    pe.wait_ge(w_a, NG // 2 + g + 1)
                for i in range(4 if g < 8 else 8):
                    if g < 8:
                        c = 4 * g + i
                        last = nc.tensor.matmul(ps[g % 4][:, i * P:i * P + P], xnT[:, c * P:c * P + P], wbc[:],
                                                start=True, stop=True)
                    else:
                        c = 8 * (g - 8) + i
                        last = nc.tensor.matmul(ps[g % 4][:, i * 64:i * 64 + 64], xnT[:, c * P:c * P + P], wdl[:],
                                                start=True, stop=True)
                last.then_inc(w_t, 1)
            pe.wait_ge(v_m, 3)
            nc.tensor.matmul(ps[5][:, 0:H], cbs2[:, :], ident[0:H, 0:H], start=True, stop=True).then_inc(pe_m, 1)
            pe.wait_ge(w_v, NG // 2 + 14)
            pe.wait_ge(w_a, NG // 2 + 14)
            for g in range(8):
                if g >= 4:
                    pe.wait_ge(w_v if g % 2 == 0 else w_a, NG // 2 + 14 + (g - 4) // 2 + 1)
                pe.wait_ge(bc_done, g // 2 + 1)
                for i in range(4):
                    c = 4 * g + i
                    last = nc.tensor.transpose(ps[g % 4][:, i * P:i * P + P], big[:, c * P:c * P + P], ident[:])
                last.then_inc(w_t, 1)
            pe.wait_ge(v_m, 5)
            for c in range(NC):
                last = nc.tensor.matmul(ps[c // 16][:, (c % 16) * H:(c % 16 + 1) * H], tmp[:, c * P:c * P + P], cbT[:],
                                        start=True, stop=True)
            last.then_inc(pe_m, 1)
            pe.wait_ge(v_m, 6)
            for i in range(2):
                nc.tensor.matmul(ps[2 + i][:], mats[:, 0, :], s[2][:, 512 * i:512 * i + 512], start=True, stop=True)
                last = nc.tensor.matmul(ps[4 + i][:], ones[:, 0:P], s[2][:, 512 * i:512 * i + 512], start=True, stop=True)
            last.then_inc(pe_m, 1)
            pe.wait_ge(v_m, 7)
            for i in range(2):
                n = 512 - H * i
                nc.tensor.matmul(ps[i][:], mats[:, 1, :], s[1][:, 512 * i:512 * i + 512], start=True, stop=False)
                last = nc.tensor.matmul(ps[i][:, 0:n], mats[:, 2, :], s[1][:, 512 * i + H:512 * i + H + n], start=False, stop=True)
            last.then_inc(pe_m, 1)
            pe.wait_ge(v_m, 8)
            for g in range(4):
                if g >= 2:
                    pe.wait_ge(v_m, 7 + g)
                for i in range(8):
                    last = nc.tensor.transpose(ps_bf[g % 2][0:3 * H, i, :], cum3[:, 8 * g + i, :], K["ident_bf"][:])
                last.then_inc(pe_m, 1)

        def weight_out(g, copy):
            b = ps[g % 4]
            if g < 8:
                return [copy(K["w_zx"][:, 512 * g:512 * g + 512], b[:])]
            if g == 8:
                return [copy(wbc[:], b[:, 0:P]), copy(wdl[:], b[:, P:P + 64]), copy(K["w_ffn"][:], b[:, 2 * P:3 * P]),
                        copy(K["prmT"][:, 0:80], b[:, 3 * P:3 * P + 80])]
            return [copy(cbT[:], b[:, 0:H])]

        @block.vector
        def _(dve):
            n = [0]

            def link(ins):
                n[0] += 1
                ins.then_inc(dch, 1)
                dve.wait_ge(dch, n[0])

            def rsqrt_refined(r, v, t):
                link(nc.vector.tensor_tensor(t, r, r, ALU.mult))
                link(nc.vector.tensor_tensor(t, t, v, ALU.mult))
                link(nc.vector.tensor_scalar(t, t, -0.5, 1.5, ALU.mult, ALU.add))
                link(nc.vector.tensor_tensor(r, r, t, ALU.mult))

            big3 = big[:].rearrange("p (c m) -> p c m", c=NC)
            st = [st32[:, i, 0:NC] for i in range(8)]
            NB = L // P
            for i in range(BATCH):
                dve.wait_ge(u_loaded[i], 16)
                k = slice(NB * i, NB * i + NB)
                link(nc.vector.tensor_reduce(st[0][:, k], big3[:, k], AX.X, ALU.add))
                link(nc.vector.tensor_scalar(st[0][:, k], st[0][:, k], 1.0 / DM, None, ALU.mult))
                nc.vector.tensor_tensor(big3[:, k], big3[:, k], bcast(st[0][:, k].unsqueeze(2), [P, NB, DM]),
                                        ALU.subtract).then_inc(centred, 1)
            xnT3 = xnT[:].rearrange("p (c m) -> p c m", c=NC)
            for i in range(BATCH):
                dve.wait_ge(squared, i + 1)
                link(nc.vector.tensor_reduce(st[1][:, NB * i:NB * i + NB], xnT3[:, NB * i:NB * i + NB], AX.X, ALU.add))
            link(nc.vector.tensor_scalar(st[1], st[1], 1.0 / DM, EPS, ALU.mult, ALU.add))
            dve.sem_inc(for_act, 1)
            for g in range(0, NG, 2):
                dve.wait_ge(w_t, g + 1)
                b = ps[g % 4]
                if g == 10:
                    nc.vector.tensor_scalar(K["w_th"][:, 512:1024], b[:], TURN, None, ALU.mult).then_inc(w_v, 1)
                elif g in (12, 14):
                    a0 = 4 * (g - 11)
                    for i in range(4):
                        link(nc.vector.tensor_scalar(K["w_o"][:, (a0 + i) * P:(a0 + i + 1) * P], b[:, i * P:i * P + P],
                                                     K["prmT"][:, a0 + i:a0 + i + 1], None, ALU.mult))
                    dve.sem_inc(w_v, 1)
                else:
                    outs = weight_out(g, nc.vector.tensor_copy)
                    for o in outs[:-1]:
                        link(o)
                    outs[-1].then_inc(w_v, 1)
            dve.wait_ge(a_m, 1)
            link(nc.vector.reciprocal(st[3], st[2]))
            rsqrt_refined(st[3], st[1], st[5])
            for i in range(BATCH):
                k = slice(NB * i, NB * i + NB)
                nc.vector.tensor_tensor(big3[:, k], big3[:, k], bcast(st[3][:, k].unsqueeze(2), [P, NB, DM]),
                                        ALU.mult).then_inc(xn_done, 1)
            link(nc.vector.tensor_reduce(K["mags"][:, 2 * NS:2 * NS + 1], stage2[:, 10 * P:11 * P], AX.X, ALU.max))
            link(nc.vector.tensor_reduce(K["mags"][:, 2 * NS + 1:2 * NS + 2], stage2[:, 10 * P:11 * P], AX.X, ALU.min))
            dve.sem_inc(v_m, 1)
            for g in range(0, 8, 2):
                dve.wait_ge(w_t, NG + g + 1)
                nc.vector.tensor_copy(xnT[:, 512 * g:512 * g + 512], ps[g % 4][:]).then_inc(w_v, 1)
            dve.wait_ge(consts, 1)
            dve.wait_ge(w_a, NG // 2 + 4)
            dve.wait_ge(w_v, NG // 2 + 4)
            for b in range(BATCH):
                link(nc.vector.tensor_tensor_scan(tcT[:, b * L:(b + 1) * L], one_row[:], xnT[:, b * L:(b + 1) * L],
                                                  0.0, ALU.mult, ALU.add))
            dve.sem_inc(v_m, 1)
            dve.wait_ge(pe_m, 1)
            link(nc.vector.tensor_copy(rowb[:], ps[4][:, 0:row.shape[1]]))
            link(nc.vector.tensor_copy(K["d_ffnb"][:], rowb[:, 3 * H:3 * H + P]))
            link(nc.vector.tensor_tensor(cb1[:], cbn[:, 0:N], cbn[:, N:2 * N], ALU.mult))
            link(nc.vector.tensor_reduce(cbs[:], cb1[:], AX.X, ALU.add))
            nc.vector.tensor_copy(cbs2[:], bcast(cbs[:], [H, P])).then_inc(v_m, 1)
            dlv = dl[:].rearrange("p (c k) -> p c k", k=64)
            for g in range(8):
                dve.wait_ge(w_t, NG + 8 + g + 1)
                dve.wait_ge(w_a, NG // 2 + 4 + g + 1)
                nc.vector.tensor_copy(big[:, 512 * g:512 * g + 512], ps[g % 4][:]).then_inc(w_v, 1)
            big64 = big[:].rearrange("p (g n) -> p g n", n=N)
            tmp64 = tmp[:].rearrange("p (g n) -> p g n", n=N)
            v64, r64, t64 = st32[:, 1, :], st32[:, 3, :], st32[:, 5, :]
            link(nc.vector.tensor_reduce(v64, tmp64, AX.X, ALU.add))
            link(nc.vector.tensor_scalar(v64, v64, 1.0 / N, EPS, ALU.mult, ALU.add))
            dve.sem_inc(for_act, 1)
            for g in (8, 10):
                dve.wait_ge(w_t, NG + 8 + g + 1)
                nc.vector.tensor_copy(dl[:, 512 * (g - 8):512 * (g - 7)], ps[g % 4][:]).then_inc(w_v, 1)
            dve.wait_ge(pe_m, 2)
            link(nc.vector.tensor_copy(cbb[:], ps[5][:, 0:H]))
            dve.wait_ge(w_a, NG // 2 + 14)
            dve.wait_ge(w_v, NG // 2 + 14)
            dve.wait_ge(a_m, 2)
            link(nc.vector.reciprocal(r64, st32[:, 2, :]))
            rsqrt_refined(r64, v64, t64)
            for i in range(BATCH):
                k = slice(2 * NB * i, 2 * NB * (i + 1))
                nc.vector.tensor_tensor(big64[:, k], big64[:, k], bcast(r64[:, k].unsqueeze(2), [P, 2 * NB, N]),
                                        ALU.mult).then_inc(bc_done, 1)
            dve.sem_inc(v_m, 1)
            dve.wait_ge(bc_done, BATCH)
            wbw = rowb[:, 3 * H + P:3 * H + P + N]
            link(nc.vector.tensor_tensor(wbw, wbw, rowb[:, 3 * H + P + N:3 * H + 2 * P], ALU.mult))
            pr = tcT[:, 0:NC * N].rearrange("p (c n) -> p c n", n=N)
            dve.wait_ge(stored, 32)
            link(nc.vector.tensor_tensor(pr, big3[:, :, 0:N], big3[:, :, N:2 * N], ALU.mult))
            for g in range(0, 8, 2):
                dve.wait_ge(w_t, NG + 20 + g + 1)
                nc.vector.tensor_scalar(tmp[:, 512 * g:512 * g + 512], ps[g % 4][:], wnc[:, 0:1], None, ALU.mult).then_inc(w_v, 1)
                if g == 2:
                    link(nc.vector.tensor_tensor(pr, pr, bcast(wbw.unsqueeze(1), [P, NC, N]), ALU.mult))
                if g == 6:
                    link(nc.vector.tensor_reduce(st[0], pr, AX.X, ALU.add))
            dve.wait_ge(w_a, NG // 2 + 18)
            dve.wait_ge(w_v, NG // 2 + 18)
            dve.sem_inc(v_m, 1)
            v3 = [x[:].rearrange("p (c h) -> p c h", h=H) for x in s]
            one_h = lambda a: bcast(rowb[:, a * H:(a + 1) * H].unsqueeze(1), [P, NC, H])
            link(nc.vector.tensor_tensor(v3[0], dlv[:, :, 0:H], one_h(0), ALU.add))
            nc.vector.scalar_tensor_tensor(out=s[1][:], in0=s[0][:], scalar=-1.0, in1=s[0][:],
                                           op0=ALU.mult, op1=ALU.min).then_inc(for_act, 1)
            dve.wait_ge(a_m, 3)
            link(nc.vector.tensor_scalar(s[2][:], s[1][:], 1.0, None, ALU.add))
            dve.sem_inc(for_act, 1)
            link(nc.vector.tensor_scalar(K["dec"][:], s[2][:], -1.0, None, ALU.add))
            dve.sem_inc(for_act, 1)
            link(nc.vector.tensor_tensor(s[1][:], s[1][:], K["dec"][:], ALU.subtract))
            link(nc.vector.tensor_scalar(s[0][:], s[0][:], 0.0, None, ALU.max))
            link(nc.vector.tensor_scalar(s[3][:], s[3][:], 1.0, None, ALU.add))
            link(nc.vector.reciprocal(s[3][:], s[3][:]))
            dve.wait_ge(a_m, 4)
            link(nc.vector.tensor_tensor(s[1][:], s[1][:], s[2][:], ALU.mult))
            link(nc.vector.tensor_tensor(s[0][:], s[0][:], s[1][:], ALU.add))
            link(nc.vector.tensor_tensor(s[0][:], s[0][:], K["kk"][:], ALU.add))
            link(nc.vector.tensor_tensor(K["kk"][:], s[3][:], s[0][:], ALU.mult))
            link(nc.vector.tensor_scalar(s[1][:], s[3][:], -1.0, 1.0, ALU.mult, ALU.add))
            link(nc.vector.tensor_tensor(s[1][:], s[1][:], s[0][:], ALU.mult))
            link(nc.vector.tensor_scalar(rowb[:, H:2 * H], rowb[:, H:2 * H], -1.0, None, ALU.mult))
            link(nc.vector.tensor_tensor(v3[2], v3[0], one_h(1), ALU.mult))
            dve.sem_inc(v_m, 1)
            dve.wait_ge(pe_m, 3)
            for i in range(2):
                o = v3[3][:, 16 * i:16 * i + 16, :]
                link(nc.vector.tensor_tensor(o, ps[i][:].rearrange("p (c h) -> p c h", h=H),
                                             bcast(st[0][:, 16 * i:16 * i + 16].unsqueeze(2), [P, 16, H]), ALU.add))
            link(nc.vector.tensor_tensor(v3[3], v3[3], bcast(cbb[:].unsqueeze(1), [P, NC, H]), ALU.add))
            dve.sem_inc(v_m, 1)
            dve.wait_ge(pe_m, 4)
            for i in range(2):
                a, b = 512 * i, 512 * i + 512
                link(nc.vector.tensor_copy(s[0][:, a:b], ps[2 + i][:]))
                link(nc.vector.tensor_tensor(K["dec"][:, a:b], ps[4 + i][:], s[0][:, a:b], ALU.subtract))
            dt3 = K["dtot"][:].rearrange("p (c r) -> p c r", r=NP)
            for i in range(2):
                for j in range(2):
                    q = slice(64 * j, 64 * j + 64)
                    link(nc.vector.tensor_copy(dt3[q, 16 * i:16 * i + 16, :],
                                               ps[4 + i][q, :].rearrange("p (c r j) -> p c r j", r=NP, j=2)[:, :, :, j]))
            c0 = s[0][:].rearrange("p (c h) -> p c h", h=H)
            for i in range(3):
                part = cum3[:, :, H * i:H * i + H]
                link(nc.vector.tensor_copy(part, c0))
                if i < 2:
                    link(nc.vector.tensor_tensor(c0, c0, part, ALU.subtract))
            dve.sem_inc(v_m, 1)
            dve.wait_ge(pe_m, 5)
            for i in range(2):
                a, b = 512 * i, 512 * i + 512
                link(nc.vector.tensor_tensor(K["kk"][:, a:b], K["kk"][:, a:b], ps[i][:], ALU.add))
                link(nc.vector.tensor_tensor(s[3][:, a:b], s[3][:, a:b], ps[i][:], ALU.mult))
            cc3 = K["cc"][:].rearrange("p (c h) -> p c h", h=H)
            link(nc.vector.tensor_tensor(cc3, one_h(2), v3[3], ALU.subtract))
            for g in range(4):
                dve.wait_ge(pe_m, 6 + g)
                nc.vector.tensor_copy(K["cumT"][0:3 * H, 1024 * g:1024 * g + 1024],
                                      ps_bf[g % 2][0:3 * H].rearrange("p c t -> p (c t)")).then_inc(v_m, 1)

        @block.scalar
        def _(act):
            n = [0]

            def link(ins):
                n[0] += 1
                ins.then_inc(ach, 1)
                act.wait_ge(ach, n[0])

            for i in range(BATCH):
                act.wait_ge(centred, i + 1)
                nc.scalar.activation(xnT[:, i * L:(i + 1) * L], big[:, i * L:(i + 1) * L], ACT.Square).then_inc(squared, 1)
            for g in range(1, NG, 2):
                act.wait_ge(w_t, g + 1)
                b = ps[g % 4]
                if g == 9:
                    nc.scalar.mul(K["w_th"][:, 0:512], b[:], TURN).then_inc(w_a, 1)
                elif g in (11, 13):
                    act.wait_ge(w_v, 5)
                    a0 = 4 * (g - 11)
                    for i in range(4):
                        link(nc.scalar.activation(K["w_o"][:, (a0 + i) * P:(a0 + i + 1) * P], b[:, i * P:i * P + P],
                                                  ACT.Copy, scale=K["prmT"][:, a0 + i:a0 + i + 1]))
                    act.sem_inc(w_a, 1)
                else:
                    weight_out(g, nc.scalar.copy)[0].then_inc(w_a, 1)
                if g == 1:
                    act.wait_ge(for_act, 1)
                    nc.scalar.activation(st32[:, 2, 0:NC], st32[:, 1, 0:NC], ACT.Sqrt).then_inc(a_m, 1)
            for g in range(1, 8, 2):
                act.wait_ge(w_t, NG + g + 1)
                nc.scalar.copy(xnT[:, 512 * g:512 * g + 512], ps[g % 4][:]).then_inc(w_a, 1)
            for g in range(12):
                act.wait_ge(w_t, NG + 8 + g + 1)
                if g < 8:
                    nc.scalar.activation(tmp[:, 512 * g:512 * g + 512], ps[g % 4][:], ACT.Square).then_inc(w_a, 1)
                elif g % 2 == 1:
                    nc.scalar.copy(dl[:, 512 * (g - 8):512 * (g - 7)], ps[g % 4][:]).then_inc(w_a, 1)
                if g == 9:
                    act.wait_ge(for_act, 2)
                    nc.scalar.activation(st32[:, 2, :], st32[:, 1, :], ACT.Sqrt).then_inc(a_m, 1)
            for g in range(1, 8, 2):
                act.wait_ge(w_t, NG + 20 + g + 1)
                nc.scalar.activation(tmp[:, 512 * g:512 * g + 512], ps[g % 4][:], ACT.Copy, scale=wnc[:, 0:1]).then_inc(w_a, 1)
            act.wait_ge(for_act, 3)
            link(nc.scalar.activation(rowb[:, H:2 * H], rowb[:, H:2 * H], ACT.Exp))
            link(nc.scalar.activation(s[3][:].rearrange("p (c h) -> p c h", h=H),
                                      dl[:].rearrange("p (c k) -> p c k", k=2 * H)[:, :, H:2 * H], ACT.Exp, scale=-1.0))
            nc.scalar.activation(s[1][:], s[1][:], ACT.Exp).then_inc(a_m, 1)
            act.wait_ge(for_act, 4)
            link(nc.scalar.activation(K["kk"][:], s[2][:], ACT.Ln))
            act.wait_ge(for_act, 5)
            nc.scalar.activation(s[2][:], K["kk"][:], ACT.Exp, scale=-1.0).then_inc(a_m, 1)
            act.wait_ge(v_m, 8)
            link(nc.scalar.activation(K["dec"][:], K["dec"][:], ACT.Exp))
            link(nc.scalar.activation(K["dtot"][:], K["dtot"][:], ACT.Exp))


def units(nc, K, scratch, cum_stored):
    xn_d, tc_d, bc_d, cum_d = scratch
    with ExitStack() as ctx:
        def sb(name, shape, dt=F32):
            return ctx.enter_context(nc.sbuf_tensor(name, shape, dt))

        def sem(name):
            return ctx.enter_context(nc.semaphore(name))

        def bank(name):
            return ctx.enter_context(nc.psum_tensor(name, [P, 512], F32))

        R = [bank("r0"), bank("r1")]
        Dp = bank("d")
        Op = bank("o")
        Sp = [bank("s0"), bank("s1")]
        Yp = [bank("y0"), bank("y1")]

        BC_LOADS = 16 * 6
        DUP = 16 * 4
        xnz = sb("xnz", [P, ST])
        xns = sb("xns", [P, ST])
        tcs = sb("tcs", [P, ST])
        bcs = sb("bcs", [P, 4, ST])
        rnd = sb("rnd", [P, ST])
        ang = sb("ang", [P, ST])
        tri = sb("tri", [P, 3, ST])
        trig = sb("trig", [P, 2, 2, ST])
        part = sb("part", [P, 4, ST])
        rot = sb("rot", [P, 2, 2, 2, ST])
        eb = sb("eb", [P, 2, ST])
        ce = sb("ce", [P, 2, ST])
        xk = sb("xk", [P, 2, CS, 4 * HD])
        xc = sb("xc", [P, 2, CS, 4 * HD])
        E = sb("E", [P, 2, ST])
        M = sb("M", [P, 4, ST])
        bw = sb("bw", [P, 2, CS, P])
        hs = sb("hs", [P, CS, 2, HD])
        th = sb("th", [P, 2, ST])
        yT = sb("yT", [P, 2, ST])
        sq = sb("sq", [P, 2, ST])
        sqa = sb("sqa", [P, ST])

        tc_loaded, xn_loaded, bc_loaded, z_loaded = sem("tc_loaded"), sem("xn_loaded"), sem("bc_loaded"), sem("z_loaded")
        cum_loaded = sem("cum_loaded")
        dup = [sem("dup0"), sem("dup1")]
        u_ready, bt_ready, x_ready, eb_ready = sem("u_ready"), sem("bt_ready"), sem("x_ready"), sem("eb_ready")
        st_ready, z_ready, out_ready, ssq_ready = sem("st_ready"), sem("z_ready"), sem("out_ready"), sem("ssq_ready")
        d_ready, s_ready, y_ready = sem("d_ready"), sem("s_ready"), sem("y_ready")
        e_ready, m_ready = sem("e_ready"), sem("m_ready")
        rounded, turned, absd = sem("rounded"), sem("turned"), sem("absd")
        sin_ready = sem("sin_ready")
        part_ready, rot_ready = sem("part_ready"), sem("rot_ready")
        ebs_ready, ce_ready = sem("ebs_ready"), sem("ce_ready")
        xk_ready, bw_ready = sem("xk_ready"), sem("bw_ready")
        th_ready, sz_ready, yt_ready, sq_ready = sem("th_ready"), sem("sz_ready"), sem("yt_ready"), sem("sq_ready")
        sqa_ready = sem("sqa_ready")
        hch = sem("hch")
        acc_done, ssq_taken = sem("acc_done"), sem("ssq_taken")
        mags_done = sem("mags_done")
        block = ctx.enter_context(nc.Block())

        def at(per, t, k):
            return t * per + max(k, 0) + 1

        T1, T2, T3, T4, T8 = NQ, 2 * NQ, 3 * NQ, 4 * NQ, 8 * NQ

        @block.sync
        def _(sp):
            def load_cum(t):
                sp.dma_start(K["pick"][3 * H:3 * (H + CS), :], cum_d[t].rearrange("c i h s -> (c i) (h s)")).then_inc(cum_loaded, 16)

            def load_bc(t):
                src = bc_d[t].rearrange("(i n) t -> n i t", i=2)
                for j in range(2):
                    sp.dma_start(bcs[64 * j:64 * j + 64, 0:4:2, :], src).then_inc(bc_loaded, 16)
                    for f in range(2):
                        r = 64 * j + 32 * f
                        sp.dma_start(bcs[r:r + 32, 1:4:2, :], src[32 * (1 - f):32 * (2 - f)]).then_inc(bc_loaded, 16)

            def spread(t, q):
                sp.wait_ge(sin_ready, at(T3, t, 3 * q + 3))
                for p in range(2):
                    for j in range(2):
                        h = 2 * p + j
                        for d in range(2):
                            r = 64 * j + 32 * d
                            sp.dma_start(trig[r:r + 32, p, :, :],
                                         tri[32 * h:32 * h + 32, d:3:2 - d, :]).then_inc(dup[p], 16)

            sp.dma_start(tcs[:], tc_d[0]).then_inc(tc_loaded, 16)
            sp.dma_start(xns[:], xn_d[0]).then_inc(xn_loaded, 16)
            load_bc(0)
            sp.dma_start(xnz[:], xn_d[0]).then_inc(z_loaded, 16)
            sp.wait_ge(cum_stored, 48)
            load_cum(0)
            spread(0, 0)
            spread(0, 1)
            with sp.Fori(0, NS) as t:
                tn = (t + 1) % NS
                for q in range(NQ):
                    if q == NQ - 3:
                        sp.wait_ge(u_ready, at(T1, t, T1))
                        sp.dma_start(tcs[:], tc_d[tn]).then_inc(tc_loaded, 16)
                    if q == NQ - 2:
                        sp.wait_ge(x_ready, at(T2, t, T2))
                        sp.dma_start(xns[:], xn_d[tn]).then_inc(xn_loaded, 16)
                        sp.wait_ge(part_ready, at(T8, t, T8))
                        load_bc(tn)
                    if q == NQ - 1:
                        sp.wait_ge(d_ready, at(T4, t, T4))
                        load_cum(tn)
                    spread(t, q + 2)
                sp.wait_ge(z_ready, at(T2, t, T2))
                sp.dma_start(xnz[:], xn_d[tn]).then_inc(z_loaded, 16)
            sp.wait_ge(tc_loaded, 16 * (NS + 1))
            sp.wait_ge(xn_loaded, 16 * (NS + 1))
            sp.wait_ge(cum_loaded, 16 * (NS + 1))
            sp.wait_ge(bc_loaded, BC_LOADS * (NS + 1))
            sp.wait_ge(z_loaded, 16 * (NS + 1))
            for p in range(2):
                sp.wait_ge(dup[p], DUP * (NS * NQ + 2))


        @block.tensor
        def _(pe):
            for s in (u_ready, bt_ready, x_ready, eb_ready, st_ready, z_ready, out_ready, ssq_ready, d_ready, s_ready, y_ready):
                pe.sem_inc(s, 1)

            def angles(q):
                w = K["w_th"][:, (q % NQ) * P:(q % NQ + 1) * P]
                nc.tensor.matmul(R[0][:], w, tcs[:], start=True, stop=True).then_inc(u_ready, 1)

            def x_by_token(q, i):
                for c in range(2):
                    last = nc.tensor.matmul(R[i][:, 256 * c:256 * c + 256], xns[:, (2 * i + c) * P:(2 * i + c + 1) * P],
                                            K["w_zx"][:, DI + q * 256:DI + q * 256 + 256], start=True, stop=True)
                last.then_inc(x_ready, 1)

            def b_by_token(q, p):
                for c in range(CS):
                    last = nc.tensor.transpose(R[p][:, c * P:c * P + P], rot[:, q % 2, p, 0, c * P:c * P + P], K["ident"][:])
                last.then_inc(bt_ready, 1)

            def exponents(t, q, tt, h):
                pe.wait_ge(ebs_ready, at(T2, t, 2 * q))
                pe.wait_ge(e_ready, at(T4, t, 4 * q + h))
                head = 4 * (q % NQ) + h
                nc.tensor.matmul(Dp[:], K["ident_bf"][:], K["mask"][:], start=True, stop=False, skip_group_check=True)
                nc.tensor.matmul(Dp[:], K["pick"][:, head * P:head * P + P], K["cumT"][:, bass.ds(tt * ST, ST)],
                                 start=False, stop=True, skip_group_check=True).then_inc(d_ready, 1)

            def row_exponents(t, q, p):
                pe.wait_ge(e_ready, at(T4, t, 4 * q + 4))
                pe.wait_ge(ebs_ready, at(T2, t, 2 * q + p))
                first = (4 * q + 2 * p) * P + HD
                nc.tensor.matmul(Dp[:], K["pick"][0:3 * H, first:first + P],
                                 K["cumT"][0:3 * H, bass.ds(t * ST, ST)], start=True, stop=True).then_inc(eb_ready, 1)

            def scores(t, q, h):
                p, rows = h // 2, slice(64 * (h % 2), 64 * (h % 2) + 64)
                pe.wait_ge(m_ready, at(T4, t, 4 * q + h - 1))
                for c in range(CS):
                    k = slice(c * P, c * P + P)
                    last = nc.tensor.matmul(Sp[h % 2][:, k], rot[rows, q % 2, p, 0, k], rot[rows, q % 2, p, 1, k],
                                            start=True, stop=True)
                last.then_inc(s_ready, 1)

            def project(t, q, chunks):
                if q == 0 and chunks[0] == 0:
                    pe.wait_ge(acc_done, at(1, t, 0))
                    nc.tensor.matmul(Op[:], K["zeros_bf"][:], K["mask"][:], start=True, stop=False, skip_group_check=True)
                pe.wait_ge(yt_ready, at(T2, t, 2 * q + 2))
                for c in chunks:
                    k = slice(c * P, c * P + P)
                    for p in range(2):
                        last = nc.tensor.matmul(Op[:, k], yT[:, p, k], K["w_o"][:, (2 * q + p) * P:(2 * q + p + 1) * P],
                                                start=False, stop=q == NQ - 1 and c == CS - 1 and p == 1,
                                                skip_group_check=True)
                if chunks[-1] == CS - 1:
                    last.then_inc(out_ready, 1)

            pe.wait_ge(tc_loaded, 16)
            angles(0)
            pe.wait_ge(turned, at(T1, 0, 1))
            angles(1)
            pe.wait_ge(xn_loaded, 16)
            pe.wait_ge(turned, at(T1, 0, 2))
            for i in range(2):
                x_by_token(0, i)
            pe.wait_ge(rot_ready, at(T4, 0, 4))
            for p in range(2):
                pe.wait_ge(xk_ready, at(T2, 0, p + 1))
                b_by_token(0, p)
            pe.wait_ge(cum_loaded, 16)
            for h in range(2):
                exponents(0, 0, 0, h)
                scores(0, 0, h)
            with pe.Fori(0, NS) as t:
                for q in range(NQ):
                    par = q % 2
                    tn = t if q < NQ - 1 else (t + 1) % NS
                    if q == NQ - 2:
                        pe.wait_ge(tc_loaded, (t + 2) * 16)
                    pe.wait_ge(bw_ready, at(T2, t, 2 * q + 1))
                    angles(q + 2)
                    if q == 0:
                        pe.wait_ge(ssq_taken, at(1, t, 0))
                    pe.wait_ge(bw_ready, at(T2, t, 2 * q + 2))
                    for c in range(CS):
                        for p in range(2):
                            for j in range(2):
                                last = nc.tensor.matmul(R[1][64 * j:64 * j + 64, (2 * c + p) * 64:(2 * c + p) * 64 + 64],
                                                        bw[:, p, c, 64 * j:64 * j + 64],
                                                        xk[:, par, c, (2 * p + j) * 64:(2 * p + j) * 64 + 64],
                                                        start=True, stop=True)
                    last.then_inc(st_ready, 1)
                    for h in (2, 3):
                        exponents(t, q, t, h)
                        scores(t, q, h)
                    row_exponents(t, q, 0)
                    if q == NQ - 2:
                        pe.wait_ge(mags_done, at(2, t, 2))
                    if q == NQ - 1:
                        pe.wait_ge(xn_loaded, (t + 2) * 16)
                    pe.wait_ge(turned, at(T1, t, q + 3))
                    x_by_token((q + 1) % NQ, 0)
                    row_exponents(t, q, 1)
                    if q > 0:
                        project(t, q - 1, (0, 1))
                    pe.wait_ge(hch, at(9 * NQ, t, 9 * q + 9))
                    x_by_token((q + 1) % NQ, 1)
                    if q > 0:
                        project(t, q - 1, (2, 3))
                    if q == 0:
                        pe.wait_ge(z_loaded, (t + 1) * 16)
                    for p in range(2):
                        pe.wait_ge(xk_ready, at(T2, t, 2 * q + 2 + p + 1))
                        w = K["w_zx"][:, (2 * q + p) * P:(2 * q + p + 1) * P]
                        nc.tensor.matmul(R[p][:], w, xnz[:], start=True, stop=True).then_inc(z_ready, 1)
                    for p in range(2):
                        pe.wait_ge(m_ready, at(T4, t, 4 * q + 2 * p + 2))
                        pe.wait_ge(ce_ready, at(T2, t, 2 * q + p + 1))
                        pe.wait_ge(yt_ready, at(T2, t, 2 * q - 1 + p))
                        for c in range(CS):
                            k = slice(c * P, c * P + P)
                            nc.tensor.matmul(Yp[p][:, k], xc[:, par, c, 128 * p:128 * p + 128], K["ident"][:],
                                             start=True, stop=False, is_transpose=True, skip_group_check=True)
                            for j in range(2):
                                nc.tensor.matmul(Yp[p][64 * j:64 * j + 64, k],
                                                 xk[:, par, c, (2 * p + j) * 64:(2 * p + j) * 64 + 64], M[:, 2 * p + j, k],
                                                 start=False, stop=False, skip_group_check=True)
                            for j in range(2):
                                rows = slice(64 * j, 64 * j + 64)
                                last = nc.tensor.matmul(Yp[p][rows, k], hs[rows, c, p, :], ce[rows, p, k],
                                                        start=False, stop=True, skip_group_check=True)
                        last.then_inc(y_ready, 1)
                    pe.wait_ge(rot_ready, at(T4, t, 4 * q + 8))
                    for p in range(2):
                        pe.wait_ge(sz_ready, at(T2, t, 2 * q + p + 1))
                        b_by_token(q + 1, p)
                    if q == NQ - 1:
                        pe.wait_ge(cum_loaded, (t + 2) * 16)
                    for h in range(2):
                        exponents(t, q + 1, tn, h)
                        scores(t, q + 1, h)
                project(t, NQ - 1, range(CS))
                pe.wait_ge(sqa_ready, at(T2, t, T2))
                pe.wait_ge(e_ready, at(T4, t, T4 + 2))
                for c in range(CS):
                    last = nc.tensor.matmul(Dp[:, c:c + 1], sqa[:, c * P:c * P + P], K["ones"][:, 0:1],
                                            start=True, stop=True)
                last.then_inc(ssq_ready, 1)

        @block.vector
        def _(dve):
            for s in (turned, bw_ready, m_ready, xk_ready, hch, part_ready, sz_ready, yt_ready, mags_done):
                dve.sem_inc(s, 1)

            def angles(t, q):
                dve.wait_ge(rounded, at(T1, t, q + 1))
                dve.wait_ge(sin_ready, at(T3, t, 3 * q))
                nc.vector.scalar_tensor_tensor(out=ang[:], in0=rnd[:], scalar=MAGIC, in1=R[0][:],
                                               op0=ALU.subtract, op1=ALU.subtract).then_inc(turned, 1)

            def x_scaled(t, q, tt, i):
                dve.wait_ge(x_ready, at(T2, t, 2 * q + i + 1))
                dve.wait_ge(y_ready, at(T2, t, 2 * q - 2))
                for dst, f in ((xk, "kk"), (xc, "cc")):
                    v = K[f][:, bass.ds(tt * (CS * H) + 2 * i * H, 2 * H)].rearrange("p (c h) -> p c h", h=H)
                    v = v[:, :, 4 * (q % NQ):4 * (q % NQ) + 4].unsqueeze(3)
                    last = nc.vector.tensor_tensor(dst[:, q % 2, 2 * i:2 * i + 2, :].rearrange("p c (h d) -> p c h d", h=4),
                                                   R[i][:].rearrange("p (c h d) -> p c h d", c=2, h=4),
                                                   bcast(v, [P, 2, 4, HD]), ALU.mult)
                last.then_inc(xk_ready, 1)

            def rotation(t, q, p, w, f):
                pair = (q % NQ) * 2 + p
                col = K["prmT"][:, 16 * (1 + 2 * w + f) + pair:16 * (1 + 2 * w + f) + pair + 1]
                if w == 0 and f == 0:
                    dve.wait_ge(dup[p], t * (DUP * NQ) + DUP * (q + 1))
                    if q % NQ == 0 and p == 0:
                        dve.wait_ge(bc_loaded, (t + (q // NQ + 1)) * BC_LOADS)
                if f == 0:
                    dve.wait_ge(rot_ready, at(T4, t, 4 * q + 2 * p + w - 1))
                nc.vector.scalar_tensor_tensor(out=part[:, 2 * w + f, :], in0=bcs[:, 2 * w + f, :], scalar=col,
                                               in1=trig[:, p, 1 - f, :], op0=ALU.add, op1=ALU.mult).then_inc(part_ready, 1)

            def b_decayed(t, q, tt):
                dve.wait_ge(st_ready, at(T1, t, q))
                for p in range(2):
                    dve.wait_ge(bt_ready, at(T2, t, 2 * q + p + 1))
                    v = K["dec"][:, bass.ds(tt * (CS * H), CS * H)].rearrange("p (c h) -> p c h", h=H)
                    v = v[:, :, 4 * (q % NQ) + 2 * p:4 * (q % NQ) + 2 * p + 2].unsqueeze(3)
                    nc.vector.tensor_tensor(bw[:, p, :, :].rearrange("p c (j n) -> p c j n", j=2),
                                            R[p][:].rearrange("p (c j n) -> p c j n", c=CS, j=2),
                                            bcast(v, [P, CS, 2, N]), ALU.mult).then_inc(bw_ready, 1)

            def scores(t, q, h):
                dve.wait_ge(e_ready, at(T4, t, 4 * q + h + 1))
                dve.wait_ge(s_ready, at(T4, t, 4 * q + h + 1))
                dve.wait_ge(y_ready, at(T2, t, 2 * q - 1 + h // 2))
                nc.vector.tensor_tensor(M[:, h, :], Sp[h % 2][:], E[:, h % 2, :], ALU.mult).then_inc(m_ready, 1)

            angles(0, 0)
            angles(0, 1)
            x_scaled(0, 0, 0, 0)
            x_scaled(0, 0, 0, 1)
            for p in range(2):
                for w in range(2):
                    for f in range(2):
                        rotation(0, 0, p, w, f)
            b_decayed(0, 0, 0)
            scores(0, 0, 0)
            scores(0, 0, 1)
            with dve.Fori(0, NS) as t:
                def state(q, c):
                    dve.wait_ge(hch, at(9 * NQ, t, 9 * q + 1 + 2 * c))
                    for p in range(2):
                        dst = hs[:, c + 1, p, :] if c < CS - 1 else K["carry"][:, 2 * q + p, :]
                        nc.vector.scalar_tensor_tensor(
                            out=dst, in0=hs[:, c, p, :], scalar=K["dtot"][:, bass.ds(t * (CS * NP) + c * NP + 2 * q + p, 1)],
                            in1=R[1][:, (2 * c + p) * 64:(2 * c + p) * 64 + 64], op0=ALU.mult, op1=ALU.add).then_inc(hch, 1)

                for q in range(NQ):
                    tn = t if q < NQ - 1 else (t + 1) % NS
                    dve.wait_ge(y_ready, at(T2, t, 2 * q))
                    dve.wait_ge(hch, at(9 * NQ, t, 9 * q))
                    nc.vector.tensor_scalar(hs[:, 0, :, :], K["carry"][:, 2 * q:2 * q + 2, :], K["goes_on"][:, bass.ds(t, 1)],
                                            None, ALU.mult).then_inc(hch, 1)
                    rotation(t, q + 1, 0, 0, 0)
                    rotation(t, q + 1, 0, 0, 1)
                    angles(t, q + 2)
                    dve.wait_ge(st_ready, at(T1, t, q + 1))
                    state(q, 0)
                    rotation(t, q + 1, 0, 1, 0)
                    state(q, 1)
                    scores(t, q, 2)
                    state(q, 2)
                    rotation(t, q + 1, 0, 1, 1)
                    state(q, 3)
                    x_scaled(t, q + 1, tn, 0)
                    x_scaled(t, q + 1, tn, 1)
                    scores(t, q, 3)
                    rotation(t, q + 1, 1, 0, 0)
                    rotation(t, q + 1, 1, 0, 1)
                    rotation(t, q + 1, 1, 1, 0)
                    rotation(t, q + 1, 1, 1, 1)
                    for p in range(2):
                        dve.wait_ge(th_ready, at(T2, t, 2 * q + p + 1))
                        nc.vector.scalar_tensor_tensor(out=th[:, p, :], in0=th[:, p, :], scalar=1.0, in1=R[p][:],
                                                       op0=ALU.add, op1=ALU.mult).then_inc(sz_ready, 1)
                    for p in range(2):
                        dve.wait_ge(sz_ready, at(T2, t, 2 * q + p + 1))
                        dve.wait_ge(y_ready, at(T2, t, 2 * q + p + 1))
                        dve.wait_ge(out_ready, at(T1, t, q))
                        dve.wait_ge(sq_ready, at(T2, t, 2 * q))
                        nc.vector.tensor_tensor(yT[:, p, :], Yp[p][:], th[:, p, :], ALU.mult).then_inc(yt_ready, 1)
                    b_decayed(t, q + 1, tn)
                    if q == 2:
                        dve.wait_ge(xn_loaded, (t + 1) * 16)
                        for i, op in enumerate((ALU.max, ALU.min)):
                            nc.vector.tensor_reduce(K["mags"][:, bass.ds(t * 2 + i, 1)], xns[:], AX.X, op).then_inc(mags_done, 1)
                    scores(t, q + 1, 0)
                    scores(t, q + 1, 1)

        @block.scalar
        def _(act):
            for s in (rounded, sin_ready, absd, e_ready, ebs_ready, th_ready, sq_ready, acc_done, ssq_taken):
                act.sem_inc(s, 1)

            def rounding(t, q):
                act.wait_ge(u_ready, at(T1, t, q + 1))
                act.wait_ge(sin_ready, at(T3, t, 3 * q))
                nc.scalar.activation(rnd[:], R[0][:], ACT.Identity, bias=K["cols"][:, 1:2]).then_inc(rounded, 1)

            def sines(t, q, first=False):
                act.wait_ge(turned, at(T1, t, q + 1))
                nc.scalar.activation(rnd[:], ang[:], ACT.Abs).then_inc(absd, 1)
                if not first:
                    for p in range(2):
                        act.wait_ge(dup[p], t * (DUP * NQ) + DUP * q)
                nc.scalar.activation(tri[:, 0, :], ang[:], ACT.Sin, scale=TWO_PI).then_inc(sin_ready, 1)
                nc.scalar.activation(tri[:, 1, :], ang[:], ACT.Sin, scale=-TWO_PI).then_inc(sin_ready, 1)
                act.wait_ge(absd, at(T1, t, q + 1))
                act.wait_ge(part_ready, at(T8, t, 8 * q))
                nc.scalar.activation(tri[:, 2, :], rnd[:], ACT.Sin, scale=-TWO_PI, bias=K["cols"][:, 0:1]).then_inc(sin_ready, 1)

            def decays(t, q, h):
                act.wait_ge(d_ready, at(T4, t, 4 * q + h + 1))
                act.wait_ge(m_ready, at(T4, t, 4 * q + h - 1))
                nc.scalar.activation(E[:, h % 2, :], Dp[:], ACT.Exp).then_inc(e_ready, 1)

            def squares(t, q, p):
                act.wait_ge(yt_ready, at(T2, t, 2 * q + p + 1))
                act.wait_ge(sqa_ready, at(T2, t, 2 * q - 1 + p))
                nc.scalar.activation(sq[:, p, :], yT[:, p, :], ACT.Square).then_inc(sq_ready, 1)

            rounding(0, 0)
            sines(0, 0, first=True)
            rounding(0, 1)
            sines(0, 1)
            decays(0, 0, 0)
            decays(0, 0, 1)
            with act.Fori(0, NS) as t:
                for q in range(NQ):
                    rounding(t, q + 2)
                    decays(t, q, 2)
                    decays(t, q, 3)
                    for p in range(2):
                        act.wait_ge(eb_ready, at(T2, t, 2 * q + p + 1))
                        act.wait_ge(ce_ready, at(T2, t, 2 * q - 1 + p))
                        nc.scalar.activation(eb[:, p, :], Dp[:], ACT.Exp).then_inc(ebs_ready, 1)
                    for p in range(2):
                        act.wait_ge(z_ready, at(T2, t, 2 * q + p + 1))
                        act.wait_ge(yt_ready, at(T2, t, 2 * q - 1 + p))
                        nc.scalar.activation(th[:, p, :], R[p][:], ACT.Tanh, scale=0.5).then_inc(th_ready, 1)
                    sines(t, q + 2)
                    squares(t, q, 0)
                    decays(t, q + 1, 0)
                    squares(t, q, 1)
                    decays(t, q + 1, 1)
                act.wait_ge(out_ready, at(T1, t, T1))
                nc.scalar.copy(K["s_acc"][:, bass.ds(t * ST, ST)], Op[:]).then_inc(acc_done, 1)
                act.wait_ge(ssq_ready, at(1, t, 1))
                nc.scalar.copy(K["ssq"][:, bass.ds(t * CS, CS)], Dp[:, 0:CS]).then_inc(ssq_taken, 1)

        @block.gpsimd
        def _(pool):
            for s in (rot_ready, ce_ready, sqa_ready):
                pool.sem_inc(s, 1)

            def sums(t, q, p):
                for w in range(2):
                    pool.wait_ge(part_ready, at(T8, t, 8 * q + 4 * p + 2 * w + 2))
                    pool.wait_ge(y_ready, at(T2, t, 2 * q - 2))
                    nc.gpsimd.tensor_tensor(rot[:, q % 2, p, w, :], part[:, 2 * w, :], part[:, 2 * w + 1, :],
                                            ALU.add).then_inc(rot_ready, 1)

            def c_decayed(t, q):
                for p in range(2):
                    pool.wait_ge(ebs_ready, at(T2, t, 2 * q + p + 1))
                    pool.wait_ge(rot_ready, at(T4, t, 4 * q + 4))
                    pool.wait_ge(y_ready, at(T2, t, 2 * q - 1 + p))
                    nc.gpsimd.tensor_tensor(ce[:, p, :], rot[:, q % 2, p, 1, :], eb[:, p, :], ALU.mult).then_inc(ce_ready, 1)

            sums(0, 0, 0)
            sums(0, 0, 1)
            with pool.Fori(0, NS) as t:
                pool.wait_ge(ssq_ready, at(1, t, 0))
                for q in range(NQ):
                    sums(t, q + 1, 0)
                    c_decayed(t, q)
                    sums(t, q + 1, 1)
                    if q == 0:
                        pool.wait_ge(sq_ready, at(T2, t, 2))
                        nc.gpsimd.tensor_tensor(sqa[:], sq[:, 0, :], sq[:, 1, :], ALU.add).then_inc(sqa_ready, 1)
                        pool.wait_ge(sqa_ready, at(T2, t, 1))
                        pool.sem_inc(sqa_ready, 1)
                        continue
                    for p in range(2):
                        pool.wait_ge(sq_ready, at(T2, t, 2 * q + p + 1))
                        pool.wait_ge(sqa_ready, at(T2, t, 2 * q + p))
                        nc.gpsimd.tensor_tensor(sqa[:], sqa[:], sq[:, p, :], ALU.add).then_inc(sqa_ready, 1)


def finish(nc, K, u, xn_d, out):
    with ExitStack() as ctx:
        def sb(name, shape, dt=F32):
            return ctx.enter_context(nc.sbuf_tensor(name, shape, dt))

        def sem(name):
            return ctx.enter_context(nc.semaphore(name))

        ps = [ctx.enter_context(nc.psum_tensor(f"f_ps{i}", [P, 512], F32)) for i in range(2)]
        AHEAD = 4
        xn = sb("f_xn", [P, AHEAD, ST])
        xin = sb("f_xin", [P, AHEAD, ST])
        v = sb("f_v", [P, 2, ST])
        mag = sb("f_mag", [P, 2, ST])
        half = sb("f_half", [P, ST], FP8)
        small = sb("f_small", [P, ST])
        wv = sb("f_wv", [P, 2, P])
        xq = sb("f_xq", [P, 2, ST], BF16)
        wq = sb("f_wq", [P, P], BF16)
        gate = sb("f_gate", [P, 2, ST])
        th = sb("f_th", [P, 2, ST])
        sr = sb("f_sr", [P, 2, ST])
        o = sb("f_o", [P, 2, ST])
        sc = sb("f_sc", [P, 6])
        r = sb("f_r", [P, 4, NC])
        am = sb("f_am", [P, 2])
        am2 = sb("f_am2", [2, 3])
        am_ready, am_out = sem("f_am_ready"), sem("f_am_out")
        loaded = [sem(f"f_loaded{i}") for i in range(AHEAD)]
        stored = [sem("f_st0"), sem("f_st1")]
        chain, for_act, root_done = sem("f_chain"), sem("f_for_act"), sem("f_root_done")
        scales_done = sem("f_scales")
        scaled = sem("f_scaled")
        xq_ready, g_ready, gate_done, th_done = sem("f_xq"), sem("f_g"), sem("f_gate_done"), sem("f_th_done")
        sr_done, prod_done, o_ready = sem("f_sr_done"), sem("f_prod_done"), sem("f_o_ready")
        block = ctx.enter_context(nc.Block())
        u_v = u.rearrange("b (s c p) m -> (b s) p c m", c=CS, p=P)
        o_v = out.rearrange("b (s c p) m -> (b s) p c m", c=CS, p=P)
        v4 = lambda a: a.rearrange("p (c m) -> p c m", c=CS)

        @block.sync
        def _(sp):
            def store(t):
                sp.wait_ge(o_ready, t + 1)
                sp.dma_start(o_v[t], v4(o[:, t % 2, :])).then_inc(stored[t % 2], 16)

            for t in range(NS):
                if t >= AHEAD:
                    sp.wait_ge(o_ready, t - AHEAD + 1)
                sp.dma_start(xn[:, t % AHEAD, :], xn_d[t]).then_inc(loaded[t % AHEAD], 16)
                sp.dma_start(v4(xin[:, t % AHEAD, :]), u_v[t]).then_inc(loaded[t % AHEAD], 16)
                if t >= AHEAD - 1:
                    store(t - AHEAD + 1)
            for t in range(NS - AHEAD + 1, NS):
                store(t)
            for i in range(2):
                sp.wait_ge(stored[i], 16 * (NS // 2))

        @block.tensor
        def _(pe):
            pe.wait_ge(am_ready, 1)
            nc.tensor.transpose(ps[0][0:2, 0:P], am[:], K["ident"][:]).then_inc(am_out, 1)
            pe.wait_ge(am_ready, 2)
            nc.tensor.matmul(ps[1][:, 0:2], K["ones"][0:2, 0:P], am2[:, 0:2], start=True, stop=True).then_inc(am_out, 1)
            for t in range(NS):
                pe.wait_ge(xq_ready, t + 2)
                if t >= 2:
                    pe.wait_ge(gate_done, t - 1)
                for c in range(CS):
                    last = nc.tensor.matmul(ps[t % 2][:, c * P:c * P + P], xq[:, t % 2, c * P:c * P + P], wq[:], start=True, stop=True)
                last.then_inc(g_ready, 1)

        @block.scalar
        def _(act):
            act.wait_ge(for_act, 1)
            nc.scalar.activation(r[:, 1, :], r[:, 0, :], ACT.Sqrt).then_inc(root_done, 1)
            act.wait_ge(scales_done, 1)
            nc.scalar.activation(wv[:, 0, :], K["w_ffn"][:], ACT.Copy, scale=sc[:, 1:2]).then_inc(scaled, 1)
            nc.scalar.activation(wv[:, 1, :], K["w_ffn"][:], ACT.Abs, scale=sc[:, 1:2]).then_inc(scaled, 1)
            for t in range(NS + 2):
                if t < NS:
                    act.wait_ge(loaded[t % AHEAD], 32 * (t // AHEAD + 1))
                    if t >= 2:
                        act.wait_ge(xq_ready, t)
                    nc.scalar.activation(v[:, t % 2, :], xn[:, t % AHEAD, :], ACT.Copy, scale=sc[:, 0:1]).then_inc(scaled, 1)
                    nc.scalar.activation(mag[:, t % 2, :], xn[:, t % AHEAD, :], ACT.Abs, scale=sc[:, 0:1]).then_inc(scaled, 1)
                if t >= 2:
                    act.wait_ge(gate_done, t - 1)
                    if t >= 4:
                        act.wait_ge(prod_done, t - 3)
                    nc.scalar.activation(th[:, t % 2, :], gate[:, t % 2, :], ACT.Tanh, scale=0.5).then_inc(th_done, 1)

        @block.vector
        def _(dve):
            n = [0]

            def link(ins):
                n[0] += 1
                ins.then_inc(chain, 1)
                dve.wait_ge(chain, n[0])

            link(nc.vector.tensor_scalar(r[:, 0, :], K["ssq"][:], 0.25 / DI, EPS, ALU.mult, ALU.add))
            dve.sem_inc(for_act, 1)
            mx = K["mags"][:].rearrange("p (t i) -> p i t", i=2)
            link(nc.vector.tensor_scalar(mx[:, 1, :], mx[:, 1, :], -1.0, None, ALU.mult))
            link(nc.vector.tensor_tensor(mx[:, 0, :], mx[:, 0, :], mx[:, 1, :], ALU.max))
            link(nc.vector.tensor_reduce(am[:, 0:1], mx[:, 0, 0:NS], AX.X, ALU.max))
            link(nc.vector.tensor_copy(am[:, 1:2], mx[:, 0, NS:NS + 1]))
            dve.sem_inc(am_ready, 1)
            dve.wait_ge(am_out, 1)
            link(nc.vector.tensor_reduce(am2[:, 2:3], ps[0][0:2, 0:P], AX.X, ALU.max))
            link(nc.vector.tensor_scalar(am2[:, 0:2], K["ident"][0:2, 0:2], am2[:, 2:3], None, ALU.mult))
            dve.sem_inc(am_ready, 1)
            dve.wait_ge(am_out, 2)
            link(nc.vector.tensor_scalar(sc[:, 0:2], ps[1][:, 0:2], 1e-12, None, ALU.max))
            link(nc.vector.reciprocal(sc[:, 0:2], sc[:, 0:2]))
            link(nc.vector.tensor_scalar(sc[:, 0:2], sc[:, 0:2], FP8_MAX, None, ALU.mult))
            dve.sem_inc(scales_done, 1)
            link(nc.vector.reciprocal(sc[:, 2:4], sc[:, 0:2]))
            link(nc.vector.tensor_tensor(sc[:, 4:5], sc[:, 2:3], sc[:, 3:4], ALU.mult))
            dve.wait_ge(root_done, 1)
            link(nc.vector.reciprocal(r[:, 2, :], r[:, 1, :]))
            link(nc.vector.tensor_tensor(r[:, 3, :], r[:, 2, :], r[:, 2, :], ALU.mult))
            link(nc.vector.tensor_tensor(r[:, 3, :], r[:, 3, :], r[:, 0, :], ALU.mult))
            link(nc.vector.tensor_scalar(r[:, 3, :], r[:, 3, :], -0.5, 1.5, ALU.mult, ALU.add))
            link(nc.vector.tensor_tensor(r[:, 2, :], r[:, 2, :], r[:, 3, :], ALU.mult))
            link(nc.vector.tensor_scalar(r[:, 2, :], r[:, 2, :], 0.25, None, ALU.mult))
            dve.sem_inc(scales_done, 1)

            def quantise(dst, x, mg, m):
                link(nc.vector.tensor_scalar(half[:, 0:m], x, 0.5, None, ALU.mult, saturate=False))
                link(nc.vector.tensor_scalar(small[:, 0:m], x, 24576.0, -24576.0, ALU.add, ALU.add))
                link(nc.vector.scalar_tensor_tensor(out=small[:, 0:m], in0=half[:, 0:m], scalar=-2.0, in1=small[:, 0:m],
                                                    op0=ALU.mult, op1=ALU.add))
                link(nc.vector.scalar_tensor_tensor(out=small[:, 0:m], in0=mg, scalar=2.0 ** -5, in1=small[:, 0:m],
                                                    op0=ALU.is_lt, op1=ALU.mult))
                nc.vector.scalar_tensor_tensor(out=dst, in0=half[:, 0:m], scalar=2.0, in1=small[:, 0:m],
                                               op0=ALU.mult, op1=ALU.add).then_inc(xq_ready, 1)

            dve.wait_ge(scaled, 2)
            quantise(wq[:], wv[:, 0, :], wv[:, 1, :], P)
            dve.wait_ge(xq_ready, 1)
            b4 = lambda a: bcast(a.unsqueeze(1), [P, CS, P])
            for t in range(NS + 2):
                if t < NS:
                    dve.wait_ge(scaled, 2 * t + 4)
                    if t >= 2:
                        dve.wait_ge(g_ready, t - 1)
                    quantise(xq[:, t % 2, :], v[:, t % 2, :], mag[:, t % 2, :], ST)
                    dve.wait_ge(xq_ready, t + 2)
                if 1 <= t <= NS:
                    i = (t - 1) % 2
                    dve.wait_ge(g_ready, t)
                    if t >= 3:
                        dve.wait_ge(prod_done, t - 2)
                        dve.wait_ge(th_done, t - 2)
                    nc.vector.scalar_tensor_tensor(out=v4(gate[:, i, :]), in0=v4(ps[i][:]), scalar=sc[:, 4:5],
                                                   in1=b4(K["d_ffnb"][:]), op0=ALU.mult, op1=ALU.add).then_inc(gate_done, 1)
                if t >= 2:
                    i = t % 2
                    dve.wait_ge(th_done, t - 1)
                    dve.wait_ge(gate_done, t - 1)
                    link(nc.vector.scalar_tensor_tensor(out=gate[:, i, :], in0=th[:, i, :], scalar=1.0, in1=gate[:, i, :],
                                                        op0=ALU.add, op1=ALU.mult))
                    dve.wait_ge(sr_done, t - 1)
                    nc.vector.tensor_tensor(sr[:, i, :], gate[:, i, :], sr[:, i, :], ALU.mult).then_inc(prod_done, 1)

        @block.gpsimd
        def _(pool):
            pool.wait_ge(scales_done, 2)
            for t in range(NS + 1):
                if t < NS:
                    if t >= 2:
                        pool.wait_ge(o_ready, t - 1)
                    nc.gpsimd.tensor_tensor(v4(sr[:, t % 2, :]), v4(K["s_acc"][:, t * ST:(t + 1) * ST]),
                                            bcast(r[:, 2, t * CS:(t + 1) * CS].unsqueeze(2), [P, CS, P]), ALU.mult).then_inc(sr_done, 1)
                if t >= 1:
                    i = (t - 1) % 2
                    pool.wait_ge(prod_done, t)
                    pool.wait_ge(loaded[(t - 1) % AHEAD], 32 * ((t - 1) // AHEAD + 1))
                    if t >= 3:
                        pool.wait_ge(stored[i], 16 * ((t - 1) // 2))
                    nc.gpsimd.tensor_tensor(o[:, i, :], sr[:, i, :], xin[:, (t - 1) % AHEAD, :], ALU.add).then_inc(o_ready, 1)


def program(nc, dram, out):
    scratch = [nc.dram_tensor(n, [NS, P, ST], F32, kind="Internal").ap() for n in ("xn_t", "tc_t", "bc_t")]
    scratch.append(nc.dram_tensor("cum_parts", [NS, CS, 3, H, P], BF16, kind="Internal").ap())
    with ExitStack() as ctx:
        shapes = dict(ident=[P, P], ones=[P, P], w_zx=[P, 2 * DI], w_th=[P, H * 32], w_o=[P, DI], w_ffn=[P, P], prmT=[P, 80],
                      cols=[P, 2], goes_on=[P, NS], carry=[P, NP, HD], s_acc=[P, TOK], kk=[P, NC * H], cc=[P, NC * H],
                      dec=[P, NC * H], dtot=[P, NC * NP], ssq=[P, NC], mags=[P, 2 * NS + 2], d_ffnb=[P, P])
        K = {n: ctx.enter_context(nc.sbuf_tensor("k_" + n, s, F32)) for n, s in shapes.items()}
        for n, s in dict(ident_bf=[P, P], zeros_bf=[P, P], mask=[P, ST], pick=[3 * (H + CS), H * P],
                          cumT=[3 * (H + CS), TOK]).items():
            K[n] = ctx.enter_context(nc.sbuf_tensor("k_" + n, s, BF16))
        cum_stored = ctx.enter_context(nc.semaphore("cum_stored"))
        prepare(nc, K, dram, scratch, cum_stored)
        units(nc, K, scratch, cum_stored)
        finish(nc, K, dram[0], scratch[0], out)


NAMES = ["u", "in_proj_w", "dt_bias", "A_log", "D", "B_norm_w", "C_norm_w", "B_bias", "C_bias", "norm_w", "out_proj_w"]


def kernel(**inputs):
    import numpy as np
    import concourse.bacc as bacc
    from concourse.bass_utils import run_bass_kernel_spmd as run

    nc = bacc.Bacc("TRN2", target_bir_lowering=False, num_devices=1)
    arrays, dram = {}, []
    for name in ["L0_attn_" + n for n in NAMES] + ["L0_ffn_weight", "L0_ffn_bias"]:
        a = np.ascontiguousarray(inputs[name])
        arrays["in_" + name] = a
        dram.append(nc.dram_tensor("in_" + name, a.shape, mybir.dt.from_np(a.dtype), kind="ExternalInput").ap())
    out = nc.dram_tensor("out", (BATCH, L, DM), F32, kind="ExternalOutput").ap()
    program(nc, dram, out)
    return run(nc, [arrays], core_ids=[0]).results[0]["out"]
```
